# Optimizing a Trainium2 kernel written in Bass

```python
import numpy as np
import jax
import jax.numpy as jnp

def _softmax(x, axis=-1):
    return jax.nn.softmax(x, axis=axis)

def _gelu(x):
    return jax.nn.gelu(x, approximate=True)

def _silu(x):
    return jax.nn.silu(x)

def _sigmoid(x):
    return jax.nn.sigmoid(x)

def _layernorm(x, axis=-1, eps=1e-05):
    m = jnp.mean(x, axis=axis, keepdims=True)
    v = jnp.var(x, axis=axis, keepdims=True)
    return (x - m) / jnp.sqrt(v + eps)

def _scatter_add(tgt, idx, src, axis=0):
    return tgt.at[idx].add(src)

def _segment_sum(src, seg, n):
    return jax.ops.segment_sum(src, seg, n)
kernel_name = 'mk_gnn_preln_d4_gnn_r32_d1a783'

def setup_inputs(seed: int=0):
    np.random.seed(seed)
    _w = jnp.asarray

    def _rec_inputs():
        import jax
        import jax.numpy as jnp
        _gk = jax.random.key(seed)
        x = -0.000202 + 1 * jax.random.normal(jax.random.fold_in(_gk, 1), (3125, 64), jnp.float32)
        _s = jax.random.randint(jax.random.fold_in(_gk, 2), (25000,), 0, 3125, jnp.int32)
        _d = jax.random.randint(jax.random.fold_in(_gk, 3), (25000,), 0, 3125, jnp.int32)
        _loop = jnp.arange(3125, dtype=jnp.int32)
        src = jnp.concatenate([_s, _d, _loop])
        dst = jnp.concatenate([_d, _s, _loop])
        _o = jnp.argsort(dst, stable=True)
        src = src[_o]
        dst = dst[_o]
        edge_attr_32 = 0.000196303 + 1.00016 * jax.random.normal(jax.random.fold_in(_gk, 12), (53125, 32), jnp.float32)
        edge_type_3 = jax.random.randint(jax.random.fold_in(_gk, 14), (53125,), 0, 3, jnp.int32)
        edge_weight = jax.random.uniform(jax.random.fold_in(_gk, 15), (53125,), jnp.float32, 0.0, 1)
        edge_weight1 = jax.random.uniform(jax.random.fold_in(_gk, 16), (53125, 1), jnp.float32, 0.0, 0.999999)
        return (x, src, dst, edge_attr_32, edge_type_3, edge_weight, edge_weight1)
    x, src, dst, edge_attr_32, edge_type_3, edge_weight, edge_weight1 = _rec_inputs()

    def _L0_gnn_setup():
        import jax, jax.numpy as jnp
        import numpy as np
        N_NODES = 3125
        N_EDGES = 31250
        D = 64
        NUM_LAYERS = 2
        NUM_REL = 3
        BN_EPS = 1e-05

        def _gru_cell(x, h, w_ih, w_hh, b_ih, b_hh):
            gi = x @ w_ih.T + b_ih
            gh = h @ w_hh.T + b_hh
            i_r, i_z, i_n = jnp.split(gi, 3, axis=-1)
            h_r, h_z, h_n = jnp.split(gh, 3, axis=-1)
            r = jax.nn.sigmoid(i_r + h_r)
            z = jax.nn.sigmoid(i_z + h_z)
            n = jnp.tanh(i_n + r * h_n)
            return (1.0 - z) * n + z * h
        key = jax.random.key(seed)
        ks = jax.random.split(key, 10)
        h = jax.random.normal(ks[0], (N_NODES, D), dtype=jnp.float32)
        norm = jax.random.uniform(ks[1], (N_EDGES,), dtype=jnp.float32)
        src = jax.random.randint(ks[2], (N_EDGES,), 0, N_NODES, dtype=jnp.int32)
        dst = jax.random.randint(ks[3], (N_EDGES,), 0, N_NODES, dtype=jnp.int32)
        rel_type = jax.random.randint(ks[4], (N_EDGES,), 0, NUM_REL, dtype=jnp.int32)
        bound = np.sqrt(6.0 / D)
        weight = jax.random.uniform(ks[5], (NUM_REL, D, D), minval=-bound, maxval=bound, dtype=jnp.float32)
        s = 1.0 / np.sqrt(D)
        w_ih = jax.random.uniform(ks[6], (3 * D, D), minval=-s, maxval=s, dtype=jnp.float32)
        w_hh = jax.random.uniform(ks[7], (3 * D, D), minval=-s, maxval=s, dtype=jnp.float32)
        b_ih = jax.random.uniform(ks[8], (3 * D,), minval=-s, maxval=s, dtype=jnp.float32)
        b_hh = jax.random.uniform(ks[9], (3 * D,), minval=-s, maxval=s, dtype=jnp.float32)
        gamma = jnp.ones((D,), dtype=jnp.float32)
        beta = jnp.zeros((D,), dtype=jnp.float32)
        return {'h': h, 'norm': norm, 'weight': weight, 'w_ih': w_ih, 'w_hh': w_hh, 'b_ih': b_ih, 'b_hh': b_hh, 'gamma': gamma, 'beta': beta, 'src': src, 'dst': dst, 'rel_type': rel_type}
    _L0_gnn_all = _L0_gnn_setup()
    _L0_gnn_in = {k: v for k, v in _L0_gnn_all.items() if k in ('weight', 'w_ih', 'w_hh', 'b_ih', 'b_hh', 'gamma', 'beta')}
    del _L0_gnn_all

    def _L1_gnn_setup():
        import jax, jax.numpy as jnp
        import numpy as np
        N = 3125
        E = 50000
        IN, H, OUT = (64, 128, 64)

        def _gcn(x, src, tgt, w, W, b, n):
            h = x @ W.T
            deg = jax.ops.segment_sum(w, tgt, num_segments=n) + 1.0
            dinv = jnp.where(deg > 0, jax.lax.rsqrt(deg), 0.0)
            norm = dinv[src] * w * dinv[tgt]
            agg = jax.ops.segment_sum(h[src] * norm[:, None], tgt, num_segments=n)
            return agg + h * (dinv * dinv)[:, None] + b
        key = jax.random.key(seed)
        ks = jax.random.split(key, 12)

        def lin(k, o, i):
            return jax.random.normal(k, (o, i), dtype=jnp.float32) / np.sqrt(i)
        return {'x': jax.random.normal(ks[0], (N, IN), dtype=jnp.float32), 'edge_index': jax.random.randint(ks[1], (2, E), 0, N), 'edge_weight': jax.random.normal(ks[2], (E,), dtype=jnp.float32), 'W1p': lin(ks[3], H, IN), 'b1p': jnp.zeros((H,), jnp.float32), 'W1n': lin(ks[4], H, IN), 'b1n': jnp.zeros((H,), jnp.float32), 'W2p': lin(ks[5], OUT, H), 'b2p': jnp.zeros((OUT,), jnp.float32), 'W2n': lin(ks[6], OUT, H), 'b2n': jnp.zeros((OUT,), jnp.float32)}
    _L1_gnn_all = _L1_gnn_setup()
    _L1_gnn_in = {k: v for k, v in _L1_gnn_all.items() if k in ('W1p', 'b1p', 'W1n', 'b1n', 'W2p', 'b2p', 'W2n', 'b2n')}
    del _L1_gnn_all

    def _L2_gnn_setup():
        import jax, jax.numpy as jnp
        import numpy as np
        N_NODES = 3125
        N_EDGES = 50000
        C = 64

        def _spline_conv(x, src, dst, u, w, root, bias, n_nodes):
            h0 = x @ w[0]
            h1 = x @ w[1]
            uc = u[:, None]
            msg = (1.0 - uc) * h0[src] + uc * h1[src]
            agg = jax.ops.segment_sum(msg, dst, num_segments=n_nodes)
            deg = jax.ops.segment_sum(jnp.ones_like(u), dst, num_segments=n_nodes)
            agg = agg / jnp.maximum(deg, 1.0)[:, None]
            return agg + x @ root + bias
        key = jax.random.key(seed)
        ks = jax.random.split(key, 10)
        x = jax.random.normal(ks[0], (N_NODES, C), dtype=jnp.float32)
        edge_index = jax.random.randint(ks[1], (2, N_EDGES), 0, N_NODES, dtype=jnp.int64)
        edge_attr = jax.random.uniform(ks[2], (N_EDGES, 1), dtype=jnp.float32)
        s = 1.0 / np.sqrt(C)
        w1 = jax.random.uniform(ks[3], (2, C, C), jnp.float32, -s, s)
        root1 = jax.random.uniform(ks[4], (C, C), jnp.float32, -s, s)
        b1 = jnp.zeros((C,), jnp.float32)
        w2 = jax.random.uniform(ks[5], (2, C, C), jnp.float32, -s, s)
        root2 = jax.random.uniform(ks[6], (C, C), jnp.float32, -s, s)
        b2 = jnp.zeros((C,), jnp.float32)
        return {'x': x, 'edge_index': edge_index, 'edge_attr': edge_attr, 'w1': w1, 'root1': root1, 'b1': b1, 'w2': w2, 'root2': root2, 'b2': b2}
    _L2_gnn_all = _L2_gnn_setup()
    _L2_gnn_in = {k: v for k, v in _L2_gnn_all.items() if k in ('w1', 'root1', 'b1', 'w2', 'root2', 'b2')}
    del _L2_gnn_all

    def _L3_gnn_setup():
        import jax, jax.numpy as jnp
        import numpy as np
        N, D, E, ED, L = (3125, 64, 25000, 32, 5)
        LN_EPS = 1e-05

        def _leaky(x):
            return jax.nn.leaky_relu(x, negative_slope=0.1)
        key = jax.random.key(seed)
        ks = jax.random.split(key, 16)
        s = 0.05
        return {'x': jax.random.normal(ks[0], (N, D), dtype=jnp.float32), 'edge_index': jax.random.randint(ks[1], (2, E), 0, N, dtype=jnp.int64), 'edge_attr': jax.random.normal(ks[2], (E, ED), dtype=jnp.float32), 'W1': jax.random.normal(ks[3], (L, D, 2 * D), dtype=jnp.float32) * s, 'b1': jnp.zeros((L, 2 * D), dtype=jnp.float32), 'W2': jax.random.normal(ks[4], (L, 2 * D, D), dtype=jnp.float32) * s, 'b2': jnp.zeros((L, D), dtype=jnp.float32), 'We1': jax.random.normal(ks[5], (L, ED, D), dtype=jnp.float32) * s, 'be1': jnp.zeros((L, D), dtype=jnp.float32), 'We2': jax.random.normal(ks[6], (L, D, D), dtype=jnp.float32) * s, 'be2': jnp.zeros((L, D), dtype=jnp.float32), 'res_w': jnp.ones((L,), dtype=jnp.float32), 'dot_scale': jnp.ones((L,), dtype=jnp.float32), 'ln_g': jnp.ones((L, D), dtype=jnp.float32), 'ln_b': jnp.zeros((L, D), dtype=jnp.float32)}
    _L3_gnn_all = _L3_gnn_setup()
    _L3_gnn_in = {k: v for k, v in _L3_gnn_all.items() if k in ('W1', 'b1', 'W2', 'b2', 'We1', 'be1', 'We2', 'be2', 'res_w', 'dot_scale', 'ln_g', 'ln_b')}
    del _L3_gnn_all
    return {'x': x, 'src': src, 'dst': dst, 'edge_attr_32': edge_attr_32, 'edge_type_3': edge_type_3, 'edge_weight': edge_weight, 'edge_weight1': edge_weight1, 'L0_gnn_weight': _L0_gnn_in['weight'], 'L0_gnn_w_ih': _L0_gnn_in['w_ih'], 'L0_gnn_w_hh': _L0_gnn_in['w_hh'], 'L0_gnn_b_ih': _L0_gnn_in['b_ih'], 'L0_gnn_b_hh': _L0_gnn_in['b_hh'], 'L0_gnn_gamma': _L0_gnn_in['gamma'], 'L0_gnn_beta': _L0_gnn_in['beta'], 'L1_gnn_W1p': _L1_gnn_in['W1p'], 'L1_gnn_b1p': _L1_gnn_in['b1p'], 'L1_gnn_W1n': _L1_gnn_in['W1n'], 'L1_gnn_b1n': _L1_gnn_in['b1n'], 'L1_gnn_W2p': _L1_gnn_in['W2p'], 'L1_gnn_b2p': _L1_gnn_in['b2p'], 'L1_gnn_W2n': _L1_gnn_in['W2n'], 'L1_gnn_b2n': _L1_gnn_in['b2n'], 'L2_gnn_w1': _L2_gnn_in['w1'], 'L2_gnn_root1': _L2_gnn_in['root1'], 'L2_gnn_b1': _L2_gnn_in['b1'], 'L2_gnn_w2': _L2_gnn_in['w2'], 'L2_gnn_root2': _L2_gnn_in['root2'], 'L2_gnn_b2': _L2_gnn_in['b2'], 'L3_gnn_W1': _L3_gnn_in['W1'], 'L3_gnn_b1': _L3_gnn_in['b1'], 'L3_gnn_W2': _L3_gnn_in['W2'], 'L3_gnn_b2': _L3_gnn_in['b2'], 'L3_gnn_We1': _L3_gnn_in['We1'], 'L3_gnn_be1': _L3_gnn_in['be1'], 'L3_gnn_We2': _L3_gnn_in['We2'], 'L3_gnn_be2': _L3_gnn_in['be2'], 'L3_gnn_res_w': _L3_gnn_in['res_w'], 'L3_gnn_dot_scale': _L3_gnn_in['dot_scale'], 'L3_gnn_ln_g': _L3_gnn_in['ln_g'], 'L3_gnn_ln_b': _L3_gnn_in['ln_b']}

def reference(x, src, dst, edge_attr_32, edge_type_3, edge_weight, edge_weight1, L0_gnn_weight, L0_gnn_w_ih, L0_gnn_w_hh, L0_gnn_b_ih, L0_gnn_b_hh, L0_gnn_gamma, L0_gnn_beta, L1_gnn_W1p, L1_gnn_b1p, L1_gnn_W1n, L1_gnn_b1n, L1_gnn_W2p, L1_gnn_b2p, L1_gnn_W2n, L1_gnn_b2n, L2_gnn_w1, L2_gnn_root1, L2_gnn_b1, L2_gnn_w2, L2_gnn_root2, L2_gnn_b2, L3_gnn_W1, L3_gnn_b1, L3_gnn_W2, L3_gnn_b2, L3_gnn_We1, L3_gnn_be1, L3_gnn_We2, L3_gnn_be2, L3_gnn_res_w, L3_gnn_dot_scale, L3_gnn_ln_g, L3_gnn_ln_b):
    import jax
    import jax.numpy as jnp

    def _L0_gnn_ref(h, norm, weight, w_ih, w_hh, b_ih, b_hh, gamma, beta, src, dst, rel_type):
        import jax, jax.numpy as jnp
        import numpy as np
        N_NODES = 3125
        N_EDGES = 31250
        D = 64
        NUM_LAYERS = 2
        NUM_REL = 3
        BN_EPS = 1e-05

        def _gru_cell(x, h, w_ih, w_hh, b_ih, b_hh):
            gi = x @ w_ih.T + b_ih
            gh = h @ w_hh.T + b_hh
            i_r, i_z, i_n = jnp.split(gi, 3, axis=-1)
            h_r, h_z, h_n = jnp.split(gh, 3, axis=-1)
            r = jax.nn.sigmoid(i_r + h_r)
            z = jax.nn.sigmoid(i_z + h_z)
            n = jnp.tanh(i_n + r * h_n)
            return (1.0 - z) * n + z * h
        output = h
        hstate = jnp.zeros_like(h)
        for _ in range(NUM_LAYERS):
            t = jnp.einsum('nd,rde->rne', output, weight)
            msg = t[rel_type, src] * norm[:, None]
            swh = jax.ops.segment_sum(msg, dst, num_segments=N_NODES)
            hstate = _gru_cell(swh, hstate, w_ih, w_hh, b_ih, b_hh)
            output = hstate
        mean = jnp.mean(output, axis=0)
        var = jnp.mean(jnp.square(output - mean), axis=0)
        return (output - mean) / jnp.sqrt(var + BN_EPS) * gamma + beta

    def _L1_gnn_ref(x, edge_index, edge_weight, W1p, b1p, W1n, b1n, W2p, b2p, W2n, b2n):
        import jax, jax.numpy as jnp
        import numpy as np
        N = 3125
        E = 50000
        IN, H, OUT = (64, 128, 64)

        def _gcn(x, src, tgt, w, W, b, n):
            h = x @ W.T
            deg = jax.ops.segment_sum(w, tgt, num_segments=n) + 1.0
            dinv = jnp.where(deg > 0, jax.lax.rsqrt(deg), 0.0)
            norm = dinv[src] * w * dinv[tgt]
            agg = jax.ops.segment_sum(h[src] * norm[:, None], tgt, num_segments=n)
            return agg + h * (dinv * dinv)[:, None] + b
        src, tgt = (edge_index[0], edge_index[1])
        n = x.shape[0]
        wp = jnp.where(edge_weight >= 0, edge_weight, 0.0)
        wn = jnp.where(edge_weight < 0, -edge_weight, 0.0)
        h = jax.nn.relu(_gcn(x, src, tgt, wp, W1p, b1p, n) - _gcn(x, src, tgt, wn, W1n, b1n, n))
        out = jax.nn.relu(_gcn(h, src, tgt, wp, W2p, b2p, n) - _gcn(h, src, tgt, wn, W2n, b2n, n))
        return out

    def _L2_gnn_ref(x, edge_index, edge_attr, w1, root1, b1, w2, root2, b2):
        import jax, jax.numpy as jnp
        import numpy as np
        N_NODES = 3125
        N_EDGES = 50000
        C = 64

        def _spline_conv(x, src, dst, u, w, root, bias, n_nodes):
            h0 = x @ w[0]
            h1 = x @ w[1]
            uc = u[:, None]
            msg = (1.0 - uc) * h0[src] + uc * h1[src]
            agg = jax.ops.segment_sum(msg, dst, num_segments=n_nodes)
            deg = jax.ops.segment_sum(jnp.ones_like(u), dst, num_segments=n_nodes)
            agg = agg / jnp.maximum(deg, 1.0)[:, None]
            return agg + x @ root + bias
        src, dst = (edge_index[0], edge_index[1])
        u = edge_attr[:, 0]
        n = x.shape[0]
        h = _spline_conv(x, src, dst, u, w1, root1, b1, n)
        h = _spline_conv(h, src, dst, u, w2, root2, b2, n)
        return h

    def _L3_gnn_ref(x, edge_index, edge_attr, W1, b1, W2, b2, We1, be1, We2, be2, res_w, dot_scale, ln_g, ln_b):
        import jax, jax.numpy as jnp
        import numpy as np
        N, D, E, ED, L = (3125, 64, 25000, 32, 5)
        LN_EPS = 1e-05

        def _leaky(x):
            return jax.nn.leaky_relu(x, negative_slope=0.1)
        src, dst = (edge_index[0], edge_index[1])
        n = x.shape[0]
        for l in range(W1.shape[0]):
            h = _leaky(x @ W1[l] + b1[l]) @ W2[l] + b2[l]
            e = _leaky(edge_attr @ We1[l] + be1[l]) @ We2[l] + be2[l]
            msg = h[src] * e * dot_scale[l]
            agg = jax.ops.segment_sum(msg, dst, num_segments=n)
            out = x + agg * res_w[l]
            mu = jnp.mean(out, axis=-1, keepdims=True)
            var = jnp.mean(jnp.square(out - mu), axis=-1, keepdims=True)
            x = (out - mu) * jax.lax.rsqrt(var + LN_EPS) * ln_g[l] + ln_b[l]
        return x
    edge_index = jnp.stack([src, dst])
    h = jnp.maximum(_layernorm(x, axis=-1), 0.0)
    x = x + _L0_gnn_ref(h, edge_weight, L0_gnn_weight, L0_gnn_w_ih, L0_gnn_w_hh, L0_gnn_b_ih, L0_gnn_b_hh, L0_gnn_gamma, L0_gnn_beta, src, dst, edge_type_3)
    h = jnp.maximum(_layernorm(x, axis=-1), 0.0)
    x = x + _L1_gnn_ref(h, edge_index, edge_weight, L1_gnn_W1p, L1_gnn_b1p, L1_gnn_W1n, L1_gnn_b1n, L1_gnn_W2p, L1_gnn_b2p, L1_gnn_W2n, L1_gnn_b2n)
    h = jnp.maximum(_layernorm(x, axis=-1), 0.0)
    x = x + _L2_gnn_ref(h, edge_index, edge_weight1, L2_gnn_w1, L2_gnn_root1, L2_gnn_b1, L2_gnn_w2, L2_gnn_root2, L2_gnn_b2)
    h = jnp.maximum(_layernorm(x, axis=-1), 0.0)
    x = x + _L3_gnn_ref(h, edge_index, edge_attr_32, L3_gnn_W1, L3_gnn_b1, L3_gnn_W2, L3_gnn_b2, L3_gnn_We1, L3_gnn_be1, L3_gnn_We2, L3_gnn_be2, L3_gnn_res_w, L3_gnn_dot_scale, L3_gnn_ln_g, L3_gnn_ln_b)
    return x

_drawn_inputs = setup_inputs


def setup_inputs(seed=0):
    import zlib

    import numpy as np

    out = dict(_drawn_inputs(seed))
    spreads = {'L0_gnn_gamma': (1.0, 0.2),
     'L0_gnn_beta': (0.0, 0.1),
     'L1_gnn_b1p': (0.0, 0.1),
     'L1_gnn_b1n': (0.0, 0.1),
     'L1_gnn_b2p': (0.0, 0.1),
     'L1_gnn_b2n': (0.0, 0.1),
     'L2_gnn_b1': (0.0, 0.1),
     'L2_gnn_b2': (0.0, 0.1),
     'L3_gnn_b1': (0.0, 0.1),
     'L3_gnn_b2': (0.0, 0.1),
     'L3_gnn_be1': (0.0, 0.1),
     'L3_gnn_be2': (0.0, 0.1),
     'L3_gnn_res_w': (1.0, 0.2),
     'L3_gnn_dot_scale': (1.0, 0.2),
     'L3_gnn_ln_g': (1.0, 0.2),
     'L3_gnn_ln_b': (0.0, 0.1)}
    factors = {}
    for name, (base, spread) in spreads.items():
        noise = np.random.default_rng([zlib.crc32(name.encode()), seed]).standard_normal(out[name].shape)
        drawn = base * np.exp(spread * noise) if base else spread * noise
        out[name] = jnp.asarray(drawn.astype(out[name].dtype))
    for name, factor in factors.items():
        out[name] = (out[name] * factor).astype(out[name].dtype)
    return out
```

```python
import concourse.bass as bass
from concourse import mybir
from contextlib import ExitStack

F32 = mybir.dt.float32
I32 = mybir.dt.int32
ALU = mybir.AluOpType
ACT = mybir.ActivationFunctionType
AX = mybir.AxisListType.X

N, D, E, ED, L3L, REL = 3125, 64, 53125, 32, 5, 3
TP, TB = 125, 25
GE, EJ = 512, 4
G = -(-E // GE)
UN = 4
GP = G + UN
WIN = 64
NC = N + WIN
TAIL = E - (G - 1) * GE
SPAN_MAX = -(-N // WIN)
FAR = 1.0e6
LN_EPS = BN_EPS = 1e-5

C_WE1, C_WE2, C_W1, C_W2, C_B2, C_G, C_B, C_BE2 = 0, 256, 384, 512, 576, 640, 704, 768
C_B1, C_BE1, C_RES, C_DOT, C_END = 1024, 1025, 1026, 1027, 1028
S_W0, S_W1, S_ROOT, S_BIAS, S_END = 0, 64, 128, 192, 256


def chunks(total, step):
    return [(i, min(i + step, total)) for i in range(0, total, step)]


def gnn_kernel(nc, a, out):
    ctx = ExitStack()
    with ctx:
        def sb(name, shape, dt=F32):
            return ctx.enter_context(nc.sbuf_tensor(name, shape, dt))

        ctx.enter_context(nc.allow_non_contiguous_dma(reason="columns of biases, loaded once"))
        table = nc.dram_tensor("table", (2 * N, D), F32, kind="Internal").ap()
        eg_dram = nc.dram_tensor("eg_dram", (L3L, 128, C_END), F32, kind="Internal").ap()

        first = sb("first", [G, 2])
        last = sb("last", [G, 1])
        dstrel = sb("dstrel", [128, GP, EJ])
        spline_w = sb("spline_w", [128, GP, EJ, 2])
        rel_w = sb("rel_w", [128, GP, EJ, REL])
        sign_w = sb("sign_w", [128, GP, EJ, 2])
        deg_w = sb("deg_w", [128, GP, EJ, 3])
        src_i = sb("src_i", [128, GP, EJ], I32)
        srcsign_i = sb("srcsign_i", [128, GP, EJ], I32)
        first_row = sb("first_row", [1, GP])
        span_row = sb("span_row", [1, G])
        span = sb("span", [1, 2], I32)
        win_row = sb("win_row", [1, GP], I32)
        win_f = sb("win_f", [1, GP])
        iota_i = sb("iota_i", [128, WIN], I32)
        iota0 = sb("iota0", [128, WIN])
        iota = sb("iota", [128, WIN])
        idx = sb("idx", [128, UN, EJ], I32)
        gath = sb("gath", [128, UN, EJ, D])
        onehot = sb("onehot", [128, 2, EJ, WIN])
        onehot_w = sb("onehot_w", [128, 2, EJ, REL, WIN])
        deg_c = sb("deg_c", [128, 2, EJ, 3])
        msg = sb("msg", [128, 2, EJ, D])
        attr_in = sb("attr_in", [128, UN, EJ * ED])
        attr_t = sb("attr_t", [128, G + 2, 128])
        hid_e = sb("hid_e", [128, 2, 2 * 128])

        x = sb("x", [TP, TB, D])
        h = sb("h", [TP, TB, D])
        y = sb("y", [TP, TB, D])
        wide = sb("wide", [TP, TB, 2 * D])
        hid_t = sb("hid_t", [128, NC])
        def laid(t, at):
            return t[:, at:at + GP * EJ].rearrange("p (g j) -> p g j", j=EJ)
        src_f = laid(onehot[:, :, :, :].rearrange("p a j w -> p (a j w)"), 0)
        type_f = laid(gath[:, :, :, :].rearrange("p s j c -> p (s j c)"), 0)
        weight = laid(gath[:, :, :, :].rearrange("p s j c -> p (s j c)"), 512)
        swh_t = hid_t[0:D + 1, :]
        raw_i = onehot_w[0:G].rearrange("p a j r w -> p (a j r w)").bitcast(I32).rearrange("p (k i) -> p k i", i=GE)
        raw_f = hid_t[0:G, 0:5 * GE].rearrange("p (k i) -> p k i", i=GE)
        h_t = sb("h_t", [D + 1, TB, TP])
        acc_all = sb("acc_all", [D + 3, REL, NC])
        acc = acc_all[0:D]
        acc_deg = acc_all[D:D + 3, 0, :]
        deg = sb("deg", [TP, TB, 3])
        ndinv = sb("ndinv", [TP, TB])
        mean = sb("mean", [TP, TB])
        var = sb("var", [TP, TB])
        scratch = wide[:, :, :].rearrange("p b c -> p (b c)")
        rz = scratch[:, 0:32 * D].rearrange("p (q b c) -> p q b c", q=2, c=2 * D)
        cand = scratch[:, 32 * D:48 * D].rearrange("p (q b c) -> p q b c", q=2, c=D)
        mix = gath[0:TP].rearrange("p s j c -> p (s j c)").rearrange("p (q b c) -> p q b c", q=2, c=D)
        bn6 = sb("bn6", [D, 7, 6])
        bn2 = sb("bn2", [D, 2])
        bnsc = sb("bnsc", [D, 4])

        ident = sb("ident", [128, 128])
        ones_row = sb("ones_row", [1, 128])
        epsc = sb("epsc", [128, 1])
        wrel = sb("wrel", [D, REL, D])
        nat = attr_in[:, :, :].rearrange("p s c -> p (s c)")
        gru_nat = nat[0:D, 0:6 * D].rearrange("p (m g e) -> p m g e", m=2, g=3)
        w_ih = sb("w_ih", [D + 1, 3, D])
        w_hh = sb("w_hh", [D + 1, 3, D])
        gb = sb("gb", [D, 2])
        w1_nat = nat[:, 6 * D:8 * D].rearrange("p (k e) -> p k e", k=2)
        w1pn = sb("w1pn", [D, 2, 2 * D])
        w2_nat = msg[0:D, 0].rearrange("p j c -> p (j c)").rearrange("p (k e) -> p k e", k=2)
        w2pn = sb("w2pn", [2 * D, 2, D])
        b1pn = sb("b1pn", [TP, 2, 2 * D])
        b2pn = sb("b2pn", [TP, 2, D])
        spl_all = sb("spl_all", [128, 2, S_END])
        spl = sb("spl", [128, S_END])
        eg_all = attr_t[:, :, :].rearrange("p g c -> p (g c)")[:, 0:L3L * C_END].rearrange("p (l c) -> p l c", c=C_END)
        eg = sb("eg", [128, C_END])

        ps = ctx.enter_context(nc.psum_tensor("ps", [128, 8, 512], F32))
        sems = []

        def sem(name):
            s = ctx.enter_context(nc.semaphore(name))
            sems.append(s)
            return s

        cleared, loads, loads2, misc = sem("cleared"), sem("loads"), sem("loads2"), sem("misc")
        dve_done, act_done, pe_step, ps_read, pool_done = (
            sem("dve_done"), sem("act_done"), sem("pe_step"), sem("ps_read"), sem("pool_done"))
        stored, h_ready, var_ready, std_ready = sem("stored"), sem("h_ready"), sem("var_ready"), sem("std_ready")
        swh_sum, swh_ready, deg_turned, deg_read = (
            sem("swh_sum"), sem("swh_ready"), sem("deg_turned"), sem("deg_read"))
        gates_done, rz_ready, pre_ready, cand_ready, hnew_ready, hnew_turned, ht_ready = (
            sem("gates_done"), sem("rz_ready"), sem("pre_ready"), sem("cand_ready"),
            sem("hnew_ready"), sem("hnew_turned"), sem("ht_ready"))
        idx_ready = [sem(f"idx_ready{s}") for s in range(UN)]
        gathered = [sem(f"gathered{s}") for s in range(UN)]
        attr_loaded = [sem(f"attr_loaded{s}") for s in range(UN)]
        idx_seen, onehot_built, onehot_ready, summed, acc_added = (
            sem("idx_seen"), sem("onehot_built"), sem("onehot_ready"), sem("summed"), sem("acc_added"))
        attr_turned, attr_kept, attr_seen = sem("attr_turned"), sem("attr_kept"), sem("attr_seen")
        hid_biased = sem("hid_biased")
        hid_sum, hid_ready, gate_done, msg_ready = (
            sem("hid_sum"), sem("hid_ready"), sem("gate_done"), sem("msg_ready"))
        out_done = sem("out_done")

        def rejoin():
            nc.multi_engine_barrier(list(mybir.ALL_ENGINES),
                                    sems_to_clear=range(sems[0].num, sems[-1].num + 1))

        def linked(eng, done):
            count = [0]

            def link(ins):
                count[0] += 1
                ins.then_inc(done, 1)
                eng.wait_ge(done, count[0])
            return link

        def by_tile(t):
            return t.rearrange("c (p b) -> c b p", b=TB)

        def row_bc(ap2, width):
            return ap2.unsqueeze(2).to_broadcast([ap2.shape[0], ap2.shape[1], width])

        def const_bc(ap1):
            return ap1.unsqueeze(1).to_broadcast([ap1.shape[0], TB, ap1.shape[1]])

        def bcast_rows(ap1, parts):
            return ap1.unsqueeze(0).to_broadcast([parts, ap1.shape[0]])

        N_CLEAR = 10
        with nc.Block() as block:
            @block.gpsimd
            def _(pool):
                nc.gpsimd.memset(raw_i[:], 0).then_inc(cleared, 1)
                nc.gpsimd.memset(raw_f[:], 0.0).then_inc(cleared, 1)
                nc.gpsimd.memset(eg_all[:], 0.0).then_inc(cleared, 1)
                nc.gpsimd.memset(spl_all[:], 0.0).then_inc(cleared, 1)
                nc.gpsimd.memset(ident[:], 0.0).then_inc(pool_done, 1)
                nc.gpsimd.iota(iota_i[:], pattern=[[1, WIN]], base=0, channel_multiplier=0).then_inc(pool_done, 1)
                nc.gpsimd.memset(attr_t[:, G:G + 2, :], 0.0).then_inc(pool_done, 1)
                pool.wait_ge(pool_done, 1)
                nc.gpsimd.affine_select(out=ident[:], in_=ident[:], compare_op=ALU.not_equal, fill=1.0,
                                        base=0, pattern=[[-1, 128]], channel_multiplier=1).then_inc(pool_done, 1)
                nc.gpsimd.memset(acc_all[:], 0.0).then_inc(pool_done, 1)
                pool.wait_ge(pool_done, 5)

            @block.vector
            def _(v):
                for t in (dstrel, src_f, type_f, weight, h_t, y, spline_w, first_row):
                    nc.vector.memset(t[:], 0.0).then_inc(dve_done, 1)
                nc.vector.memset(ones_row[:], 1.0).then_inc(dve_done, 1)
                nc.vector.memset(epsc[:], LN_EPS).then_inc(dve_done, 1)
                v.wait_ge(dve_done, 10)
                nc.vector.memset(h_t[D:D + 1, :, :], 1.0).then_inc(dve_done, 1)
                v.wait_ge(pool_done, 4)
                nc.vector.tensor_copy(iota0[:], iota_i[:]).then_inc(dve_done, 1)
                v.wait_ge(dve_done, 12)

            @block.sync
            def _(sp):
                sp.wait_ge(cleared, 2)
                n = 0
                full, tail = (G - 1) * GE, TAIL
                for k, name in enumerate(("src", "dst", "edge_type_3")):
                    v = a[name]
                    sp.dma_start(raw_i[0:G - 1, k, :], v[0:full].rearrange("(g i) -> g i", i=GE)).then_inc(loads, 16)
                    sp.dma_start(raw_i[G - 1:G, k, 0:tail], v[full:E].unsqueeze(0)).then_inc(loads, 16)
                    n += 2
                sp.dma_start(raw_i[G - 1:G, 1, tail:GE], a["dst"][E - (GE - tail):E].unsqueeze(0)).then_inc(loads, 16)
                n += 1
                for k, v in ((3, a["edge_weight"]), (4, a["edge_weight1"].rearrange("e o -> (e o)"))):
                    sp.dma_start(raw_f[0:G - 1, k, :], v[0:full].rearrange("(g i) -> g i", i=GE)).then_inc(loads, 16)
                    sp.dma_start(raw_f[G - 1:G, k, 0:tail], v[full:E].unsqueeze(0)).then_inc(loads, 16)
                    n += 2
                sp.dma_start(x[:], a["x"].rearrange("(p b) c -> p b c", b=TB)).then_inc(loads, 16)
                sp.dma_start(wrel[:], a["L0_gnn_weight"].rearrange("r d e -> d r e")).then_inc(loads, 16)
                sp.dma_start(gru_nat[:, 0], a["L0_gnn_w_ih"].rearrange("(g d) e -> d g e", g=3)).then_inc(loads, 16)
                sp.dma_start(gru_nat[:, 1], a["L0_gnn_w_hh"].rearrange("(g d) e -> d g e", g=3)).then_inc(loads, 16)
                bi, bh = a["L0_gnn_b_ih"].unsqueeze(0), a["L0_gnn_b_hh"].unsqueeze(0)
                w_ih_row = w_ih[D:D + 1].rearrange("p g e -> p (g e)")
                sp.dma_start(w_ih_row[:, 0:D], bi[:, 2 * D:3 * D]).then_inc(loads, 16)
                sp.dma_start(w_ih_row[:, D:3 * D], bi[:, 0:2 * D]).then_inc(loads, 16)
                sp.dma_start(w_hh[D:D + 1].rearrange("p g e -> p (g e)"), bh).then_inc(loads, 16)
                sp.dma_start(gb[:, 0:1], a["L0_gnn_gamma"].unsqueeze(1)).then_inc(loads, 16)
                sp.dma_start(gb[:, 1:2], a["L0_gnn_beta"].unsqueeze(1)).then_inc(loads, 16)
                n += 9
                for k, s in enumerate("pn"):
                    sp.dma_start(w1_nat[:, k], a[f"L1_gnn_W1{s}"]).then_inc(loads, 16)
                    sp.dma_start(w2_nat[:, k], a[f"L1_gnn_W2{s}"]).then_inc(loads, 16)
                    sp.dma_start(b1pn[:, k], bcast_rows(a[f"L1_gnn_b1{s}"], TP)).then_inc(loads, 16)
                    sp.dma_start(b2pn[:, k], bcast_rows(a[f"L1_gnn_b2{s}"], TP)).then_inc(loads, 16)
                    n += 4
                sp.wait_ge(loads, 16 * n)

            @block.scalar
            def _(act):
                act.wait_ge(cleared, 4)
                n = 0
                for l in (0, 1):
                    sp_w = a[f"L2_gnn_w{l + 1}"]
                    for k in (0, 1):
                        act.dma_start(spl_all[0:D, l, S_W0 + k * D:S_W0 + (k + 1) * D], sp_w[k]).then_inc(loads2, 16)
                    act.dma_start(spl_all[0:D, l, S_ROOT:S_ROOT + D], a[f"L2_gnn_root{l + 1}"]).then_inc(loads2, 16)
                    act.dma_start(spl_all[D:D + 1, l, S_ROOT:S_ROOT + D],
                                  a[f"L2_gnn_b{l + 1}"].unsqueeze(0)).then_inc(loads2, 16)
                    n += 4
                for j in range(EJ):
                    o = C_WE1 + j * D
                    act.dma_start(eg_all[ED * j:ED * j + ED, :, o:o + D],
                                  a["L3_gnn_We1"].rearrange("l k d -> k l d")).then_inc(loads2, 16)
                    n += 1
                for j in range(2):
                    o = C_WE2 + j * D
                    act.dma_start(eg_all[D * j:D * j + D, :, o:o + D],
                                  a["L3_gnn_We2"].rearrange("l k d -> k l d")).then_inc(loads2, 16)
                    act.dma_start(eg_all[D * j:D * j + D, :, C_BE1:C_BE1 + 1],
                                  a["L3_gnn_be1"].rearrange("l k -> k l").unsqueeze(2)).then_inc(loads2, 16)
                    n += 2
                act.dma_start(eg_all[0:D, :, C_W1:C_W1 + 2 * D],
                              a["L3_gnn_W1"].rearrange("l k d -> k l d")).then_inc(loads2, 16)
                act.dma_start(eg_all[:, :, C_W2:C_W2 + D],
                              a["L3_gnn_W2"].rearrange("l k d -> k l d")).then_inc(loads2, 16)
                act.dma_start(eg_all[:, :, C_B1:C_B1 + 1],
                              a["L3_gnn_b1"].rearrange("l k -> k l").unsqueeze(2)).then_inc(loads2, 16)
                n += 3
                for c, name in ((C_B2, "b2"), (C_G, "ln_g"), (C_B, "ln_b")):
                    v = a[f"L3_gnn_{name}"]
                    act.dma_start(eg_all[:, :, c:c + D],
                                  v.unsqueeze(0).to_broadcast([128, L3L, D])).then_inc(loads2, 16)
                    n += 1
                for j in range(EJ):
                    o = C_BE2 + j * D
                    act.dma_start(eg_all[0:1, :, o:o + D], a["L3_gnn_be2"].unsqueeze(0)).then_inc(loads2, 16)
                    n += 1
                for c, name in ((C_RES, "res_w"), (C_DOT, "dot_scale")):
                    v = a[f"L3_gnn_{name}"]
                    act.dma_start(eg_all[:, :, c:c + 1],
                                  v.unsqueeze(0).unsqueeze(2).to_broadcast([128, L3L, 1])).then_inc(loads2, 16)
                    n += 1
                act.wait_ge(loads2, 16 * n)
                act.dma_start(eg_dram.rearrange("l p c -> p l c"), eg_all[:, :, :]).then_inc(stored, 16)
                act.wait_ge(stored, 16)
        rejoin()

        EDGE_COLS = (dstrel, src_f, type_f, weight)

        def layer_norm(v, link, src, dst, weighted=None):
            link(nc.vector.tensor_reduce(mean[:], src[:], AX, ALU.add))
            link(nc.vector.tensor_scalar(mean[:], mean[:], 1.0 / D, None, ALU.mult))
            link(nc.vector.tensor_tensor(dst[:], src[:], row_bc(mean[:], D), op=ALU.subtract))
            sq = wide[:, :, 0:D]
            link(nc.vector.tensor_tensor(sq, dst[:], dst[:], op=ALU.mult))
            link(nc.vector.tensor_reduce(var[:], sq, AX, ALU.add))
            nc.vector.tensor_scalar(var[:], var[:], 1.0 / D, None, ALU.mult).then_inc(var_ready, 1)
            v.wait_ge(std_ready, 1)
            link(nc.vector.reciprocal(var[:], var[:]))
            link(nc.vector.tensor_tensor(dst[:], dst[:], row_bc(var[:], D), op=ALU.mult))
            if weighted:
                link(nc.vector.tensor_tensor(dst[:], dst[:], const_bc(weighted[0]), op=ALU.mult))
                link(nc.vector.tensor_tensor(dst[:], dst[:], const_bc(weighted[1]), op=ALU.add))

        def std(act):
            act.wait_ge(var_ready, 1)
            nc.scalar.activation(var[:], var[:], ACT.Sqrt, bias=epsc[0:TP, :]).then_inc(std_ready, 1)

        def relu(link, t):
            link(nc.vector.tensor_scalar(t[:], t[:], 0.0, None, ALU.max))

        table_h = table[0:N, :].rearrange("(p b) c -> p b c", b=TB)
        table_n = table[N:2 * N, :].rearrange("(p b) c -> p b c", b=TB)

        with nc.Block() as block:
            @block.vector
            def _(v):
                link = linked(v, dve_done)
                link(nc.vector.tensor_copy(raw_f[:, 0:3, :].rearrange("p a i -> p (a i)"),
                                           raw_i[:, :, :].rearrange("p a i -> p (a i)")))
                link(nc.vector.tensor_reduce(first[:, 0:1], raw_f[:, 1, :], AX, ALU.min))
                link(nc.vector.tensor_reduce(last[:], raw_f[:, 1, :], AX, ALU.max))
                link(nc.vector.tensor_tensor(first[:, 1:2], last[:], first[:, 0:1], op=ALU.subtract))
                nc.vector.tensor_scalar(raw_f[:, 1, :], raw_f[:, 1, :], first[:, 0:1], None,
                                        ALU.subtract).then_inc(misc, 1)
                for k, dst in ((0, src_f), (1, dstrel), (2, type_f), (3, weight)):
                    v.wait_ge(pe_step, k + 1)
                    nc.vector.tensor_copy(dst[:, 0:G, :],
                                          ps[:, k, 0:EJ * G].rearrange("p (j g) -> p g j", j=EJ)).then_inc(ps_read, 1)
                v.wait_ge(pe_step, 5)
                nc.vector.tensor_copy(spline_w[:, 0:G, :, 1],
                                      ps[:, 4, 0:EJ * G].rearrange("p (j g) -> p g j", j=EJ)).then_inc(ps_read, 1)
                v.wait_ge(pe_step, 6)
                nc.vector.tensor_copy(first_row[:, 0:G], ps[0:1, 5, 0:G]).then_inc(ps_read, 1)
                nc.vector.tensor_copy(span_row[:], ps[0:1, 5, 128:128 + G]).then_inc(ps_read, 1)
                v.wait_ge(ps_read, 7)
                link(nc.vector.tensor_scalar(spline_w[:, :, :, 0], spline_w[:, :, :, 1], -1.0, 1.0, ALU.mult, ALU.add))
                for r in range(REL):
                    link(nc.vector.scalar_tensor_tensor(rel_w[:, :, :, r], type_f[:], float(r), weight[:],
                                                        ALU.is_equal, ALU.mult))
                for t in (sign_w, deg_w):
                    link(nc.vector.tensor_scalar(t[:, :, :, 0], weight[:], 0.0, None, ALU.max))
                    link(nc.vector.tensor_scalar(t[:, :, :, 1], weight[:], -1.0, 0.0, ALU.mult, ALU.max))
                link(nc.vector.memset(deg_w[:, :, :, 2], 1.0))
                link(nc.vector.tensor_copy(src_i[:], src_f[:]))
                link(nc.vector.tensor_scalar(type_f[:], weight[:], 0.0, float(N), ALU.is_lt, ALU.mult))
                link(nc.vector.tensor_tensor(srcsign_i[:], type_f[:], src_f[:], op=ALU.add))
                link(nc.vector.tensor_reduce(span_row[:, 0:1], span_row[:], AX, ALU.max))
                link(nc.vector.tensor_copy(span[:, 0:1], span_row[:, 0:1]))
                link(nc.vector.tensor_scalar(span[:, 0:1], span[:, 0:1], WIN.bit_length() - 1, None,
                                             ALU.logical_shift_right))
                link(nc.vector.tensor_scalar(span[:, 0:1], span[:, 0:1], 1.0, None, ALU.add))
                layer_norm(v, link, x, h)
                relu(link, h)
                nc.vector.tensor_tensor(b1pn[:, 0], b1pn[:, 0], b1pn[:, 1], op=ALU.subtract).then_inc(h_ready, 1)
                nc.vector.tensor_tensor(b2pn[:, 0], b2pn[:, 0], b2pn[:, 1], op=ALU.subtract).then_inc(h_ready, 1)
                v.wait_ge(h_ready, 2)

            @block.gpsimd
            def _(pool):
                pool.wait_ge(misc, 1)
                nc.gpsimd.affine_select(out=raw_f[:, 1, :], in_=raw_f[:, 1, :], compare_op=ALU.is_ge, fill=FAR,
                                        base=E - 1, pattern=[[-1, GE]], channel_multiplier=-GE).then_inc(pool_done, 1)
                pool.wait_ge(pool_done, 1)

            @block.tensor
            def _(pe):
                pe.wait_ge(misc, 1)
                for k in range(5):
                    if k == 1:
                        pe.wait_ge(pool_done, 1)
                    for j in range(EJ):
                        t = nc.tensor.transpose(ps[:, k, j * G:(j + 1) * G],
                                                raw_f[:, k, :].rearrange("g (p j) -> g j p", j=EJ)[:, j, :],
                                                ident[0:G, 0:G])
                    t.then_inc(pe_step, 1)
                for k in range(2):
                    t = nc.tensor.transpose(ps[0:1, 5, k * 128:k * 128 + G], first[:, k:k + 1], ident[0:G, 0:G])
                t.then_inc(pe_step, 1)
                for m, nat in enumerate((0, 1)):
                    for g in range(3):
                        t = nc.tensor.transpose(ps[0:D, 6, (3 * m + g) * D:(3 * m + g + 1) * D],
                                                gru_nat[:, nat, g, :], ident[0:D, 0:D])
                t.then_inc(swh_sum, 1)
                for k in range(2):
                    nc.tensor.transpose(ps[0:D, 7, k * 128:(k + 1) * 128], w1_nat[:, k, :], ident[:, :])
                for k in range(2):
                    t = nc.tensor.transpose(ps[:, 7, 256 + k * D:256 + (k + 1) * D], w2_nat[:, k, :], ident[0:D, 0:D])
                t.then_inc(swh_sum, 1)

            @block.scalar
            def _(act):
                act.wait_ge(swh_sum, 1)
                g_ih = ps[0:D, 6, 0:3 * D].rearrange("p (g e) -> p g e", g=3)
                nc.scalar.copy(w_ih[0:D, 0, :], g_ih[:, 2, :]).then_inc(act_done, 1)
                nc.scalar.copy(w_ih[0:D, 1:3, :], g_ih[:, 0:2, :]).then_inc(act_done, 1)
                nc.scalar.copy(w_hh[0:D, :, :], ps[0:D, 6, 3 * D:6 * D].rearrange("p (g e) -> p g e", g=3)).then_inc(act_done, 1)
                act.wait_ge(swh_sum, 2)
                nc.scalar.copy(w1pn[:], ps[0:D, 7, 0:256].rearrange("p (k e) -> p k e", k=2)).then_inc(act_done, 1)
                nc.scalar.copy(w2pn[:], ps[:, 7, 256:256 + 2 * D].rearrange("p (k e) -> p k e", k=2)).then_inc(act_done, 1)
                std(act)
                act.wait_ge(act_done, 5)

            @block.sync
            def _(sp):
                sp.wait_ge(h_ready, 1)
                sp.dma_start(table_h, h[:]).then_inc(stored, 16)
                sp.wait_ge(stored, 16)
        rejoin()

        SPAN = nc.values_load(span[0:1, 0:1], min_val=1, max_val=SPAN_MAX)

        def reset_windows():
            with nc.Block(no_gpsimd_drain=True) as block:
                @block.vector
                def _(v):
                    nc.vector.tensor_copy(iota[:], iota0[:]).then_inc(dve_done, 1)
                    nc.vector.tensor_copy(win_f[:], first_row[:]).then_inc(dve_done, 1)
                    nc.vector.tensor_copy(win_row[:], first_row[:]).then_inc(dve_done, 1)
                    v.wait_ge(dve_done, 3)

        def next_windows(v, at):
            nc.vector.tensor_scalar(iota[:], iota[:], float(WIN), None, ALU.add).then_inc(dve_done, 1)
            nc.vector.tensor_scalar(win_f[:], win_f[:], float(WIN), float(N), ALU.add, ALU.min).then_inc(dve_done, 1)
            v.wait_ge(dve_done, at + 2)
            nc.vector.tensor_copy(win_row[:], win_f[:]).then_inc(dve_done, 1)
            v.wait_ge(dve_done, at + 3)

        def gather_rows(pool, rows):
            with pool.Fori(0, G // UN) as i:
                for s in range(UN):
                    pool.wait_ge(idx_ready[s], i + 1)
                    pool.sem_inc(idx_seen, 1)
                    for j in range(EJ):
                        nc.gpsimd.indirect_dma_start(
                            out=gath[:, s, j, :], out_offset=None, in_=table[0:rows, :],
                            in_offset=bass.IndirectOffsetOnAxis(ap=idx[:, s, j:j + 1], axis=0),
                        ).then_inc(gathered[s], 16)
            for s in range(UN):
                pool.wait_ge(gathered[s], 16 * EJ * (G // UN))
            pool.dma_reset(range(gathered[0].num, gathered[-1].num + 1))

        def build_onehot(g, slot):
            return nc.vector.tensor_tensor(
                onehot[:, slot], iota[:].unsqueeze(1).to_broadcast([128, EJ, WIN]),
                dstrel[:, bass.ds(g, 1), :].rearrange("p a j -> p (a j)").unsqueeze(2).to_broadcast([128, EJ, WIN]),
                op=ALU.is_equal)

        def copy_index(index, g, slot):
            return nc.vector.tensor_scalar(idx[:, slot, :], index[:, bass.ds(g, 1), :].rearrange("p a j -> p (a j)"),
                                           0.0, None, ALU.add)

        def weighted_pass(index, weights, R, first_layer):
            def weigh(g, slot):
                return nc.vector.tensor_tensor(
                    onehot_w[:, slot, :, 0:R, :],
                    onehot[:, slot].unsqueeze(2).to_broadcast([128, EJ, R, WIN]),
                    weights[:, bass.ds(g, 1), :, :].rearrange("p a j r -> p (a j) r").unsqueeze(3)
                    .to_broadcast([128, EJ, R, WIN]), op=ALU.mult)

            adds = 2 if first_layer else 1

            def prepare(v, g, slot):
                build_onehot(g, slot).then_inc(onehot_built, 1)
                if first_layer:
                    nc.vector.tensor_copy(deg_c[:, slot].rearrange("p j r -> p (j r)"),
                                          deg_w[:, bass.ds(g, 1), :, :].rearrange("p a j r -> p (a j r)")
                                          ).then_inc(onehot_built, 1)
                v.wait_ge(onehot_built, adds * (g + 1))
                weigh(g, slot).then_inc(onehot_ready, 1)

            with nc.Block(no_gpsimd_drain=True) as block:
                @block.gpsimd
                def _(pool):
                    gather_rows(pool, 2 * N if index is srcsign_i else N)

                @block.vector
                def _(v):
                    for s in range(UN):
                        copy_index(index, s, s).then_inc(idx_ready[s], 1)
                    prepare(v, 0, 0)
                    with v.Fori(0, G // UN) as i:
                        for s in range(UN):
                            g = i * UN + s
                            prepare(v, g + 1, (s + 1) % 2)
                            col = v.value_load(win_row[0:1, bass.ds(g, 1)], min_val=0, max_val=N)
                            v.wait_ge(summed, g + 1)
                            nc.vector.tensor_tensor(
                                acc[:, 0:R, bass.ds(col, WIN)], acc[:, 0:R, bass.ds(col, WIN)],
                                ps[0:D, s % 2, 0:R * WIN].rearrange("p (r w) -> p r w", r=R),
                                op=ALU.add).then_inc(acc_added, 1)
                            if first_layer:
                                nc.vector.tensor_tensor(
                                    acc_deg[:, bass.ds(col, WIN)], acc_deg[:, bass.ds(col, WIN)],
                                    ps[D:D + 3, s % 2, 256:256 + WIN], op=ALU.add).then_inc(acc_added, 1)
                            copy_index(index, g + UN, s).then_inc(idx_ready[s], 1)
                            v.wait_ge(acc_added, adds * g + adds)
                    next_windows(v, 0)

                @block.tensor
                def _(pe):
                    with pe.Fori(0, G // UN) as i:
                        for s in range(UN):
                            g = i * UN + s
                            if first_layer:
                                pe.wait_ge(attr_loaded[s], i * 16 + 16)
                                pe.wait_ge(attr_kept, g + 1)
                                nc.tensor.transpose(ps[:, 2 + s % 2, 0:128], attr_in[:, s, :],
                                                    ident[:, :]).then_inc(attr_turned, 1)
                            pe.wait_ge(gathered[s], i * (16 * EJ) + 16 * EJ)
                            pe.wait_ge(onehot_ready, g + 1)
                            for j in range(EJ):
                                m = nc.tensor.matmul(ps[0:D, s % 2, 0:R * WIN], gath[:, s, j, :],
                                                     onehot_w[:, s % 2, j, 0:R, :].rearrange("p r w -> p (r w)"),
                                                     start=(j == 0), stop=(j == EJ - 1))
                            if first_layer:
                                for j in range(EJ):
                                    m = nc.tensor.matmul(
                                        ps[D:D + 3, s % 2, 256:256 + WIN],
                                        deg_c[:, s % 2, j, :],
                                        onehot[:, s % 2, j, :], start=(j == 0), stop=(j == EJ - 1))
                            m.then_inc(summed, 1)

                if first_layer:
                    @block.scalar
                    def _(act):
                        act.sem_inc(attr_kept, 2)
                        with act.Fori(0, G // UN) as i:
                            for s in range(UN):
                                g = i * UN + s
                                act.wait_ge(attr_turned, g + 1)
                                act.sem_inc(attr_seen, 1)
                                nc.scalar.copy(attr_t[:, bass.ds(g, 1), :].rearrange("p a c -> p (a c)"),
                                               ps[:, 2 + s % 2, 0:128]).then_inc(attr_kept, 1)

                    @block.sync
                    def _(sp):
                        attr = a["edge_attr_32"]

                        def load(g, s, parts=128):
                            rows = attr[bass.ds(g * GE, parts * EJ), :]
                            sp.dma_start(attr_in[0:parts, s, :],
                                         rows.rearrange("(p j) k -> p (j k)", j=EJ)).then_inc(attr_loaded[s], 16)
                        for s in range(UN):
                            load(s, s)
                        with sp.Fori(0, G // UN - 2) as i:
                            for s in range(UN):
                                sp.wait_ge(attr_turned, i * UN + s + 1)
                                load(i * UN + s + UN, s)
                        for s in range(UN - 1):
                            sp.wait_ge(attr_turned, G - 2 * UN + s + 1)
                            load(G - UN + s, s)
                        sp.wait_ge(attr_turned, G - UN)
                        whole, rest = TAIL // EJ, TAIL % EJ
                        if rest:
                            e0 = E - rest
                            sp.dma_start(attr_in[whole:whole + 1, UN - 1, 0:rest * ED],
                                         attr[e0:E, :].rearrange("j k -> (j k)").unsqueeze(0)).then_inc(loads, 16)
                            sp.wait_ge(loads, 16)
                        load(G - 1, UN - 1, parts=whole)
            rejoin()

        def weighted_round(index, weights, R, first_layer=False):
            reset_windows()
            rejoin()
            with nc.Fori(0, SPAN):
                weighted_pass(index, weights, R, first_layer)

        def turn_h(pe, src, n_wait, banks=(0, 1), turned=None, free=None, base=0):
            for c, (b0, b1) in enumerate(chunks(TB, 4)):
                if n_wait is not None and c >= 2:
                    pe.wait_ge(free, base + c - 1)
                for b in range(b0, b1):
                    t = nc.tensor.transpose(ps[0:D, banks[c % 2], (b - b0) * TP:(b - b0 + 1) * TP],
                                            src[:, b, :], ident[0:TP, 0:TP])
                t.then_inc(turned, 1)

        GRU_CHUNKS = chunks(TB, 8)
        with nc.Fori(0, 2):
            weighted_round(src_i, rel_w, REL, first_layer=True)
            with nc.Block() as block:
                def turn(pe, q):
                    pe.wait_ge(hnew_ready, q + 1)
                    b0, b1 = GRU_CHUNKS[q]
                    for c in range(2):
                        for b in range(b0 + 4 * c, max(b0 + 4 * c + 1, min(b1, b0 + 4 * c + 4))):
                            src_b = min(b, b1 - 1)
                            m = nc.tensor.transpose(ps[0:D, 4 * (q % 2) + c, (b - b0 - 4 * c) * TP:(b - b0 - 4 * c + 1) * TP],
                                                    h[:, src_b, :], ident[0:TP, 0:TP])
                        m.then_inc(hnew_turned, 1)

                @block.tensor
                def _(pe):
                    for c, (n0, n1) in enumerate(chunks(N, 512)):
                        if c >= 2:
                            pe.wait_ge(swh_ready, c - 1)
                        for r in range(REL):
                            m = nc.tensor.matmul(ps[0:D, c % 2, 0:n1 - n0], wrel[:, r, :], acc[:, r, n0:n1],
                                                 start=(r == 0), stop=(r == REL - 1))
                        m.then_inc(swh_sum, 1)
                    for b in range(TB):
                        m = nc.tensor.transpose(ps[0:TP, 2, 3 * b:3 * b + 3],
                                                acc_deg[:, b:b + TB * (TP - 1) + 1:TB], ident[D:D + 3, D:D + 3])
                    m.then_inc(deg_turned, 1)
                    pe.wait_ge(swh_ready, len(chunks(N, 512)))
                    pe.wait_ge(deg_read, 1)
                    pe.wait_ge(pool_done, 1)
                    for q, (b0, b1) in enumerate(GRU_CHUNKS):
                        if q >= 2:
                            pe.wait_ge(ht_ready, 2 * q - 2)
                        for b in range(b0, b1):
                            t = ps[0:TP, 4 * (q % 2) + (b - b0) // 2,
                                   256 * ((b - b0) % 2):256 * ((b - b0) % 2) + 256]
                            s_b = swh_t[:, b:b + TB * (TP - 1) + 1:TB]
                            nc.tensor.matmul(t[:, 0:3 * D], s_b, w_ih[:].rearrange("p g e -> p (g e)"),
                                             start=True, stop=False)
                            nc.tensor.matmul(t[:, D:3 * D], h_t[:, b, :], w_hh[:, 0:2, :].rearrange("p g e -> p (g e)"),
                                             start=False, stop=True)
                            m = nc.tensor.matmul(t[:, 3 * D:4 * D], h_t[:, b, :], w_hh[:, 2, :], start=True, stop=True)
                        m.then_inc(gates_done, 1)
                        if q >= 1:
                            turn(pe, q - 1)
                    turn(pe, len(GRU_CHUNKS) - 1)

                @block.scalar
                def _(act):
                    for c, (n0, n1) in enumerate(chunks(N, 512)):
                        act.wait_ge(swh_sum, c + 1)
                        nc.scalar.copy(swh_t[0:D, n0:n1], ps[0:D, c % 2, 0:n1 - n0]).then_inc(swh_ready, 1)

                    def keep(q):
                        b0, b1 = GRU_CHUNKS[q]
                        for c in range(2):
                            act.wait_ge(hnew_turned, 2 * q + c + 1)
                            t0, t1 = min(b0 + 4 * c, b1 - 1), min(b1, b0 + 4 * c + 4)
                            nc.scalar.copy(h_t[0:D, t0:t1, :],
                                           ps[0:D, 4 * (q % 2) + c, 0:(t1 - t0) * TP]
                                           .rearrange("p (b n) -> p b n", n=TP)).then_inc(ht_ready, 1)
                            if c == 0 and t1 == b1:
                                act.wait_ge(ht_ready, 2 * q + 1)

                    for q, (b0, b1) in enumerate(GRU_CHUNKS):
                        act.wait_ge(gates_done, q + 1)
                        t = ps[0:TP, 4 * (q % 2):4 * (q % 2) + 4, :].rearrange("p k (t c) -> p (k t) c", t=2)[:, 0:b1 - b0, :]
                        nc.scalar.activation(rz[:, q % 2, 0:b1 - b0, :], t[:, :, D:3 * D], ACT.Sigmoid).then_inc(rz_ready, 1)
                        act.wait_ge(pre_ready, q + 1)
                        nc.scalar.activation(cand[:, q % 2, 0:b1 - b0, :], cand[:, q % 2, 0:b1 - b0, :],
                                             ACT.Tanh).then_inc(cand_ready, 1)
                        if q >= 1:
                            keep(q - 1)
                    keep(len(GRU_CHUNKS) - 1)

                @block.vector
                def _(v):
                    link = linked(v, dve_done)
                    v.wait_ge(deg_turned, 1)
                    nc.vector.tensor_copy(deg[:], ps[0:TP, 2, 0:3 * TB].rearrange("p (b k) -> p b k", k=3)).then_inc(deg_read, 1)
                    for q, (b0, b1) in enumerate(GRU_CHUNKS):
                        n = b1 - b0
                        t = ps[0:TP, 4 * (q % 2):4 * (q % 2) + 4, :].rearrange("p k (t c) -> p (k t) c", t=2)[:, 0:n, :]
                        r_, z_ = rz[:, q % 2, 0:n, 0:D], rz[:, q % 2, 0:n, D:2 * D]
                        cn, mx = cand[:, q % 2, 0:n, :], mix[:, q % 2, 0:n, :]
                        v.wait_ge(rz_ready, q + 1)
                        link(nc.vector.tensor_tensor(cn, r_, t[:, :, 3 * D:4 * D], op=ALU.mult))
                        nc.vector.tensor_tensor(cn, cn, t[:, :, 0:D], op=ALU.add).then_inc(pre_ready, 1)
                        v.wait_ge(cand_ready, q + 1)
                        link(nc.vector.tensor_tensor(mx, y[:, b0:b1, :], cn, op=ALU.subtract))
                        link(nc.vector.tensor_tensor(mx, mx, z_, op=ALU.mult))
                        nc.vector.tensor_tensor(h[:, b0:b1, :], cn, mx, op=ALU.add).then_inc(hnew_ready, 1)
                    v.wait_ge(hnew_ready, len(GRU_CHUNKS))
                    link(nc.vector.tensor_copy(y[:], h[:]))

                @block.sync
                def _(sp):
                    sp.wait_ge(hnew_ready, len(GRU_CHUNKS))
                    sp.dma_start(table_h, h[:]).then_inc(stored, 16)
                    sp.wait_ge(stored, 16)

                @block.gpsimd
                def _(pool):
                    nc.gpsimd.memset(swh_t[D:D + 1, :], 1.0).then_inc(pool_done, 1)
                    pool.wait_ge(pool_done, 1)
                    pool.wait_ge(swh_sum, len(chunks(N, 512)))
                    pool.wait_ge(deg_turned, 1)
                    nc.gpsimd.memset(acc_all[:], 0.0).then_inc(pool_done, 1)
                    pool.wait_ge(pool_done, 2)
            rejoin()

        def signed_tables_pe(pe, src, n_turn):
            for k in range(2):
                for c, (b0, b1) in enumerate(chunks(TB, 4)):
                    i = k * n_turn + c
                    if i >= 2:
                        pe.wait_ge(ps_read, i - 1)
                    for b in range(b0, b1):
                        t = nc.tensor.transpose(ps[0:D, 4 + i % 2, (b - b0) * TP:(b - b0 + 1) * TP],
                                                src(k, b), ident[0:TP, 0:TP])
                    t.then_inc(pe_step, 1)

        def signed_tables_act(act, n_turn):
            for k in range(2):
                for c, (b0, b1) in enumerate(chunks(TB, 4)):
                    i = k * n_turn + c
                    act.wait_ge(pe_step, i + 1)
                    nc.scalar.copy(by_tile(acc[:, k, 0:N])[:, b0:b1, :],
                                   ps[0:D, 4 + i % 2, 0:(b1 - b0) * TP].rearrange("p (b n) -> p b n", n=TP)
                                   ).then_inc(ps_read, 1)

        T4 = len(chunks(TB, 4))
        with nc.Block() as block:
            @block.vector
            def _(v):
                link = linked(v, dve_done)
                flat = h_t[0:D].rearrange("p b n -> p (b n)")
                for c, (n0, n1) in enumerate(chunks(N, 512)):
                    link(nc.vector.bn_stats(bn6[:, c, :], flat[:, n0:n1]))
                nc.vector.bn_aggr(bn2[:], bn6[:].rearrange("p c k -> p (c k)")).then_inc(misc, 1)
                v.wait_ge(misc, 2)
                link(nc.vector.reciprocal(bnsc[:, 0:1], bnsc[:, 2:3]))
                link(nc.vector.tensor_tensor(bnsc[:, 0:1], bnsc[:, 0:1], gb[:, 0:1], op=ALU.mult))
                link(nc.vector.tensor_scalar(hid_t[0:D, 0:N], flat, bn2[:, 0:1], None, ALU.subtract))
                nc.vector.tensor_scalar(hid_t[0:D, 0:N], hid_t[0:D, 0:N], bnsc[:, 0:1], gb[:, 1:2],
                                        ALU.mult, ALU.add).then_inc(swh_ready, 1)
                for c, (b0, b1) in enumerate(chunks(TB, 8)):
                    v.wait_ge(swh_sum, c + 1)
                    nc.vector.tensor_tensor(x[:, b0:b1, :], x[:, b0:b1, :],
                                            ps[0:TP, c % 2, 0:(b1 - b0) * D].rearrange("p (b c) -> p b c", c=D),
                                            op=ALU.add).then_inc(deg_read, 1)
                v.wait_ge(deg_read, 4)
                link(nc.vector.tensor_scalar(deg[:, :, 0:2], deg[:, :, 0:2], 1.0, None, ALU.add))
                nc.vector.tensor_scalar(deg[:, :, 2:3], deg[:, :, 2:3], 1.0, None, ALU.max).then_inc(deg_turned, 1)
                v.wait_ge(deg_turned, 2)
                link(nc.vector.reciprocal(deg[:], deg[:]))
                link(nc.vector.tensor_scalar(ndinv[:], deg[:, :, 1], -1.0, None, ALU.mult))
                layer_norm(v, link, x, h)
                relu(link, h)
                for k in range(2):
                    nc.vector.tensor_tensor(wide[:, :, k * D:(k + 1) * D], h[:], row_bc(deg[:, :, k], D),
                                            op=ALU.mult).then_inc(h_ready, 1)

            @block.scalar
            def _(act):
                act.wait_ge(misc, 1)
                nc.scalar.activation(bnsc[:, 2:3], bn2[:, 1:2], ACT.Sqrt, bias=epsc[0:D, :]).then_inc(misc, 1)
                act.wait_ge(deg_turned, 1)
                nc.scalar.activation(deg[:, :, 0:2], deg[:, :, 0:2], ACT.Sqrt).then_inc(deg_turned, 1)
                std(act)
                signed_tables_act(act, T4)

            @block.tensor
            def _(pe):
                pe.wait_ge(swh_ready, 1)
                for c, (b0, b1) in enumerate(chunks(TB, 8)):
                    if c >= 2:
                        pe.wait_ge(deg_read, c - 1)
                    for b in range(b0, b1):
                        t = nc.tensor.transpose(ps[0:TP, c % 2, (b - b0) * D:(b - b0 + 1) * D],
                                                hid_t[0:D, b * TP:(b + 1) * TP], ident[0:D, 0:D])
                    t.then_inc(swh_sum, 1)
                pe.wait_ge(h_ready, 2)
                signed_tables_pe(pe, lambda k, b: wide[:, b, k * D:(k + 1) * D], T4)

            @block.sync
            def _(sp):
                sp.wait_ge(h_ready, 1)
                sp.dma_start(table_h, wide[:, :, 0:D]).then_inc(stored, 16)
                sp.wait_ge(h_ready, 2)
                sp.dma_start(table_n, wide[:, :, D:2 * D]).then_inc(stored, 16)
                sp.wait_ge(stored, 32)
        rejoin()

        weighted_round(srcsign_i, sign_w, 2)

        with nc.Block() as block:
            @block.tensor
            def _(pe):
                for c, (b0, b1) in enumerate(chunks(TB, 2)):
                    if c >= 2:
                        pe.wait_ge(swh_ready, c - 1)
                    for b in range(b0, b1):
                        for k in range(2):
                            m = nc.tensor.matmul(ps[0:TP, c % 2, (2 * (b - b0) + k) * 128:(2 * (b - b0) + k + 1) * 128],
                                                 acc[:, k, b:b + TB * (TP - 1) + 1:TB], w1pn[:, k, :],
                                                 start=True, stop=True)
                    m.then_inc(swh_sum, 1)
                pe.wait_ge(h_ready, 1)
                for c, (b0, b1) in enumerate(chunks(TB, 4)):
                    if c >= 2:
                        pe.wait_ge(ht_ready, c - 1)
                    for b in range(b0, b1):
                        m = nc.tensor.transpose(ps[:, 2 + c % 2, (b - b0) * TP:(b - b0 + 1) * TP], wide[:, b, :],
                                                ident[0:TP, 0:TP])
                    m.then_inc(hnew_turned, 1)
                for c, (b0, b1) in enumerate(chunks(TB, 4)):
                    pe.wait_ge(ht_ready, c + 1)
                    if c >= 2:
                        pe.wait_ge(deg_read, c - 1)
                    for b in range(b0, b1):
                        m = nc.tensor.matmul(ps[0:TP, 6 + c % 2, (b - b0) * 128:(b - b0 + 1) * 128],
                                             hid_t[:, b * TP:(b + 1) * TP], w2pn[:].rearrange("p k e -> p (k e)"),
                                             start=True, stop=True)
                    m.then_inc(gates_done, 1)
                pe.wait_ge(deg_read, T4)
                signed_tables_pe(pe, lambda k, b: wide[:, b, k * D:(k + 1) * D], T4)

            @block.scalar
            def _(act):
                for c, (b0, b1) in enumerate(chunks(TB, 4)):
                    act.wait_ge(hnew_turned, c + 1)
                    nc.scalar.copy(hid_t[:, b0 * TP:b1 * TP], ps[:, 2 + c % 2, 0:(b1 - b0) * TP]).then_inc(ht_ready, 1)
                signed_tables_act(act, T4)

            @block.vector
            def _(v):
                link = linked(v, dve_done)
                for c, (b0, b1) in enumerate(chunks(TB, 2)):
                    v.wait_ge(swh_sum, c + 1)
                    for b in range(b0, b1):
                        o = 2 * (b - b0) * 128
                        nc.vector.scalar_tensor_tensor(wide[:, b, :], ps[0:TP, c % 2, o:o + 128], deg[:, b, 0:1],
                                                       b1pn[:, 0], ALU.mult, ALU.add).then_inc(misc, 1)
                    v.wait_ge(misc, b1)
                    for b in range(b0, b1):
                        o = (2 * (b - b0) + 1) * 128
                        m = nc.vector.scalar_tensor_tensor(wide[:, b, :], ps[0:TP, c % 2, o:o + 128], ndinv[:, b:b + 1],
                                                           wide[:, b, :], ALU.mult, ALU.add)
                    m.then_inc(swh_ready, 1)
                v.wait_ge(swh_ready, len(chunks(TB, 2)))
                nc.vector.tensor_scalar(wide[:], wide[:], 0.0, None, ALU.max).then_inc(h_ready, 1)
                v.wait_ge(hnew_turned, T4)
                for c, (b0, b1) in enumerate(chunks(TB, 4)):
                    v.wait_ge(gates_done, c + 1)
                    nc.vector.tensor_tensor(
                        wide[:, b0:b1, :].rearrange("p b (k e) -> p b k e", k=2),
                        ps[0:TP, 6 + c % 2, 0:(b1 - b0) * 128].rearrange("p (b k e) -> p b k e", k=2, e=D),
                        deg[:, b0:b1, 0:2].unsqueeze(3).to_broadcast([TP, b1 - b0, 2, D]),
                        op=ALU.mult).then_inc(deg_read, 1)

            @block.sync
            def _(sp):
                sp.wait_ge(deg_read, T4)
                sp.dma_start(table_h, wide[:, :, 0:D]).then_inc(stored, 16)
                sp.dma_start(table_n, wide[:, :, D:2 * D]).then_inc(stored, 16)
                sp.wait_ge(stored, 32)
        rejoin()

        weighted_round(srcsign_i, sign_w, 2)

        def turned_h_pe(pe, src):
            for c, (b0, b1) in enumerate(chunks(TB, 4)):
                if c >= 2:
                    pe.wait_ge(ht_ready, c - 1)
                for b in range(b0, b1):
                    m = nc.tensor.transpose(ps[0:D, 6 + c % 2, (b - b0) * TP:(b - b0 + 1) * TP], src[:, b, :],
                                            ident[0:TP, 0:TP])
                m.then_inc(hnew_turned, 1)

        def turned_h_act(act):
            for c, (b0, b1) in enumerate(chunks(TB, 4)):
                act.wait_ge(hnew_turned, c + 1)
                nc.scalar.copy(h_t[0:D, b0:b1, :], ps[0:D, 6 + c % 2, 0:(b1 - b0) * TP]
                               .rearrange("p (b n) -> p b n", n=TP)).then_inc(ht_ready, 1)

        with nc.Block() as block:
            @block.tensor
            def _(pe):
                for c, (b0, b1) in enumerate(chunks(TB, 4)):
                    if c >= 2:
                        pe.wait_ge(swh_ready, c - 1)
                    for b in range(b0, b1):
                        for k in range(2):
                            o = (2 * (b - b0) + k) * D
                            m = nc.tensor.transpose(ps[0:TP, c % 2, o:o + D], acc[:, k, b:b + TB * (TP - 1) + 1:TB],
                                                    ident[0:D, 0:D])
                    m.then_inc(swh_sum, 1)
                pe.wait_ge(h_ready, 1)
                turned_h_pe(pe, h)

            @block.vector
            def _(v):
                link = linked(v, dve_done)
                for c, (b0, b1) in enumerate(chunks(TB, 4)):
                    v.wait_ge(swh_sum, c + 1)
                    nc.vector.tensor_tensor(
                        wide[:, b0:b1, :].rearrange("p b (k e) -> p b k e", k=2),
                        ps[0:TP, c % 2, 0:(b1 - b0) * 128].rearrange("p (b k e) -> p b k e", k=2, e=D),
                        deg[:, b0:b1, 0:2].unsqueeze(3).to_broadcast([TP, b1 - b0, 2, D]),
                        op=ALU.mult).then_inc(swh_ready, 1)
                v.wait_ge(swh_ready, T4)
                link(nc.vector.tensor_tensor(h[:], wide[:, :, 0:D], wide[:, :, D:2 * D], op=ALU.subtract))
                link(nc.vector.tensor_tensor(h[:], h[:], const_bc(b2pn[:, 0]), op=ALU.add))
                link(nc.vector.tensor_scalar(h[:], h[:], 0.0, None, ALU.max))
                link(nc.vector.tensor_tensor(x[:], x[:], h[:], op=ALU.add))
                layer_norm(v, link, x, h)
                nc.vector.tensor_scalar(h[:], h[:], 0.0, None, ALU.max).then_inc(h_ready, 1)

            @block.scalar
            def _(act):
                std(act)
                turned_h_act(act)

            @block.gpsimd
            def _(pool):
                pool.wait_ge(swh_sum, T4)
                nc.gpsimd.memset(acc[:, 0:2, :], 0.0).then_inc(pool_done, 1)
                pool.wait_ge(pool_done, 1)

            @block.sync
            def _(sp):
                sp.wait_ge(h_ready, 1)
                sp.dma_start(table_h, h[:]).then_inc(stored, 16)
                sp.wait_ge(stored, 16)
        rejoin()

        with nc.Fori(0, 2) as l:
            weighted_round(src_i, spline_w, 2)
            with nc.Block() as block:
                @block.tensor
                def _(pe):
                    pe.wait_ge(cleared, 1)
                    for c, (b0, b1) in enumerate(chunks(TB, 4)):
                        if c >= 2:
                            pe.wait_ge(swh_ready, c - 1)
                        for b in range(b0, b1):
                            o = 2 * (b - b0) * D
                            for k, col in enumerate((S_W0, S_W1)):
                                nc.tensor.matmul(ps[0:TP, c % 2, o:o + D], acc[:, k, b:b + TB * (TP - 1) + 1:TB],
                                                 spl[0:D, col:col + D], start=(k == 0), stop=(k == 1))
                            m = nc.tensor.matmul(ps[0:TP, c % 2, o + D:o + 2 * D], h_t[:, b, :],
                                                 spl[0:D + 1, S_ROOT:S_ROOT + D], start=True, stop=True)
                        m.then_inc(swh_sum, 1)
                    pe.wait_ge(h_ready, 1)
                    turned_h_pe(pe, h)

                @block.vector
                def _(v):
                    nc.vector.tensor_copy(spl[:], spl_all[:, bass.ds(l, 1), :].rearrange("p a c -> p (a c)")).then_inc(cleared, 1)
                    for c, (b0, b1) in enumerate(chunks(TB, 4)):
                        v.wait_ge(swh_sum, c + 1)
                        t = ps[0:TP, c % 2, 0:(b1 - b0) * 128].rearrange("p (b k e) -> p b k e", k=2, e=D)
                        nc.vector.tensor_tensor(wide[:, b0:b1, 0:D], t[:, :, 0, :], row_bc(deg[:, b0:b1, 2], D),
                                                op=ALU.mult).then_inc(misc, 1)
                        v.wait_ge(misc, c + 1)
                        nc.vector.tensor_tensor(h[:, b0:b1, :], wide[:, b0:b1, 0:D], t[:, :, 1, :],
                                                op=ALU.add).then_inc(swh_ready, 1)
                    v.wait_ge(swh_ready, T4)
                    v.sem_inc(h_ready, 1)

                @block.scalar
                def _(act):
                    turned_h_act(act)

                @block.gpsimd
                def _(pool):
                    pool.wait_ge(swh_sum, T4)
                    nc.gpsimd.memset(acc[:, 0:2, :], 0.0).then_inc(pool_done, 1)
                    pool.wait_ge(pool_done, 1)

                @block.sync
                def _(sp):
                    sp.wait_ge(h_ready, 1)
                    sp.dma_start(table_h, h[:]).then_inc(stored, 16)
                    sp.wait_ge(stored, 16)
            rejoin()

        with nc.Block() as block:
            @block.vector
            def _(v):
                link = linked(v, dve_done)
                link(nc.vector.tensor_tensor(x[:], x[:], h[:], op=ALU.add))
                layer_norm(v, link, x, y)
                relu(link, y)

            @block.scalar
            def _(act):
                std(act)
        rejoin()

        with nc.Fori(0, L3L) as l:
            with nc.Block() as block:
                @block.tensor
                def _(pe):
                    turned_h_pe(pe, y)
                    pe.wait_ge(loads, 16)
                    pe.wait_ge(ht_ready, T4)
                    flat = h_t[0:D].rearrange("p b n -> p (b n)")
                    for c, (n0, n1) in enumerate(chunks(N, 500)):
                        if c >= 2:
                            pe.wait_ge(rz_ready, c - 1)
                        nc.tensor.matmul(ps[:, c % 2, 0:n1 - n0], eg[0:D, C_W1:C_W1 + 2 * D], flat[:, n0:n1],
                                         start=True, stop=True).then_inc(swh_sum, 1)
                    for c, (b0, b1) in enumerate(chunks(TB, 8)):
                        pe.wait_ge(cand_ready, min(2 * c + 2, len(chunks(N, 500))))
                        if c >= 2:
                            pe.wait_ge(swh_ready, c - 1)
                        for b in range(b0, b1):
                            m = nc.tensor.matmul(ps[0:TP, 2 + c % 2, (b - b0) * D:(b - b0 + 1) * D],
                                                 hid_t[:, b * TP:(b + 1) * TP], eg[:, C_W2:C_W2 + D],
                                                 start=True, stop=True)
                        m.then_inc(gates_done, 1)

                @block.vector
                def _(v):
                    for c, (n0, n1) in enumerate(chunks(N, 500)):
                        v.wait_ge(rz_ready, c + 1)
                        nc.vector.scalar_tensor_tensor(hid_t[:, n0:n1], hid_t[:, n0:n1], 0.1, hid_t[:, n0:n1],
                                                       ALU.mult, ALU.max).then_inc(cand_ready, 1)
                    for c, (b0, b1) in enumerate(chunks(TB, 8)):
                        v.wait_ge(gates_done, c + 1)
                        nc.vector.tensor_tensor(
                            h[:, b0:b1, :], ps[0:TP, 2 + c % 2, 0:(b1 - b0) * D].rearrange("p (b e) -> p b e", e=D),
                            eg[0:TP, C_B2:C_B2 + D].unsqueeze(1).to_broadcast([TP, b1 - b0, D]),
                            op=ALU.add).then_inc(swh_ready, 1)

                @block.scalar
                def _(act):
                    turned_h_act(act)
                    act.wait_ge(loads, 16)
                    for c, (n0, n1) in enumerate(chunks(N, 500)):
                        act.wait_ge(swh_sum, c + 1)
                        nc.scalar.activation(hid_t[:, n0:n1], ps[:, c % 2, 0:n1 - n0], ACT.Identity,
                                             bias=eg[:, C_B1:C_B1 + 1]).then_inc(rz_ready, 1)

                @block.gpsimd
                def _(pool):
                    nc.gpsimd.memset(acc[:, 0, :], 0.0).then_inc(pool_done, 1)
                    pool.wait_ge(pool_done, 1)

                @block.sync
                def _(sp):
                    sp.dma_start(eg[:], eg_dram[bass.ds(l, 1)].rearrange("a p c -> (a p) c")).then_inc(loads, 16)
                    sp.wait_ge(swh_ready, len(chunks(TB, 8)))
                    sp.dma_start(table_h, h[:]).then_inc(stored, 16)
                    sp.wait_ge(stored, 16)
            rejoin()
            reset_windows()
            rejoin()
            with nc.Fori(0, SPAN):
                with nc.Block(no_gpsimd_drain=True) as block:
                    @block.gpsimd
                    def _(pool):
                        gather_rows(pool, N)

                    @block.scalar
                    def _(act):
                        with act.Fori(0, (G + 2) // 2) as i:
                            for s in range(2):
                                act.wait_ge(hid_sum, i * 2 + s + 1)
                                nc.scalar.activation(hid_e[:, s, :], ps[:, 2 + s, 0:256], ACT.Identity,
                                                     bias=eg[:, C_BE1:C_BE1 + 1]).then_inc(hid_biased, 1)

                    @block.tensor
                    def _(pe):
                        def hidden(g, s):
                            for k in range(2):
                                m = nc.tensor.matmul(ps[:, 2 + s, 128 * k:128 * k + 128],
                                                     eg[:, C_WE1 + 128 * k:C_WE1 + 128 * k + 128],
                                                     attr_t[:, bass.ds(g, 1), :].rearrange("p a c -> p (a c)"),
                                                     start=True, stop=True)
                            m.then_inc(hid_sum, 1)

                        def gates(s):
                            nc.tensor.matmul(ps[:, 4 + s, 0:256], ones_row[:], eg[0:1, C_BE2:C_BE2 + 256],
                                             start=True, stop=False)
                            for k in range(2):
                                m = nc.tensor.matmul(ps[:, 4 + s, 128 * k:128 * k + 128], hid_e[:, s, 128 * k:128 * k + 128],
                                                     eg[:, C_WE2:C_WE2 + 128], start=False, stop=(k == 1))
                            m.then_inc(gate_done, 1)

                        hidden(0, 0)
                        hidden(1, 1)
                        pe.wait_ge(hid_ready, 1)
                        gates(0)
                        with pe.Fori(0, G // UN) as i:
                            for s in range(UN):
                                g = i * UN + s
                                pe.wait_ge(hid_ready, g + 2)
                                gates((s + 1) % 2)
                                hidden(g + 2, s % 2)
                                pe.wait_ge(msg_ready, g + 1)
                                for j in range(EJ):
                                    m = nc.tensor.matmul(ps[0:D, s % 2, 0:WIN], msg[:, s % 2, j, :],
                                                         onehot[:, s % 2, j, :], start=(j == 0), stop=(j == EJ - 1))
                                m.then_inc(summed, 1)

                    @block.vector
                    def _(v):
                        for s in range(UN):
                            copy_index(src_i, s, s).then_inc(idx_ready[s], 1)
                        build_onehot(0, 0).then_inc(onehot_built, 1)
                        v.wait_ge(onehot_built, 1)

                        def leak(g, s):
                            v.wait_ge(hid_biased, g + 1)
                            nc.vector.scalar_tensor_tensor(hid_e[:, s, :], hid_e[:, s, :], 0.1, hid_e[:, s, :],
                                                           ALU.mult, ALU.max).then_inc(hid_ready, 1)
                        leak(0, 0)
                        leak(1, 1)
                        with v.Fori(0, G // UN) as i:
                            for s in range(UN):
                                g = i * UN + s
                                v.wait_ge(gathered[s], i * (16 * EJ) + 16 * EJ)
                                v.wait_ge(gate_done, g + 1)
                                nc.vector.tensor_tensor(msg[:, s % 2].rearrange("p j c -> p (j c)"),
                                                        gath[:, s].rearrange("p j c -> p (j c)"),
                                                        ps[:, 4 + s % 2, 0:256], op=ALU.mult).then_inc(msg_ready, 1)
                                build_onehot(g + 1, (s + 1) % 2).then_inc(onehot_built, 1)
                                col = v.value_load(win_row[0:1, bass.ds(g, 1)], min_val=0, max_val=N)
                                v.wait_ge(summed, g + 1)
                                nc.vector.tensor_tensor(acc[:, 0, bass.ds(col, WIN)], acc[:, 0, bass.ds(col, WIN)],
                                                        ps[0:D, s % 2, 0:WIN], op=ALU.add).then_inc(acc_added, 1)
                                copy_index(src_i, g + UN, s).then_inc(idx_ready[s], 1)
                                leak(g + 2, s % 2)
                                v.wait_ge(onehot_built, g + 2)
                                v.wait_ge(acc_added, g + 1)
                        next_windows(v, 0)
                rejoin()

            with nc.Block() as block:
                @block.tensor
                def _(pe):
                    for c, (b0, b1) in enumerate(chunks(TB, 8)):
                        if c >= 2:
                            pe.wait_ge(swh_ready, c - 1)
                        for b in range(b0, b1):
                            m = nc.tensor.transpose(ps[0:TP, c % 2, (b - b0) * D:(b - b0 + 1) * D],
                                                    acc[:, 0, b:b + TB * (TP - 1) + 1:TB], ident[0:D, 0:D])
                        m.then_inc(swh_sum, 1)

                @block.vector
                def _(v):
                    link = linked(v, dve_done)
                    link(nc.vector.tensor_tensor(eg[:, C_RES:C_RES + 1], eg[:, C_RES:C_RES + 1],
                                                 eg[:, C_DOT:C_DOT + 1], op=ALU.mult))
                    for c, (b0, b1) in enumerate(chunks(TB, 8)):
                        v.wait_ge(swh_sum, c + 1)
                        nc.vector.scalar_tensor_tensor(
                            y[:, b0:b1, :].rearrange("p b e -> p (b e)"), ps[0:TP, c % 2, 0:(b1 - b0) * D],
                            eg[0:TP, C_RES:C_RES + 1], y[:, b0:b1, :].rearrange("p b e -> p (b e)"),
                            ALU.mult, ALU.add).then_inc(swh_ready, 1)
                    v.wait_ge(swh_ready, len(chunks(TB, 8)))
                    layer_norm(v, link, y, h, (eg[0:TP, C_G:C_G + D], eg[0:TP, C_B:C_B + D]))
                    link(nc.vector.tensor_copy(y[:], h[:]))

                @block.scalar
                def _(act):
                    std(act)
            rejoin()

        with nc.Block() as block:
            @block.vector
            def _(v):
                nc.vector.tensor_tensor(x[:], x[:], y[:], op=ALU.add).then_inc(h_ready, 1)

            @block.sync
            def _(sp):
                sp.wait_ge(h_ready, 1)
                sp.dma_start(out.rearrange("(p b) c -> p b c", b=TB), x[:]).then_inc(out_done, 16)
                sp.wait_ge(out_done, 16)


def kernel(**inputs):
    import numpy as np
    import concourse.bacc as bacc
    from concourse.bass_utils import run_bass_kernel_spmd as run

    nc = bacc.Bacc("TRN2", target_bir_lowering=False, num_devices=1)
    arrays, args = {}, {}
    for name, value in inputs.items():
        arr = np.ascontiguousarray(value)
        arrays[f"in_{name}"] = arr
        args[name] = nc.dram_tensor(f"in_{name}", arr.shape, mybir.dt.from_np(arr.dtype), kind="ExternalInput").ap()
    out = nc.dram_tensor("out", (N, D), F32, kind="ExternalOutput").ap()
    gnn_kernel(nc, args, out)
    r = run(nc, [arrays], core_ids=[0])
    return r.results[0]["out"]
```

```python
import concourse.bass as bass
from concourse import mybir
from contextlib import ExitStack

F32 = mybir.dt.float32
I32 = mybir.dt.int32
BF16 = mybir.dt.bfloat16
F16 = mybir.dt.float16
ALU = mybir.AluOpType
ACT = mybir.ActivationFunctionType
AX = mybir.AxisListType.X

N, D, E, ED, L3L, REL = 3125, 64, 53125, 32, 5, 3
TP, TB = 125, 25
GE, EJ = 512, 4
G = -(-E // GE)
UN = 4
GP = G + UN
WIN = 64
NC = N + WIN
TAIL = E - (G - 1) * GE
SPAN_MAX = -(-N // WIN)
PAIRS = GP // 2
MID = N // 2
NEVER = 5000.0
PARTS = 3
FAR = 1.0e6
LN_EPS = BN_EPS = 1e-5

C_WE1, C_WE2, C_W1, C_W2, C_B2, C_G, C_B, C_BE2 = 0, 256, 384, 512, 576, 640, 704, 768
C_B1, C_BE1, C_RES, C_DOT, C_END = 1024, 1025, 1026, 1027, 1028
S_W, S_ROOT, S_END = 0, 64, 128


def chunks(total, step):
    return [(i, min(i + step, total)) for i in range(0, total, step)]


def gnn_kernel(nc, a, out):
    ctx = ExitStack()
    with ctx:
        def sb(name, shape, dt=F32):
            return ctx.enter_context(nc.sbuf_tensor(name, shape, dt))

        ctx.enter_context(nc.allow_non_contiguous_dma(reason="columns of biases, loaded once"))
        table = nc.dram_tensor("table", (2 * N, D), F32, kind="Internal").ap()
        eg_dram = nc.dram_tensor("eg_dram", (L3L, 128, C_END), F32, kind="Internal").ap()

        src_rows = nc.dram_tensor("src_rows", (PAIRS, 2 * 128), F16, kind="Internal").ap()
        sign_rows = nc.dram_tensor("sign_rows", (PAIRS, 2 * 128), F16, kind="Internal").ap()

        sign_all = nc.dram_tensor("sign_all", (G, 2, 128), F16, kind="Internal").ap()

        first = sb("first", [G, 2])
        last = sb("last", [G, 1])
        dstrel = sb("dstrel", [128, GP, EJ])
        spline_w = sb("spline_w", [128, GP, EJ, 2])
        rel_w = sb("rel_w", [128, GP, EJ, REL])
        w_c = sb("w_c", [128, 2, EJ, 2])
        sign_w = sb("sign_w", [128, GP, EJ, 2])
        deg_w = sb("deg_w", [128, GP, EJ, 3])
        src_i = sb("src_i", [128, GP, EJ], I32)
        srcsign_i = sb("srcsign_i", [128, GP, EJ], I32)
        first_row = sb("first_row", [1, GP])
        span_row = sb("span_row", [1, G])
        span = sb("span", [1, 2], I32)
        win_row = sb("win_row", [1, GP], I32)
        win_f = sb("win_f", [1, GP])
        iota_i = sb("iota_i", [128, WIN], I32)
        iota0 = sb("iota0", [128, WIN])
        iota = sb("iota", [128, WIN])
        idx = sb("idx", [128, UN, EJ], I32)
        gath = sb("gath", [128, UN, EJ, D])
        onehot = sb("onehot", [128, 2, EJ, WIN])
        msg_w = sb("msg_w", [128, 2, EJ, REL * D + 3])
        msg = sb("msg", [128, 2, EJ, D])
        attr_in = sb("attr_in", [128, UN, EJ * ED])
        attr_t = sb("attr_t", [128, G + 2, 128])
        hid_e = sb("hid_e", [128, 2, 2 * 128])

        x = sb("x", [TP, TB, D])
        h = sb("h", [TP, TB, D])
        y = sb("y", [TP, TB, D])
        wide = sb("wide", [TP, TB, 2 * D])
        hid_t = sb("hid_t", [128, TB * 128])
        def laid(t, at):
            return t[:, at:at + GP * EJ].rearrange("p (g j) -> p g j", j=EJ)
        src_f = laid(onehot[:, :, :, :].rearrange("p a j w -> p (a j w)"), 0)
        type_f = laid(gath[:, :, :, :].rearrange("p s j c -> p (s j c)"), 0)
        weight = laid(gath[:, :, :, :].rearrange("p s j c -> p (s j c)"), 512)
        raw_i = msg_w[0:G].rearrange("p a j c -> p (a j c)")[:, 0:3 * GE].bitcast(I32).rearrange("p (k i) -> p k i", i=GE)
        raw_f = hid_t[0:G, 0:5 * GE].rearrange("p (k i) -> p k i", i=GE)
        h_t = sb("h_t", [D + 1, TB, TP])
        acc01 = sb("acc01", [2 * D, NC])
        acc2_all = sb("acc2", [128, NC])
        acc2 = acc2_all[0:D + 3, :]
        deg = sb("deg", [TP, TB, 3])
        ndinv = sb("ndinv", [TP, TB])
        mean = sb("mean", [TP, TB])
        nbias = sb("nbias", [TP, TB])
        var = sb("var", [TP, TB])
        scratch = wide[:, :, :].rearrange("p b c -> p (b c)")
        rz = scratch[:, 0:32 * D].rearrange("p (q b c) -> p q b c", q=2, c=2 * D)
        cand = scratch[:, 32 * D:48 * D].rearrange("p (q b c) -> p q b c", q=2, c=D)
        mix = gath[0:TP].rearrange("p s j c -> p (s j c)").rearrange("p (q b c) -> p q b c", q=2, c=D)
        stats = sb("stats", [TP, TB, 6])
        parts_n = TB * PARTS * D
        parts = [sb("parts", [TP, TB, PARTS * D], BF16)[:, :, :],
                 acc2_all[0:TP, 0:parts_n // 2].bitcast(BF16).rearrange("p (b c) -> p b c", b=TB)]
        src_hot = [t.bitcast(BF16).rearrange("p (b c) -> p b c", b=TB) for t in (scratch[:, :], hid_t[0:TP, :])]
        src_bc = sb("src_bc", [128, 2, 2 * 128], F16)
        node_i = sb("node_i", [TP, TB], I32)
        node_no = sb("node_no", [TP, TB, 128], F16)
        rows16 = sb("rows16", [G, 3, 128], F16)
        sign16 = sb("sign16", [G, 128])
        bn6 = sb("bn6", [D, 7, 6])
        bn2 = sb("bn2", [D, 2])
        bnsc = sb("bnsc", [D, 4])

        ident = sb("ident", [128, 128])
        epsc = sb("epsc", [128, 1])
        wrel = sb("wrel", [D, REL, D])
        wrel_t = sb("wrel_t", [D, REL * D])
        m01 = sb("m01", [2 * D, 3 * D])
        m2 = sb("m2", [D, 3 * D])
        b_in = sb("b_in", [TP, D])
        nat = attr_in[:, :, :].rearrange("p s c -> p (s c)")
        gru_nat = nat[0:D, 0:6 * D].rearrange("p (m g e) -> p m g e", m=2, g=3)
        w_ih = sb("w_ih", [D + 1, 3, D])
        w_hh = sb("w_hh", [D + 1, 3, D])
        gb = sb("gb", [D, 2])
        w1_nat = nat[:, 6 * D:8 * D].rearrange("p (k e) -> p k e", k=2)
        w1pn = sb("w1pn", [2 * D, 2, 2 * D])
        w2_nat = msg[0:D, 0].rearrange("p j c -> p (j c)").rearrange("p (k e) -> p k e", k=2)
        w2pn = sb("w2pn", [2 * D, 2, D])
        b1pn = sb("b1pn", [TP, 2, 2 * D])
        b2pn = sb("b2pn", [TP, 2, D])
        spl_all = sb("spl_all", [128, 2, S_END])
        spl = sb("spl", [128, S_END])
        eg_all = attr_t[:, :, :].rearrange("p g c -> p (g c)")[:, 0:L3L * C_END].rearrange("p (l c) -> p l c", c=C_END)
        eg = acc2_all[:, 0:C_END]

        ps = ctx.enter_context(nc.psum_tensor("ps", [128, 8, 512], F32))
        sems = []

        def sem(name):
            s = ctx.enter_context(nc.semaphore(name))
            sems.append(s)
            return s

        cleared, loads, loads2 = sem("cleared"), sem("loads"), sem("loads2")
        dve_done, act_done, pe_step, ps_read, pool_done = (
            sem("dve_done"), sem("act_done"), sem("pe_step"), sem("ps_read"), sem("pool_done"))
        norm_ready, windows_set, msgw_ready = sem("norm_ready"), sem("windows_set"), sem("msgw_ready")
        targets_local, weights_turned, bn_ready = sem("targets_local"), sem("weights_turned"), sem("bn_ready")
        rows16_ready = sem("rows16_ready")
        last_weighed = sem("last_weighed")
        tables_ready, part_ready = sem("tables_ready"), sem("part_ready")
        stored, h_ready, var_ready, std_ready = sem("stored"), sem("h_ready"), sem("var_ready"), sem("std_ready")
        swh_sum, swh_ready, deg_turned, deg_read = (
            sem("swh_sum"), sem("swh_ready"), sem("deg_turned"), sem("deg_read"))
        gates_done, rz_ready, pre_ready, cand_ready, hnew_ready, hnew_turned, ht_ready = (
            sem("gates_done"), sem("rz_ready"), sem("pre_ready"), sem("cand_ready"),
            sem("hnew_ready"), sem("hnew_turned"), sem("ht_ready"))
        idx_ready = [sem(f"idx_ready{s}") for s in range(UN)]
        gathered = [sem(f"gathered{s}") for s in range(UN)]
        attr_loaded = [sem(f"attr_loaded{s}") for s in range(UN)]
        idx_seen, onehot_built, onehot_ready, summed, acc_added = (
            sem("idx_seen"), sem("onehot_built"), sem("onehot_ready"), sem("summed"), sem("acc_added"))
        attr_turned, attr_kept, attr_seen = sem("attr_turned"), sem("attr_kept"), sem("attr_seen")
        hid_biased = sem("hid_biased")
        hid_sum, hid_ready, gate_done, msg_ready = (
            sem("hid_sum"), sem("hid_ready"), sem("gate_done"), sem("msg_ready"))
        out_done = sem("out_done")
        src_loaded = [sem(f"src_loaded{q}") for q in range(2)]
        hot_ready, rows_gathered, rows_summed, gate_biased = (
            sem("hot_ready"), sem("rows_gathered"), sem("rows_summed"), sem("gate_biased"))

        def rejoin():
            nc.multi_engine_barrier(list(mybir.ALL_ENGINES),
                                    sems_to_clear=range(sems[0].num, sems[-1].num + 1))

        def linked(eng, done):
            count = [0]

            def link(ins):
                count[0] += 1
                ins.then_inc(done, 1)
                eng.wait_ge(done, count[0])
            return link

        def by_tile(t):
            return t.rearrange("c (p b) -> c b p", b=TB)

        def row_bc(ap2, width):
            return ap2.unsqueeze(2).to_broadcast([ap2.shape[0], ap2.shape[1], width])

        def const_bc(ap1):
            return ap1.unsqueeze(1).to_broadcast([ap1.shape[0], TB, ap1.shape[1]])

        def bcast_rows(ap1, parts):
            return ap1.unsqueeze(0).to_broadcast([parts, ap1.shape[0]])

        N_CLEAR = 10
        with nc.Block() as block:
            @block.gpsimd
            def _(pool):
                nc.gpsimd.memset(raw_i[:], 0).then_inc(cleared, 1)
                nc.gpsimd.memset(raw_f[:], 0.0).then_inc(cleared, 1)
                nc.gpsimd.memset(eg_all[:], 0.0).then_inc(cleared, 1)
                nc.gpsimd.memset(spl_all[:], 0.0).then_inc(cleared, 1)
                nc.gpsimd.memset(ident[:], 0.0).then_inc(pool_done, 1)
                nc.gpsimd.iota(iota_i[:], pattern=[[1, WIN]], base=0, channel_multiplier=0).then_inc(pool_done, 1)
                nc.gpsimd.iota(node_i[:], pattern=[[1, TB]], base=-MID, channel_multiplier=TB).then_inc(pool_done, 1)
                nc.gpsimd.memset(attr_t[:, G:G + 2, :], 0.0).then_inc(pool_done, 1)
                pool.wait_ge(pool_done, 1)
                nc.gpsimd.affine_select(out=ident[:], in_=ident[:], compare_op=ALU.not_equal, fill=1.0,
                                        base=0, pattern=[[-1, 128]], channel_multiplier=1).then_inc(pool_done, 1)
                nc.gpsimd.memset(acc01[:], 0.0).then_inc(pool_done, 1)
                nc.gpsimd.memset(acc2[:], 0.0).then_inc(pool_done, 1)
                pool.wait_ge(pool_done, 7)

            @block.vector
            def _(v):
                for t in (dstrel, src_f, type_f, weight, h_t, y, spline_w, first_row, w1pn):
                    nc.vector.memset(t[:], 0.0).then_inc(dve_done, 1)
                nc.vector.memset(epsc[:], LN_EPS).then_inc(dve_done, 1)
                v.wait_ge(dve_done, 10)
                nc.vector.memset(h_t[D:D + 1, :, :], 1.0).then_inc(dve_done, 1)
                v.wait_ge(pool_done, 5)
                nc.vector.tensor_copy(iota0[:], iota_i[:]).then_inc(dve_done, 1)
                nc.vector.tensor_copy(node_no[:], row_bc(node_i[:], 128)).then_inc(dve_done, 1)
                nc.vector.memset(src_bc[:], 0.0).then_inc(dve_done, 1)
                v.wait_ge(dve_done, 14)

            @block.sync
            def _(sp):
                sp.wait_ge(cleared, 2)
                n = 0
                full, tail = (G - 1) * GE, TAIL
                for k, name in enumerate(("src", "dst", "edge_type_3")):
                    v = a[name]
                    sp.dma_start(raw_i[0:G - 1, k, :], v[0:full].rearrange("(g i) -> g i", i=GE)).then_inc(loads, 16)
                    sp.dma_start(raw_i[G - 1:G, k, 0:tail], v[full:E].unsqueeze(0)).then_inc(loads, 16)
                    n += 2
                sp.dma_start(raw_i[G - 1:G, 1, tail:GE], a["dst"][E - (GE - tail):E].unsqueeze(0)).then_inc(loads, 16)
                n += 1
                for k, v in ((3, a["edge_weight"]), (4, a["edge_weight1"].rearrange("e o -> (e o)"))):
                    sp.dma_start(raw_f[0:G - 1, k, :], v[0:full].rearrange("(g i) -> g i", i=GE)).then_inc(loads, 16)
                    sp.dma_start(raw_f[G - 1:G, k, 0:tail], v[full:E].unsqueeze(0)).then_inc(loads, 16)
                    n += 2
                sp.dma_start(x[:], a["x"].rearrange("(p b) c -> p b c", b=TB)).then_inc(loads, 16)
                sp.dma_start(wrel[:], a["L0_gnn_weight"].rearrange("r d e -> d r e")).then_inc(loads, 16)
                sp.dma_start(gru_nat[:, 0], a["L0_gnn_w_ih"].rearrange("(g d) e -> d g e", g=3)).then_inc(loads, 16)
                sp.dma_start(gru_nat[:, 1], a["L0_gnn_w_hh"].rearrange("(g d) e -> d g e", g=3)).then_inc(loads, 16)
                bi, bh = a["L0_gnn_b_ih"].unsqueeze(0), a["L0_gnn_b_hh"].unsqueeze(0)
                w_ih_row = w_ih[D:D + 1].rearrange("p g e -> p (g e)")
                sp.dma_start(w_ih_row[:, 0:D], bi[:, 2 * D:3 * D]).then_inc(loads, 16)
                sp.dma_start(w_ih_row[:, D:3 * D], bi[:, 0:2 * D]).then_inc(loads, 16)
                sp.dma_start(w_hh[D:D + 1].rearrange("p g e -> p (g e)"), bh).then_inc(loads, 16)
                sp.dma_start(b_in[:], bcast_rows(a["L0_gnn_b_ih"][2 * D:3 * D], TP)).then_inc(loads, 16)
                sp.dma_start(gb[:, 0:1], a["L0_gnn_gamma"].unsqueeze(1)).then_inc(loads, 16)
                sp.dma_start(gb[:, 1:2], a["L0_gnn_beta"].unsqueeze(1)).then_inc(loads, 16)
                n += 10
                for k, s in enumerate("pn"):
                    sp.dma_start(w1_nat[:, k], a[f"L1_gnn_W1{s}"]).then_inc(loads, 16)
                    sp.dma_start(w2_nat[:, k], a[f"L1_gnn_W2{s}"]).then_inc(loads, 16)
                    sp.dma_start(b1pn[:, k], bcast_rows(a[f"L1_gnn_b1{s}"], TP)).then_inc(loads, 16)
                    sp.dma_start(b2pn[:, k], bcast_rows(a[f"L1_gnn_b2{s}"], TP)).then_inc(loads, 16)
                    n += 4
                sp.wait_ge(loads, 16 * n)

            @block.scalar
            def _(act):
                act.wait_ge(cleared, 4)
                n = 0
                for l in (0, 1):
                    sp_w = a[f"L2_gnn_w{l + 1}"]
                    act.dma_start(spl_all[:, l, S_W:S_W + D], sp_w.rearrange("k d e -> (k d) e")).then_inc(loads2, 16)
                    act.dma_start(spl_all[0:D, l, S_ROOT:S_ROOT + D], a[f"L2_gnn_root{l + 1}"]).then_inc(loads2, 16)
                    act.dma_start(spl_all[D:D + 1, l, S_ROOT:S_ROOT + D],
                                  a[f"L2_gnn_b{l + 1}"].unsqueeze(0)).then_inc(loads2, 16)
                    n += 3
                for j in range(EJ):
                    o = C_WE1 + j * D
                    act.dma_start(eg_all[ED * j:ED * j + ED, :, o:o + D],
                                  a["L3_gnn_We1"].rearrange("l k d -> k l d")).then_inc(loads2, 16)
                    n += 1
                for j in range(2):
                    o = C_WE2 + j * D
                    act.dma_start(eg_all[D * j:D * j + D, :, o:o + D],
                                  a["L3_gnn_We2"].rearrange("l k d -> k l d")).then_inc(loads2, 16)
                    act.dma_start(eg_all[D * j:D * j + D, :, C_BE1:C_BE1 + 1],
                                  a["L3_gnn_be1"].rearrange("l k -> k l").unsqueeze(2)).then_inc(loads2, 16)
                    n += 2
                act.dma_start(eg_all[0:D, :, C_W1:C_W1 + 2 * D],
                              a["L3_gnn_W1"].rearrange("l k d -> k l d")).then_inc(loads2, 16)
                act.dma_start(eg_all[:, :, C_W2:C_W2 + D],
                              a["L3_gnn_W2"].rearrange("l k d -> k l d")).then_inc(loads2, 16)
                act.dma_start(eg_all[:, :, C_B1:C_B1 + 1],
                              a["L3_gnn_b1"].rearrange("l k -> k l").unsqueeze(2)).then_inc(loads2, 16)
                n += 3
                for c, name in ((C_B2, "b2"), (C_G, "ln_g"), (C_B, "ln_b")):
                    v = a[f"L3_gnn_{name}"]
                    act.dma_start(eg_all[:, :, c:c + D],
                                  v.unsqueeze(0).to_broadcast([128, L3L, D])).then_inc(loads2, 16)
                    n += 1
                for j in range(EJ):
                    o = C_BE2 + j * D
                    act.dma_start(eg_all[:, :, o:o + D],
                                  a["L3_gnn_be2"].unsqueeze(0).to_broadcast([128, L3L, D])).then_inc(loads2, 16)
                    n += 1
                for c, name in ((C_RES, "res_w"), (C_DOT, "dot_scale")):
                    v = a[f"L3_gnn_{name}"]
                    act.dma_start(eg_all[:, :, c:c + 1],
                                  v.unsqueeze(0).unsqueeze(2).to_broadcast([128, L3L, 1])).then_inc(loads2, 16)
                    n += 1
                act.wait_ge(loads2, 16 * n)
                act.dma_start(eg_dram.rearrange("l p c -> p l c"), eg_all[:, :, :]).then_inc(stored, 16)
                act.wait_ge(stored, 16)
        rejoin()

        HALF = 13

        def node_stats(v, link, src):
            for b in range(TB):
                s = nc.vector.bn_stats(stats[:, b, :], src[:, b, :])
            link(s)
            gap = nbias
            link(nc.vector.tensor_tensor(gap[:], stats[:, :, 1], stats[:, :, 4], op=ALU.subtract))
            link(nc.vector.tensor_tensor(gap[:], gap[:], gap[:], op=ALU.mult))
            link(nc.vector.tensor_tensor(var[:], stats[:, :, 2], stats[:, :, 5], op=ALU.add))
            link(nc.vector.tensor_scalar(var[:], var[:], 1.0 / D, None, ALU.mult))
            nc.vector.scalar_tensor_tensor(var[:], gap[:], 0.25, var[:], ALU.mult, ALU.add).then_inc(var_ready, 1)
            link(nc.vector.tensor_tensor(mean[:], stats[:, :, 1], stats[:, :, 4], op=ALU.add))
            link(nc.vector.tensor_scalar(mean[:], mean[:], 0.5, None, ALU.mult))
            v.wait_ge(std_ready, 1)
            link(nc.vector.reciprocal(var[:], var[:]))
            nc.vector.scalar_tensor_tensor(nbias[:], mean[:], -1.0, var[:], ALU.mult, ALU.mult).then_inc(norm_ready, 1)

        def norm_tiles_dve(v, link, src, dst):
            for b in range(HALF):
                s = nc.vector.tensor_scalar(dst[:, b, :], src[:, b, :], mean[:, b:b + 1], var[:, b:b + 1],
                                            ALU.subtract, ALU.mult)
            link(s)

        def norm_tiles_act(act, src, dst, func, done):
            act.wait_ge(var_ready, 1)
            nc.scalar.activation(var[:], var[:], ACT.Sqrt, bias=epsc[0:TP, :]).then_inc(std_ready, 1)
            act.wait_ge(norm_ready, 1)
            for b in range(HALF, TB):
                s = nc.scalar.activation(dst[:, b, :], src[:, b, :], func, bias=nbias[:, b:b + 1],
                                         scale=var[:, b:b + 1])
            s.then_inc(done, 1)

        def layer_norm_relu(v, link, src, dst, done):
            node_stats(v, link, src)
            norm_tiles_dve(v, link, src, dst)
            link(nc.vector.tensor_scalar(dst[:, 0:HALF, :], dst[:, 0:HALF, :], 0.0, None, ALU.max))
            v.sem_inc(done, 1)

        def make_parts(v, link, rows, left, out_parts):
            for k in range(PARTS):
                part = out_parts[..., k * D:(k + 1) * D]
                link(nc.vector.tensor_copy(part, rows if k == 0 else left))
                if k < PARTS - 1:
                    link(nc.vector.tensor_tensor(left, rows if k == 0 else left, part, op=ALU.subtract))

        def parts_of_h(v, link, b0, b1):
            left = hid_t[0:TP, :].rearrange("p (b k c) -> p b k c", b=TB, k=2)[:, b0:b1, 0, :]
            make_parts(v, link, h[:, b0:b1, :], left, parts[0][:, b0:b1, :])

        def first_windows(v):
            nc.vector.tensor_copy(iota[:], iota0[:]).then_inc(windows_set, 1)
            nc.vector.tensor_copy(win_f[:], first_row[:]).then_inc(windows_set, 1)
            nc.vector.tensor_copy(win_row[:], first_row[:]).then_inc(windows_set, 1)

        table_h = table[0:N, :].rearrange("(p b) c -> p b c", b=TB)
        table_n = table[N:2 * N, :].rearrange("(p b) c -> p b c", b=TB)

        def flat(ap):
            return ap.rearrange("p a b -> p (a b)")

        def node_cols(ap, b):
            return ap[:, b:b + TB * (TP - 1) + 1:TB]

        with nc.Block() as block:
            @block.vector
            def _(v):
                link = linked(v, dve_done)
                link(nc.vector.tensor_copy(flat(raw_f[:, 0:3, :]), flat(raw_i)))
                link(nc.vector.tensor_reduce(first[:, 0:1], raw_f[:, 1, :], AX, ALU.min))
                link(nc.vector.tensor_reduce(last[:], raw_f[:, 1, :], AX, ALU.max))
                link(nc.vector.tensor_tensor(first[:, 1:2], last[:], first[:, 0:1], op=ALU.subtract))
                nc.vector.tensor_scalar(raw_f[:, 1, :], raw_f[:, 1, :], first[:, 0:1], None,
                                        ALU.subtract).then_inc(targets_local, 1)
                for k, dst in ((0, src_f), (1, dstrel), (2, type_f), (3, weight)):
                    v.wait_ge(pe_step, k + 1)
                    nc.vector.tensor_copy(dst[:, 0:G, :],
                                          ps[:, k, 0:EJ * G].rearrange("p (j g) -> p g j", j=EJ)).then_inc(ps_read, 1)
                v.wait_ge(pe_step, 5)
                nc.vector.tensor_copy(spline_w[:, 0:G, :, 1],
                                      ps[:, 4, 0:EJ * G].rearrange("p (j g) -> p g j", j=EJ)).then_inc(ps_read, 1)
                v.wait_ge(pe_step, 6)
                nc.vector.tensor_copy(first_row[:, 0:G], ps[0:1, 5, 0:G]).then_inc(ps_read, 1)
                nc.vector.tensor_copy(span_row[:], ps[0:1, 5, 128:128 + G]).then_inc(ps_read, 1)
                v.wait_ge(ps_read, 7)
                nc.vector.tensor_scalar(spline_w[:, :, :, 0], spline_w[:, :, :, 1], -1.0, 1.0, ALU.mult, ALU.add)
                for r in range(REL):
                    nc.vector.scalar_tensor_tensor(rel_w[:, :, :, r], type_f[:], float(r), weight[:],
                                                   ALU.is_equal, ALU.mult)
                for t in (sign_w, deg_w):
                    nc.vector.tensor_scalar(t[:, :, :, 0], weight[:], 0.0, None, ALU.max)
                    nc.vector.tensor_scalar(t[:, :, :, 1], weight[:], -1.0, 0.0, ALU.mult, ALU.max)
                nc.vector.memset(deg_w[:, :, :, 2], 1.0)
                link(nc.vector.tensor_copy(src_i[:], src_f[:]))
                link(nc.vector.tensor_scalar(type_f[:], weight[:], 0.0, float(N), ALU.is_lt, ALU.mult))
                link(nc.vector.tensor_tensor(srcsign_i[:], type_f[:], src_f[:], op=ALU.add))
                link(nc.vector.tensor_reduce(span_row[:, 0:1], span_row[:], AX, ALU.max))
                link(nc.vector.tensor_copy(span[:, 0:1], span_row[:, 0:1]))
                link(nc.vector.tensor_scalar(span[:, 0:1], span[:, 0:1], WIN.bit_length() - 1, None,
                                             ALU.logical_shift_right))
                link(nc.vector.tensor_scalar(span[:, 0:1], span[:, 0:1], 1.0, None, ALU.add))
                w3 = raw_f[:, 3, :].rearrange("g (p j) -> g j p", j=EJ)[:, EJ - 1, :]
                s3 = raw_f[:, 0, :].rearrange("g (p j) -> g j p", j=EJ)[:, EJ - 1, :]
                link(nc.vector.tensor_scalar(rows16[:, 0, :], s3, float(-MID), None, ALU.add))
                for k, op in ((1, ALU.is_lt), (2, ALU.is_ge)):
                    link(nc.vector.tensor_scalar(sign16[:], w3, 0.0, NEVER, op, ALU.mult))
                    link(nc.vector.tensor_tensor(rows16[:, k, :], sign16[:], rows16[:, 0, :], op=ALU.add))
                v.sem_inc(rows16_ready, 1)
                layer_norm_relu(v, link, x, h, h_ready)
                first_windows(v)
                parts_of_h(v, link, 0, HALF)
                link(nc.vector.tensor_tensor(b1pn[:, 0], b1pn[:, 0], b1pn[:, 1], op=ALU.subtract))
                link(nc.vector.tensor_tensor(b2pn[:, 0], b2pn[:, 0], b2pn[:, 1], op=ALU.subtract))
                v.wait_ge(act_done, 3)
                link(nc.vector.tensor_tensor(w_hh[D:D + 1, 0:2, :], w_hh[D:D + 1, 0:2, :], w_ih[D:D + 1, 1:3, :],
                                             op=ALU.add))
                v.wait_ge(h_ready, 2)
                parts_of_h(v, link, HALF, TB)

            @block.gpsimd
            def _(pool):
                pool.wait_ge(targets_local, 1)
                nc.gpsimd.affine_select(out=raw_f[:, 1, :], in_=raw_f[:, 1, :], compare_op=ALU.is_ge, fill=FAR,
                                        base=E - 1, pattern=[[-1, GE]], channel_multiplier=-GE).then_inc(pool_done, 1)
                pool.wait_ge(pool_done, 1)

            @block.tensor
            def _(pe):
                for m in (0, 1):
                    for g in range(3):
                        t = nc.tensor.transpose(ps[0:D, 6, (3 * m + g) * D:(3 * m + g + 1) * D],
                                                gru_nat[:, m, g, :], ident[0:D, 0:D])
                t.then_inc(weights_turned, 1)
                for k in range(2):
                    nc.tensor.transpose(ps[0:D, 7, k * 128:(k + 1) * 128], w1_nat[:, k, :], ident[:, :])
                for k in range(2):
                    t = nc.tensor.transpose(ps[:, 7, 256 + k * D:256 + (k + 1) * D], w2_nat[:, k, :], ident[0:D, 0:D])
                t.then_inc(weights_turned, 1)
                pe.wait_ge(targets_local, 1)
                for k in range(5):
                    if k == 1:
                        pe.wait_ge(pool_done, 1)
                    for j in range(EJ):
                        t = nc.tensor.transpose(ps[:, k, j * G:(j + 1) * G],
                                                raw_f[:, k, :].rearrange("g (p j) -> g j p", j=EJ)[:, j, :],
                                                ident[0:G, 0:G])
                    t.then_inc(pe_step, 1)
                for k in range(2):
                    t = nc.tensor.transpose(ps[0:1, 5, k * 128:k * 128 + G], first[:, k:k + 1], ident[0:G, 0:G])
                t.then_inc(pe_step, 1)
                pe.wait_ge(act_done, 5)
                for r in range(REL):
                    t = nc.tensor.transpose(ps[0:D, 6, r * D:(r + 1) * D], wrel[:, r, :], ident[0:D, 0:D])
                t.then_inc(weights_turned, 1)
                pe.wait_ge(act_done, 6)
                w_ih_k = w_ih[0:D].rearrange("p g e -> p (g e)")
                nc.tensor.matmul(ps[:, 7, 0:3 * D], wrel_t[:, 0:2 * D], w_ih_k, start=True, stop=True)
                nc.tensor.matmul(ps[0:D, 7, 256:256 + 3 * D], wrel_t[:, 2 * D:3 * D], w_ih_k,
                                 start=True, stop=True).then_inc(weights_turned, 1)

            @block.scalar
            def _(act):
                act.wait_ge(weights_turned, 1)
                g_ih = ps[0:D, 6, 0:3 * D].rearrange("p (g e) -> p g e", g=3)
                nc.scalar.copy(w_ih[0:D, 0, :], g_ih[:, 2, :]).then_inc(act_done, 1)
                nc.scalar.copy(w_ih[0:D, 1:3, :], g_ih[:, 0:2, :]).then_inc(act_done, 1)
                nc.scalar.copy(w_hh[0:D, :, :], ps[0:D, 6, 3 * D:6 * D].rearrange("p (g e) -> p g e", g=3)).then_inc(act_done, 1)
                act.wait_ge(weights_turned, 2)
                for k in range(2):
                    c = nc.scalar.copy(w1pn[k * D:(k + 1) * D, k, :], ps[0:D, 7, k * 128:(k + 1) * 128])
                c.then_inc(act_done, 1)
                nc.scalar.copy(w2pn[:], ps[:, 7, 256:256 + 2 * D].rearrange("p (k e) -> p k e", k=2)).then_inc(act_done, 1)
                act.wait_ge(weights_turned, 3)
                nc.scalar.copy(wrel_t[:], ps[0:D, 6, 0:REL * D]).then_inc(act_done, 1)
                act.wait_ge(weights_turned, 4)
                nc.scalar.copy(m01[:], ps[:, 7, 0:3 * D]).then_inc(act_done, 1)
                nc.scalar.copy(m2[:], ps[0:D, 7, 256:256 + 3 * D]).then_inc(act_done, 1)
                norm_tiles_act(act, x, h, ACT.Relu, h_ready)
                act.wait_ge(act_done, 8)

            @block.sync
            def _(sp):
                sp.wait_ge(rows16_ready, 1)
                for pair, k, at in ((src_rows, 0, None), (sign_rows, 1, 0), (sign_rows, 2, 1)):
                    rows = pair[0:G // 2, :].rearrange("m (e p) -> m e p", e=2)
                    if at is None:
                        sp.dma_start(rows.rearrange("m e p -> (m e) p"), rows16[:, k, :]).then_inc(stored, 16)
                    else:
                        sp.dma_start(sign_all[:, at, :], rows16[:, k, :]).then_inc(stored, 16)
                sp.wait_ge(stored, 48)
                sp.dma_start(sign_rows[0:G // 2, :].rearrange("m (k p) -> m k p", k=2),
                             sign_all.rearrange("(m e) k p -> m e k p", e=2)[:, 1]).then_inc(loads, 16)
                sp.dma_start(src_rows[G // 2:PAIRS, :], src_rows[0:PAIRS - G // 2, :]).then_inc(loads, 16)
                sp.wait_ge(loads, 32)
                sp.dma_start(sign_rows[G // 2:PAIRS, :], sign_rows[0:PAIRS - G // 2, :]).then_inc(loads, 16)
                sp.wait_ge(h_ready, 2)
                sp.dma_start(table_h, h[:]).then_inc(stored, 16)
                sp.wait_ge(loads, 48)
                sp.wait_ge(stored, 64)
        rejoin()

        SPAN = nc.values_load(span[0:1, 0:1], min_val=1, max_val=SPAN_MAX)

        def next_windows(v):
            nc.vector.tensor_scalar(iota[:], iota[:], float(WIN), None, ALU.add).then_inc(windows_set, 1)
            nc.vector.tensor_scalar(win_f[:], win_f[:], float(WIN), float(N), ALU.add, ALU.min).then_inc(windows_set, 1)
            v.wait_ge(windows_set, 2)
            nc.vector.tensor_copy(win_row[:], win_f[:]).then_inc(windows_set, 1)
            v.wait_ge(windows_set, 3)

        def on_pe(s, both):
            return both or s % 2 == 1

        def gather_rows(pool, rows, both):
            with pool.Fori(0, G // UN) as i:
                for s in range(UN):
                    pool.wait_ge(idx_ready[s], i + 1)
                    pool.sem_inc(idx_seen, 1)
                    for j in range(EJ - on_pe(s, both)):
                        nc.gpsimd.indirect_dma_start(
                            out=gath[:, s, j, :], out_offset=None, in_=table[0:rows, :],
                            in_offset=bass.IndirectOffsetOnAxis(ap=idx[:, s, j:j + 1], axis=0),
                        ).then_inc(gathered[s], 16)
            for s in range(UN):
                pool.wait_ge(gathered[s], 16 * (EJ - on_pe(s, both)) * (G // UN))
            pool.dma_reset(range(gathered[0].num, gathered[-1].num + 1))

        def rows_here(eng, i, s, both):
            per_turn = 16 * (EJ - on_pe(s, both))
            eng.wait_ge(gathered[s], i * per_turn + per_turn)
            if both:
                eng.wait_ge(rows_summed, i * UN + s + 1)
            elif on_pe(s, both):
                eng.wait_ge(rows_summed, i * 2 + s // 2 + 1)

        def load_sources(sp, pairs, m, q):
            row = pairs[bass.ds(m, 1), :].to_broadcast([128, 2 * 128])
            sp.dma_start(src_bc[:, q, :], row).then_inc(src_loaded[q], 16)

        def hot_half(q, half, both, signed):
            e0 = 0 if both or signed else 1
            b0, b1 = (0, 13) if half == 0 else (13, TB)
            shape = [TP, b1 - b0, 2 - e0, 128]
            columns = src_bc[0:TP, q, 128 * e0:256].rearrange("p (e c) -> p e c", e=2 - e0)
            return nc.vector.tensor_tensor(
                src_hot[q][:, b0:b1, 128 * e0:256].rearrange("p b (e c) -> p b e c", e=2 - e0),
                columns.unsqueeze(1).to_broadcast(shape),
                node_no[:, b0:b1, :].unsqueeze(2).to_broadcast(shape), op=ALU.is_equal)

        def gather_pe(q, odd, signed, bank):
            terms = [(k, b) for k in range(1 + signed) for b in range(TB)]
            for n, (k, b) in enumerate(terms):
                c0 = k * 128 if signed else odd * 128
                m = nc.tensor.matmul(ps[:, bank, 0:PARTS * D], src_hot[q][:, b, c0:c0 + 128], parts[k][:, b, :],
                                     start=(n == 0), stop=(n == len(terms) - 1))
            m.then_inc(rows_gathered, 1)

        def sum_parts(slot, bank):
            return nc.vector.tensor_reduce(gath[:, slot, EJ - 1, :],
                                           ps[:, bank, 0:PARTS * D].rearrange("p (k c) -> p c k", k=PARTS),
                                           AX, ALU.add)

        def step_hot_dve(v, i, s, both, signed):
            if s % 2 == 0:
                v.wait_ge(src_loaded[s // 2], i * 16 + 32)
                hot_half(s // 2, 0, both, signed)
            else:
                hot_half(s // 2, 1, both, signed).then_inc(hot_ready, 1)

        def step_gather_pe(pe, i, s, both, signed):
            if on_pe(s, both):
                pe.wait_ge(hot_ready, i * 2 + s // 2 + 2)
                pe.wait_ge(rows_summed, i * UN + s + 1 if both else i * 2 + s // 2 + 1)
                gather_pe((s // 2 + 1) % 2, s % 2, signed, 6 + s % 2)

        def step_sum_dve(v, i, s, both):
            if on_pe(s, both):
                v.wait_ge(rows_gathered, i * UN + s + 3 if both else i * 2 + s // 2 + 2)
                sum_parts((s + 2) % UN, 6 + s % 2).then_inc(rows_summed, 1)

        def first_hot_dve(v, both, signed):
            for q in range(2):
                v.wait_ge(src_loaded[q], 16)
                hot_half(q, 0, both, signed)
                hot_half(q, 1, both, signed).then_inc(hot_ready, 1)
            for g in range(2):
                if on_pe(g, both):
                    v.wait_ge(rows_gathered, g + 1 if both else 1)
                    sum_parts(g, 6 + g).then_inc(rows_summed, 1)

        def first_gather_pe(pe, both, signed):
            pe.wait_ge(hot_ready, 1)
            for g in range(2):
                if on_pe(g, both):
                    gather_pe(0, g, signed, 6 + g)

        def group(ap, g):
            return ap[:, bass.ds(g, 1), :].rearrange("p a j -> p (a j)")

        def build_onehot(g, slot):
            return nc.vector.tensor_tensor(
                onehot[:, slot], iota[:].unsqueeze(1).to_broadcast([128, EJ, WIN]),
                group(dstrel, g).unsqueeze(2).to_broadcast([128, EJ, WIN]), op=ALU.is_equal)

        def copy_index(index, g, slot):
            return nc.vector.tensor_scalar(idx[:, slot, :], group(index, g), 0.0, None, ALU.add)

        def weighted_pass(index, weights, R, first_layer, both):
            signed = index is srcsign_i
            rows, pairs = (2 * N, sign_rows) if signed else (N, src_rows)
            built = 3 if first_layer else 2
            adds = 2 if first_layer else 1

            with nc.Block(no_gpsimd_drain=True) as block:
                @block.gpsimd
                def _(pool):
                    gather_rows(pool, rows, both)

                @block.vector
                def _(v):
                    def prepare(g, slot):
                        build_onehot(g, slot).then_inc(onehot_ready, 1)
                        nc.vector.tensor_copy(w_c[:, slot],
                                              weights[:, bass.ds(g, 1), :, 0:2].rearrange("p a j r -> p (a j) r")
                                              ).then_inc(onehot_ready, 1)
                        if first_layer:
                            nc.vector.tensor_copy(msg_w[:, slot, :, REL * D:REL * D + 3],
                                                  deg_w[:, bass.ds(g, 1), :, :].rearrange("p a j r -> p (a j) r")
                                                  ).then_inc(onehot_ready, 1)

                    def weigh_last(g, slot):
                        w = weights[:, bass.ds(g, 1), :, R - 1].rearrange("p a j -> p (a j)")
                        nc.vector.tensor_tensor(msg_w[:, slot % 2, :, 2 * D:3 * D], gath[:, slot],
                                                w.unsqueeze(2).to_broadcast([128, EJ, D]),
                                                op=ALU.mult).then_inc(last_weighed, 1)

                    for s in range(UN):
                        copy_index(index, s, s).then_inc(idx_ready[s], 1)
                    prepare(0, 0)
                    first_hot_dve(v, both, signed)
                    with v.Fori(0, G // UN) as i:
                        for s in range(UN):
                            g = i * UN + s
                            if first_layer:
                                rows_here(v, i, s, both)
                                weigh_last(g, s)
                            prepare(g + 1, (s + 1) % 2)
                            step_hot_dve(v, i, s, both, signed)
                            col = v.value_load(win_row[0:1, bass.ds(g, 1)], min_val=0, max_val=N)
                            v.wait_ge(summed, g + 1)
                            nc.vector.tensor_tensor(acc01[:, bass.ds(col, WIN)], acc01[:, bass.ds(col, WIN)],
                                                    ps[:, s % 2, 0:WIN], op=ALU.add).then_inc(acc_added, 1)
                            if first_layer:
                                nc.vector.tensor_tensor(acc2[:, bass.ds(col, WIN)], acc2[:, bass.ds(col, WIN)],
                                                        ps[0:D + 3, s % 2, WIN:2 * WIN], op=ALU.add).then_inc(acc_added, 1)
                            copy_index(index, g + UN, s).then_inc(idx_ready[s], 1)
                            step_sum_dve(v, i, s, both)
                            v.wait_ge(acc_added, adds * g + adds)
                    next_windows(v)

                @block.scalar
                def _(act):
                    if first_layer:
                        act.sem_inc(attr_kept, 2)
                    with act.Fori(0, G // UN) as i:
                        for s in range(UN):
                            g = i * UN + s
                            rows_here(act, i, s, both)
                            act.wait_ge(onehot_ready, built * g + built)
                            for j in range(EJ):
                                for r in range(2):
                                    m = nc.scalar.activation(msg_w[:, s % 2, j, r * D:(r + 1) * D], gath[:, s, j, :],
                                                             ACT.Copy, scale=w_c[:, s % 2, j, r:r + 1])
                            m.then_inc(msgw_ready, 1)
                            if first_layer:
                                act.wait_ge(attr_turned, g + 1)
                                act.sem_inc(attr_seen, 1)
                                nc.scalar.copy(attr_t[:, bass.ds(g, 1), :].rearrange("p a c -> p (a c)"),
                                               ps[:, 2 + s % 2, 0:128]).then_inc(attr_kept, 1)

                @block.tensor
                def _(pe):
                    first_gather_pe(pe, both, signed)
                    with pe.Fori(0, G // UN) as i:
                        for s in range(UN):
                            g = i * UN + s
                            step_gather_pe(pe, i, s, both, signed)
                            if first_layer:
                                pe.wait_ge(attr_loaded[s], i * 16 + 16)
                                pe.wait_ge(attr_kept, g + 1)
                                nc.tensor.transpose(ps[:, 2 + s % 2, 0:128], attr_in[:, s, :],
                                                    ident[:, :]).then_inc(attr_turned, 1)
                            pe.wait_ge(onehot_ready, built * g + built)
                            pe.wait_ge(msgw_ready, g + 1)
                            if first_layer:
                                pe.wait_ge(last_weighed, g + 1)
                            for j in range(EJ):
                                m = nc.tensor.matmul(ps[:, s % 2, 0:WIN], msg_w[:, s % 2, j, 0:2 * D],
                                                     onehot[:, s % 2, j, :], start=(j == 0), stop=(j == EJ - 1))
                            if first_layer:
                                for j in range(EJ):
                                    m = nc.tensor.matmul(ps[0:D + 3, s % 2, WIN:2 * WIN],
                                                         msg_w[:, s % 2, j, 2 * D:3 * D + 3],
                                                         onehot[:, s % 2, j, :], start=(j == 0), stop=(j == EJ - 1))
                            m.then_inc(summed, 1)

                @block.sync
                def _(sp):
                    for q in range(2):
                        load_sources(sp, pairs, q, q)
                    if not first_layer:
                        source_loop(sp, pairs)
                        return
                    attr = a["edge_attr_32"]

                    def load(g, s, parts=128):
                        rows = attr[bass.ds(g * GE, parts * EJ), :]
                        sp.dma_start(attr_in[0:parts, s, :],
                                     rows.rearrange("(p j) k -> p (j k)", j=EJ)).then_inc(attr_loaded[s], 16)
                    for s in range(UN):
                        load(s, s)

                    def sources_before(i, s):
                        if s == 1:
                            next_sources(sp, pairs, i, 1)
                        if s == 3:
                            next_sources(sp, pairs, i + 1, 0)
                    next_sources(sp, pairs, 0, 0)
                    with sp.Fori(0, G // UN - 2) as i:
                        for s in range(UN):
                            sources_before(i, s)
                            sp.wait_ge(attr_turned, i * UN + s + 1)
                            load(i * UN + s + UN, s)
                    for s in range(UN - 1):
                        sources_before(G // UN - 2, s)
                        sp.wait_ge(attr_turned, G - 2 * UN + s + 1)
                        load(G - UN + s, s)
                    sources_before(G // UN - 2, UN - 1)
                    sp.wait_ge(attr_turned, G - UN)
                    whole, rest = TAIL // EJ, TAIL % EJ
                    if rest:
                        e0 = E - rest
                        sp.dma_start(attr_in[whole:whole + 1, UN - 1, 0:rest * ED],
                                     attr[e0:E, :].rearrange("j k -> (j k)").unsqueeze(0)).then_inc(loads, 16)
                        sp.wait_ge(loads, 16)
                    load(G - 1, UN - 1, parts=whole)
                    next_sources(sp, pairs, G // UN - 1, 1)
                    for q in range(2):
                        sp.wait_ge(src_loaded[q], 16 * (G // UN + 1))
            rejoin()

        def next_sources(sp, pairs, i, q):
            sp.wait_ge(hot_ready, i * 2 + q + 1)
            load_sources(sp, pairs, i * 2 + q + 2, q)

        def source_loop(sp, pairs):
            with sp.Fori(0, G // UN) as i:
                for q in range(2):
                    next_sources(sp, pairs, i, q)
            for q in range(2):
                sp.wait_ge(src_loaded[q], 16 * (G // UN + 1))

        def weighted_round(index, weights, R, first_layer=False, both=False):
            with nc.Fori(0, SPAN):
                weighted_pass(index, weights, R, first_layer, both)

        C4 = chunks(TB, 4)
        C8 = chunks(TB, 8)

        def tiles4(bank, b0, b1, parts=D):
            return ps[0:parts, bank, 0:(b1 - b0) * TP].rearrange("p (b n) -> p b n", n=TP)

        CG = [(0, 8), (8, 15), (15, 21), (21, TB)]
        with nc.Fori(0, 2):
            weighted_round(src_i, rel_w, REL, first_layer=True)
            with nc.Block() as block:
                @block.tensor
                def _(pe):
                    def gates(q):
                        b0, b1 = CG[q]
                        for b in range(b0, b1):
                            t = ps[0:TP, 4 * (q % 2) + (b - b0) // 2,
                                   256 * ((b - b0) % 2):256 * ((b - b0) % 2) + 256]
                            nc.tensor.matmul(t[:, 0:3 * D], node_cols(acc01, b), m01[:], start=True, stop=False)
                            nc.tensor.matmul(t[:, 0:3 * D], node_cols(acc2[0:D], b), m2[:], start=False, stop=False)
                            nc.tensor.matmul(t[:, D:3 * D], h_t[:, b, :], w_hh[:, 0:2, :].rearrange("p g e -> p (g e)"),
                                             start=False, stop=True)
                            m = nc.tensor.matmul(t[:, 3 * D:4 * D], h_t[:, b, :], w_hh[:, 2, :], start=True, stop=True)
                        m.then_inc(gates_done, 1)

                    def turn(q):
                        pe.wait_ge(hnew_ready, q + 1)
                        b0, b1 = CG[q]
                        for c in range(-(-(b1 - b0) // 4)):
                            for b in range(b0 + 4 * c, min(b1, b0 + 4 * c + 4)):
                                o = (b - b0 - 4 * c) * TP
                                m = nc.tensor.transpose(ps[0:D, 4 * (q % 2) + c, o:o + TP], h[:, b, :],
                                                        ident[0:TP, 0:TP])
                            m.then_inc(hnew_turned, 1)

                    for b in range(TB):
                        m = nc.tensor.transpose(ps[0:TP, 7, 3 * b:3 * b + 3], node_cols(acc2[D:D + 3], b),
                                                ident[D:D + 3, D:D + 3])
                    m.then_inc(deg_turned, 1)
                    for q in range(len(CG)):
                        if q == 1:
                            pe.wait_ge(deg_read, 1)
                        if q >= 2:
                            pe.wait_ge(ht_ready, 2 * q - 2)
                        gates(q)
                        if q >= 1:
                            turn(q - 1)
                    turn(len(CG) - 1)

                def gate_bank(q):
                    n = CG[q][1] - CG[q][0]
                    return ps[0:TP, 4 * (q % 2):4 * (q % 2) + 4, :].rearrange("p k (t c) -> p (k t) c", t=2)[:, 0:n, :]

                @block.scalar
                def _(act):
                    def keep(q):
                        b0, b1 = CG[q]
                        for c in range(-(-(b1 - b0) // 4)):
                            act.wait_ge(hnew_turned, 2 * q + c + 1)
                            t0, t1 = b0 + 4 * c, min(b1, b0 + 4 * c + 4)
                            nc.scalar.copy(h_t[0:D, t0:t1, :], tiles4(4 * (q % 2) + c, t0, t1)).then_inc(ht_ready, 1)

                    for q, (b0, b1) in enumerate(CG):
                        act.wait_ge(gates_done, q + 1)
                        nc.scalar.activation(rz[:, q % 2, 0:b1 - b0, :], gate_bank(q)[:, :, D:3 * D],
                                             ACT.Sigmoid).then_inc(rz_ready, 1)
                        act.wait_ge(pre_ready, q + 1)
                        nc.scalar.activation(cand[:, q % 2, 0:b1 - b0, :], cand[:, q % 2, 0:b1 - b0, :],
                                             ACT.Tanh).then_inc(cand_ready, 1)
                        if q >= 1:
                            keep(q - 1)
                    keep(len(CG) - 1)

                @block.vector
                def _(v):
                    link = linked(v, dve_done)
                    first_windows(v)
                    v.wait_ge(deg_turned, 1)
                    nc.vector.tensor_copy(deg[:], ps[0:TP, 7, 0:3 * TB].rearrange("p (b k) -> p b k", k=3)).then_inc(deg_read, 1)
                    for q, (b0, b1) in enumerate(CG):
                        n = b1 - b0
                        t = gate_bank(q)
                        r_, z_ = rz[:, q % 2, 0:n, 0:D], rz[:, q % 2, 0:n, D:2 * D]
                        cn, mx = cand[:, q % 2, 0:n, :], mix[:, q % 2, 0:n, :]
                        v.wait_ge(rz_ready, q + 1)
                        link(nc.vector.tensor_tensor(cn, r_, t[:, :, 3 * D:4 * D], op=ALU.mult))
                        link(nc.vector.tensor_tensor(cn, cn, t[:, :, 0:D], op=ALU.add))
                        nc.vector.tensor_tensor(cn, cn, b_in[:].unsqueeze(1).to_broadcast([TP, n, D]),
                                                op=ALU.add).then_inc(pre_ready, 1)
                        v.wait_ge(cand_ready, q + 1)
                        link(nc.vector.tensor_tensor(mx, y[:, b0:b1, :], cn, op=ALU.subtract))
                        link(nc.vector.tensor_tensor(mx, mx, z_, op=ALU.mult))
                        nc.vector.tensor_tensor(h[:, b0:b1, :], cn, mx, op=ALU.add).then_inc(hnew_ready, 1)
                        v.wait_ge(hnew_ready, q + 1)
                        link(nc.vector.tensor_copy(y[:, b0:b1, :], h[:, b0:b1, :]))
                        parts_of_h(v, link, b0, b1)

                @block.sync
                def _(sp):
                    sp.wait_ge(hnew_ready, len(CG))
                    sp.dma_start(table_h, h[:]).then_inc(stored, 16)
                    sp.wait_ge(stored, 16)

                @block.gpsimd
                def _(pool):
                    pool.wait_ge(gates_done, len(CG))
                    nc.gpsimd.memset(acc01[:], 0.0).then_inc(pool_done, 1)
                    nc.gpsimd.memset(acc2[:], 0.0).then_inc(pool_done, 1)
                    pool.wait_ge(pool_done, 2)
            rejoin()

        def start_sums_pe(pe):
            for c, (b0, b1) in enumerate(C4):
                if c >= 2:
                    pe.wait_ge(ps_read, c - 1)
                for b in range(b0, b1):
                    t = nc.tensor.transpose(ps[:, 4 + c % 2, (b - b0) * TP:(b - b0 + 1) * TP], wide[:, b, :],
                                            ident[0:TP, 0:TP])
                t.then_inc(pe_step, 1)

        def signed_parts(v, link):
            for k in range(2):
                make_parts(v, link, wide[:, :, k * D:(k + 1) * D],
                           hid_t[0:TP, :].rearrange("p (b k c) -> p b k c", b=TB, k=2)[:, :, k, :], parts[k])

        def start_sums_act(act):
            for c, (b0, b1) in enumerate(C4):
                act.wait_ge(pe_step, c + 1)
                nc.scalar.copy(by_tile(acc01[:, 0:N])[:, b0:b1, :], tiles4(4 + c % 2, b0, b1, 128)).then_inc(ps_read, 1)

        with nc.Block() as block:
            @block.vector
            def _(v):
                link = linked(v, dve_done)
                h_flat = flat(h_t[0:D])
                for c, (n0, n1) in enumerate(chunks(N, 512)):
                    s = nc.vector.bn_stats(bn6[:, c, :], h_flat[:, n0:n1])
                link(s)
                nc.vector.bn_aggr(bn2[:], bn6[:].rearrange("p c k -> p (c k)")).then_inc(bn_ready, 1)
                link(nc.vector.tensor_scalar(deg[:, :, 0:2], deg[:, :, 0:2], 1.0, None, ALU.add))
                nc.vector.tensor_scalar(deg[:, :, 2:3], deg[:, :, 2:3], 1.0, None, ALU.max).then_inc(deg_turned, 1)
                v.wait_ge(bn_ready, 2)
                link(nc.vector.reciprocal(bnsc[:, 0:1], bnsc[:, 2:3]))
                link(nc.vector.tensor_tensor(bnsc[:, 0:1], bnsc[:, 0:1], gb[:, 0:1], op=ALU.mult))
                link(nc.vector.scalar_tensor_tensor(bnsc[:, 1:2], bn2[:, 0:1], -1.0, bnsc[:, 0:1], ALU.mult, ALU.mult))
                nc.vector.tensor_tensor(bnsc[:, 1:2], bnsc[:, 1:2], gb[:, 1:2], op=ALU.add).then_inc(bn_ready, 1)
                v.wait_ge(deg_turned, 2)
                link(nc.vector.reciprocal(deg[:], deg[:]))
                link(nc.vector.tensor_scalar(ndinv[:], deg[:, :, 1], -1.0, None, ALU.mult))
                for c, (b0, b1) in enumerate(C8):
                    v.wait_ge(swh_sum, c + 1)
                    nc.vector.tensor_tensor(x[:, b0:b1, :], x[:, b0:b1, :],
                                            ps[0:TP, 2 + c % 2, 0:(b1 - b0) * D].rearrange("p (b c) -> p b c", c=D),
                                            op=ALU.add).then_inc(deg_read, 1)
                v.wait_ge(deg_read, len(C8))
                layer_norm_relu(v, link, x, h, h_ready)
                v.wait_ge(h_ready, 2)
                for k in range(2):
                    nc.vector.tensor_tensor(wide[:, :, k * D:(k + 1) * D], h[:], row_bc(deg[:, :, k], D),
                                            op=ALU.mult).then_inc(tables_ready, 1)
                v.wait_ge(tables_ready, 2)
                signed_parts(v, link)
                first_windows(v)

            @block.scalar
            def _(act):
                act.wait_ge(bn_ready, 1)
                nc.scalar.activation(bnsc[:, 2:3], bn2[:, 1:2], ACT.Sqrt, bias=epsc[0:D, :]).then_inc(bn_ready, 1)
                act.wait_ge(deg_turned, 1)
                nc.scalar.activation(deg[:, :, 0:2], deg[:, :, 0:2], ACT.Sqrt).then_inc(deg_turned, 1)
                act.wait_ge(bn_ready, 3)
                for c, (b0, b1) in enumerate(C8):
                    nc.scalar.activation(hid_t[0:D, b0 * TP:b1 * TP], flat(h_t[0:D, b0:b1, :]), ACT.Identity,
                                         bias=bnsc[:, 1:2], scale=bnsc[:, 0:1]).then_inc(swh_ready, 1)
                norm_tiles_act(act, x, h, ACT.Relu, h_ready)
                start_sums_act(act)

            @block.tensor
            def _(pe):
                for c, (b0, b1) in enumerate(C8):
                    pe.wait_ge(swh_ready, c + 1)
                    if c >= 2:
                        pe.wait_ge(deg_read, c - 1)
                    for b in range(b0, b1):
                        t = nc.tensor.transpose(ps[0:TP, 2 + c % 2, (b - b0) * D:(b - b0 + 1) * D],
                                                hid_t[0:D, b * TP:(b + 1) * TP], ident[0:D, 0:D])
                    t.then_inc(swh_sum, 1)
                pe.wait_ge(tables_ready, 2)
                start_sums_pe(pe)

            @block.sync
            def _(sp):
                sp.wait_ge(tables_ready, 1)
                sp.dma_start(table_h, wide[:, :, 0:D]).then_inc(stored, 16)
                sp.wait_ge(tables_ready, 2)
                sp.dma_start(table_n, wide[:, :, D:2 * D]).then_inc(stored, 16)
                sp.wait_ge(stored, 32)
        rejoin()

        weighted_round(srcsign_i, sign_w, 2)

        C2 = chunks(TB, 2)
        with nc.Block() as block:
            @block.tensor
            def _(pe):
                def second(c):
                    b0, b1 = C4[c]
                    pe.wait_ge(h_ready, c + 1)
                    if c >= 2:
                        pe.wait_ge(ht_ready, c - 1)
                    for b in range(b0, b1):
                        m = nc.tensor.transpose(ps[:, 2 + c % 2, (b - b0) * TP:(b - b0 + 1) * TP], wide[:, b, :],
                                                ident[0:TP, 0:TP])
                    m.then_inc(hnew_turned, 1)

                def third(c):
                    b0, b1 = C4[c]
                    pe.wait_ge(ht_ready, c + 1)
                    if c >= 2:
                        pe.wait_ge(deg_read, c - 1)
                    for b in range(b0, b1):
                        m = nc.tensor.matmul(ps[0:TP, 6 + c % 2, (b - b0) * 128:(b - b0 + 1) * 128],
                                             hid_t[:, b * TP:(b + 1) * TP], flat(w2pn[:]), start=True, stop=True)
                    m.then_inc(gates_done, 1)

                for c, (b0, b1) in enumerate(C2):
                    if c >= 2:
                        pe.wait_ge(swh_ready, c - 1)
                    for b in range(b0, b1):
                        m = nc.tensor.matmul(ps[0:TP, c % 2, (b - b0) * 256:(b - b0 + 1) * 256],
                                             node_cols(acc01, b), flat(w1pn[:]), start=True, stop=True)
                    m.then_inc(swh_sum, 1)
                    if c >= 3 and c % 2 == 1:
                        second(c // 2 - 1)
                        if c >= 5:
                            third(c // 2 - 2)
                second(len(C4) - 2)
                third(len(C4) - 3)
                second(len(C4) - 1)
                third(len(C4) - 2)
                third(len(C4) - 1)
                pe.wait_ge(deg_read, len(C4))
                start_sums_pe(pe)

            @block.scalar
            def _(act):
                for c, (b0, b1) in enumerate(C4):
                    act.wait_ge(hnew_turned, c + 1)
                    nc.scalar.copy(hid_t[:, b0 * TP:b1 * TP], ps[:, 2 + c % 2, 0:(b1 - b0) * TP]).then_inc(ht_ready, 1)
                start_sums_act(act)

            @block.vector
            def _(v):
                def first_out(c):
                    b0, b1 = C2[c]
                    v.wait_ge(swh_sum, c + 1)
                    for b in range(b0, b1):
                        o = (b - b0) * 256
                        m = nc.vector.scalar_tensor_tensor(wide[:, b, :], ps[0:TP, c % 2, o:o + 128], deg[:, b, 0:1],
                                                           b1pn[:, 0], ALU.mult, ALU.add)
                    m.then_inc(part_ready, 1)
                    v.wait_ge(part_ready, c + 1)
                    for b in range(b0, b1):
                        o = (b - b0) * 256 + 128
                        m = nc.vector.scalar_tensor_tensor(wide[:, b, :], ps[0:TP, c % 2, o:o + 128], ndinv[:, b:b + 1],
                                                           wide[:, b, :], ALU.mult, ALU.add)
                    m.then_inc(swh_ready, 1)

                def next_tables(c):
                    b0, b1 = C4[c]
                    v.wait_ge(gates_done, c + 1)
                    nc.vector.tensor_tensor(
                        wide[:, b0:b1, :].rearrange("p b (k e) -> p b k e", k=2),
                        ps[0:TP, 6 + c % 2, 0:(b1 - b0) * 128].rearrange("p (b k e) -> p b k e", k=2, e=D),
                        deg[:, b0:b1, 0:2].unsqueeze(3).to_broadcast([TP, b1 - b0, 2, D]),
                        op=ALU.mult).then_inc(deg_read, 1)

                for c, (b0, b1) in enumerate(C4):
                    first_out(2 * c)
                    if 2 * c + 1 < len(C2):
                        first_out(2 * c + 1)
                    v.wait_ge(swh_ready, min(2 * c + 2, len(C2)))
                    nc.vector.tensor_scalar(wide[:, b0:b1, :], wide[:, b0:b1, :], 0.0, None, ALU.max).then_inc(h_ready, 1)
                    if c >= 3:
                        next_tables(c - 3)
                for c in range(len(C4) - 3, len(C4)):
                    next_tables(c)
                v.wait_ge(deg_read, len(C4))
                signed_parts(v, linked(v, dve_done))
                first_windows(v)

            @block.sync
            def _(sp):
                sp.wait_ge(deg_read, len(C4))
                sp.dma_start(table_h, wide[:, :, 0:D]).then_inc(stored, 16)
                sp.dma_start(table_n, wide[:, :, D:2 * D]).then_inc(stored, 16)
                sp.wait_ge(stored, 32)
        rejoin()

        weighted_round(srcsign_i, sign_w, 2)

        def turn_nodes(pe, src, c):
            b0, b1 = C4[c]
            if c >= 2:
                pe.wait_ge(ht_ready, c - 1)
            for b in range(b0, b1):
                m = nc.tensor.transpose(ps[0:D, 6 + c % 2, (b - b0) * TP:(b - b0 + 1) * TP], src[:, b, :],
                                        ident[0:TP, 0:TP])
            m.then_inc(hnew_turned, 1)

        def keep_nodes(act, c):
            b0, b1 = C4[c]
            act.wait_ge(hnew_turned, c + 1)
            nc.scalar.copy(h_t[0:D, b0:b1, :], tiles4(6 + c % 2, b0, b1)).then_inc(ht_ready, 1)

        with nc.Block() as block:
            @block.tensor
            def _(pe):
                for c, (b0, b1) in enumerate(C4):
                    if c >= 2:
                        pe.wait_ge(swh_ready, c - 1)
                    for b in range(b0, b1):
                        m = nc.tensor.transpose(ps[0:TP, c % 2, (b - b0) * 128:(b - b0 + 1) * 128],
                                                node_cols(acc01, b), ident[:, :])
                    m.then_inc(swh_sum, 1)
                pe.wait_ge(h_ready, 2)
                for c in range(len(C4)):
                    turn_nodes(pe, h, c)

            @block.vector
            def _(v):
                link = linked(v, dve_done)
                for c, (b0, b1) in enumerate(C4):
                    v.wait_ge(swh_sum, c + 1)
                    nc.vector.tensor_tensor(
                        wide[:, b0:b1, :].rearrange("p b (k e) -> p b k e", k=2),
                        ps[0:TP, c % 2, 0:(b1 - b0) * 128].rearrange("p (b k e) -> p b k e", k=2, e=D),
                        deg[:, b0:b1, 0:2].unsqueeze(3).to_broadcast([TP, b1 - b0, 2, D]),
                        op=ALU.mult).then_inc(swh_ready, 1)
                v.wait_ge(swh_ready, len(C4))
                link(nc.vector.tensor_tensor(h[:], wide[:, :, 0:D], wide[:, :, D:2 * D], op=ALU.subtract))
                link(nc.vector.tensor_tensor(h[:], h[:], const_bc(b2pn[:, 0]), op=ALU.add))
                link(nc.vector.scalar_tensor_tensor(flat(x[:]), flat(h[:]), 0.0, flat(x[:]), ALU.max, ALU.add))
                layer_norm_relu(v, link, x, h, h_ready)
                first_windows(v)
                parts_of_h(v, link, 0, HALF)
                v.wait_ge(h_ready, 2)
                parts_of_h(v, link, HALF, TB)

            @block.scalar
            def _(act):
                norm_tiles_act(act, x, h, ACT.Relu, h_ready)
                for c in range(len(C4)):
                    keep_nodes(act, c)

            @block.gpsimd
            def _(pool):
                pool.wait_ge(swh_sum, len(C4))
                nc.gpsimd.memset(acc01[:], 0.0).then_inc(pool_done, 1)
                pool.wait_ge(pool_done, 1)

            @block.sync
            def _(sp):
                sp.wait_ge(h_ready, 2)
                sp.dma_start(table_h, h[:]).then_inc(stored, 16)
                sp.wait_ge(stored, 16)
        rejoin()

        with nc.Fori(0, 2) as l:
            weighted_round(src_i, spline_w, 2, both=True)
            with nc.Block() as block:
                @block.tensor
                def _(pe):
                    pe.wait_ge(cleared, 1)
                    for c, (b0, b1) in enumerate(C4):
                        if c >= 2:
                            pe.wait_ge(swh_ready, c - 1)
                        for b in range(b0, b1):
                            o = 2 * (b - b0) * D
                            nc.tensor.matmul(ps[0:TP, c % 2, o:o + D], node_cols(acc01, b), spl[:, S_W:S_W + D],
                                             start=True, stop=True)
                            m = nc.tensor.matmul(ps[0:TP, c % 2, o + D:o + 2 * D], h_t[:, b, :],
                                                 spl[0:D + 1, S_ROOT:S_ROOT + D], start=True, stop=True)
                        m.then_inc(swh_sum, 1)
                        if c >= 1:
                            pe.wait_ge(swh_ready, c)
                            turn_nodes(pe, h, c - 1)
                    pe.wait_ge(swh_ready, len(C4))
                    turn_nodes(pe, h, len(C4) - 1)

                @block.vector
                def _(v):
                    link = linked(v, dve_done)
                    first_windows(v)
                    nc.vector.tensor_copy(spl[:], spl_all[:, bass.ds(l, 1), :].rearrange("p a c -> p (a c)")).then_inc(cleared, 1)
                    for c, (b0, b1) in enumerate(C4):
                        v.wait_ge(swh_sum, c + 1)
                        t = ps[0:TP, c % 2, 0:(b1 - b0) * 128].rearrange("p (b k e) -> p b k e", k=2, e=D)
                        nc.vector.tensor_tensor(wide[:, b0:b1, 0:D], t[:, :, 0, :], row_bc(deg[:, b0:b1, 2], D),
                                                op=ALU.mult).then_inc(part_ready, 1)
                        v.wait_ge(part_ready, c + 1)
                        nc.vector.tensor_tensor(h[:, b0:b1, :], wide[:, b0:b1, 0:D], t[:, :, 1, :],
                                                op=ALU.add).then_inc(swh_ready, 1)
                        v.wait_ge(swh_ready, c + 1)
                        parts_of_h(v, link, b0, b1)

                @block.scalar
                def _(act):
                    for c in range(len(C4)):
                        keep_nodes(act, c)

                @block.gpsimd
                def _(pool):
                    pool.wait_ge(swh_sum, len(C4))
                    nc.gpsimd.memset(acc01[:], 0.0).then_inc(pool_done, 1)
                    pool.wait_ge(pool_done, 1)

                @block.sync
                def _(sp):
                    sp.wait_ge(swh_ready, len(C4))
                    sp.dma_start(table_h, h[:]).then_inc(stored, 16)
                    sp.wait_ge(stored, 16)
            rejoin()

        with nc.Block() as block:
            @block.vector
            def _(v):
                link = linked(v, dve_done)
                link(nc.vector.tensor_tensor(x[:], x[:], h[:], op=ALU.add))
                layer_norm_relu(v, link, x, y, h_ready)

            @block.scalar
            def _(act):
                norm_tiles_act(act, x, y, ACT.Relu, h_ready)
        rejoin()

        with nc.Fori(0, L3L) as l:
            with nc.Block() as block:
                @block.tensor
                def _(pe):
                    def first_product(c):
                        b0, b1 = C4[c]
                        pe.wait_ge(ht_ready, c + 1)
                        if c == 0:
                            pe.wait_ge(loads, 16)
                        if c >= 2:
                            pe.wait_ge(rz_ready, c - 1)
                        nc.tensor.matmul(ps[:, c % 2, 0:(b1 - b0) * TP], eg[0:D, C_W1:C_W1 + 2 * D],
                                         flat(h_t[0:D, b0:b1, :]), start=True, stop=True).then_inc(swh_sum, 1)

                    def second_product(c):
                        b0, b1 = C4[c]
                        pe.wait_ge(cand_ready, c + 1)
                        if c >= 2:
                            pe.wait_ge(swh_ready, c - 1)
                        for b in range(b0, b1):
                            m = nc.tensor.matmul(ps[0:TP, 2 + c % 2, (b - b0) * D:(b - b0 + 1) * D],
                                                 hid_t[:, b * TP:(b + 1) * TP], eg[:, C_W2:C_W2 + D],
                                                 start=True, stop=True)
                        m.then_inc(gates_done, 1)

                    turn_nodes(pe, y, 0)
                    for c in range(len(C4)):
                        if c + 1 < len(C4):
                            turn_nodes(pe, y, c + 1)
                        first_product(c)
                        if c >= 1:
                            second_product(c - 1)
                    second_product(len(C4) - 1)

                @block.scalar
                def _(act):
                    keep_nodes(act, 0)
                    for c, (b0, b1) in enumerate(C4):
                        if c + 1 < len(C4):
                            keep_nodes(act, c + 1)
                        act.wait_ge(swh_sum, c + 1)
                        nc.scalar.activation(hid_t[:, b0 * TP:b1 * TP], ps[:, c % 2, 0:(b1 - b0) * TP], ACT.Identity,
                                             bias=eg[:, C_B1:C_B1 + 1]).then_inc(rz_ready, 1)

                @block.vector
                def _(v):
                    def leaky(c):
                        b0, b1 = C4[c]
                        v.wait_ge(rz_ready, c + 1)
                        t = hid_t[:, b0 * TP:b1 * TP]
                        nc.vector.scalar_tensor_tensor(t, t, 0.1, t, ALU.mult, ALU.max).then_inc(cand_ready, 1)

                    def table_rows(c):
                        b0, b1 = C4[c]
                        v.wait_ge(gates_done, c + 1)
                        nc.vector.tensor_tensor(
                            h[:, b0:b1, :], ps[0:TP, 2 + c % 2, 0:(b1 - b0) * D].rearrange("p (b e) -> p b e", e=D),
                            eg[0:TP, C_B2:C_B2 + D].unsqueeze(1).to_broadcast([TP, b1 - b0, D]),
                            op=ALU.add).then_inc(swh_ready, 1)

                    link = linked(v, dve_done)

                    def table_parts(c):
                        b0, b1 = C4[c]
                        v.wait_ge(swh_ready, c + 1)
                        make_parts(v, link, h[:, b0:b1, :], wide[:, b0:b1, 0:D], parts[0][:, b0:b1, :])

                    first_windows(v)
                    for c in range(len(C4)):
                        leaky(c)
                        if c >= 1:
                            table_rows(c - 1)
                            table_parts(c - 1)
                    table_rows(len(C4) - 1)
                    table_parts(len(C4) - 1)

                @block.gpsimd
                def _(pool):
                    nc.gpsimd.memset(acc01[0:D, :], 0.0).then_inc(pool_done, 1)
                    pool.wait_ge(pool_done, 1)

                @block.sync
                def _(sp):
                    sp.dma_start(eg[:], eg_dram[bass.ds(l, 1)].rearrange("a p c -> (a p) c")).then_inc(loads, 16)
                    sp.wait_ge(swh_ready, len(C4))
                    sp.dma_start(table_h, h[:]).then_inc(stored, 16)
                    sp.wait_ge(stored, 16)
            rejoin()
            with nc.Fori(0, SPAN):
                with nc.Block(no_gpsimd_drain=True) as block:
                    @block.gpsimd
                    def _(pool):
                        gather_rows(pool, N, False)

                    @block.sync
                    def _(sp):
                        for q in range(2):
                            load_sources(sp, src_rows, q, q)
                        source_loop(sp, src_rows)

                    @block.scalar
                    def _(act):
                        with act.Fori(0, (G + 2) // 2) as i:
                            for s in range(2):
                                act.wait_ge(hid_sum, i * 2 + s + 1)
                                nc.scalar.activation(hid_e[:, s, :], ps[:, 2 + s, 0:256], ACT.Identity,
                                                     bias=eg[:, C_BE1:C_BE1 + 1]).then_inc(hid_biased, 1)

                    @block.tensor
                    def _(pe):
                        def hidden(g, s):
                            for k in range(2):
                                m = nc.tensor.matmul(ps[:, 2 + s, 128 * k:128 * k + 128],
                                                     eg[:, C_WE1 + 128 * k:C_WE1 + 128 * k + 128],
                                                     attr_t[:, bass.ds(g, 1), :].rearrange("p a c -> p (a c)"),
                                                     start=True, stop=True)
                            m.then_inc(hid_sum, 1)

                        def gates(s):
                            for k in range(2):
                                m = nc.tensor.matmul(ps[:, 4 + s, 128 * k:128 * k + 128], hid_e[:, s, 128 * k:128 * k + 128],
                                                     eg[:, C_WE2:C_WE2 + 128], start=True, stop=True)
                            m.then_inc(gate_done, 1)

                        hidden(0, 0)
                        hidden(1, 1)
                        pe.wait_ge(hid_ready, 1)
                        gates(0)
                        first_gather_pe(pe, False, False)
                        with pe.Fori(0, G // UN) as i:
                            for s in range(UN):
                                g = i * UN + s
                                pe.wait_ge(hid_ready, g + 2)
                                gates((s + 1) % 2)
                                hidden(g + 2, s % 2)
                                pe.wait_ge(msg_ready, g + 1)
                                for j in range(EJ):
                                    m = nc.tensor.matmul(ps[0:D, s % 2, 0:WIN], msg[:, s % 2, j, :],
                                                         onehot[:, s % 2, j, :], start=(j == 0), stop=(j == EJ - 1))
                                m.then_inc(summed, 1)
                                step_gather_pe(pe, i, s, False, False)

                    @block.vector
                    def _(v):
                        def leak(g, s):
                            v.wait_ge(hid_biased, g + 1)
                            nc.vector.scalar_tensor_tensor(hid_e[:, s, :], hid_e[:, s, :], 0.1, hid_e[:, s, :],
                                                           ALU.mult, ALU.max).then_inc(hid_ready, 1)

                        for s in range(UN):
                            copy_index(src_i, s, s).then_inc(idx_ready[s], 1)
                        build_onehot(0, 0).then_inc(onehot_ready, 1)
                        v.wait_ge(onehot_ready, 1)
                        leak(0, 0)
                        leak(1, 1)
                        first_hot_dve(v, False, False)
                        with v.Fori(0, G // UN) as i:
                            for s in range(UN):
                                g = i * UN + s
                                m = msg[:, s % 2].rearrange("p j c -> p (j c)")
                                v.wait_ge(gate_done, g + 1)
                                nc.vector.tensor_tensor(m, eg[:, C_BE2:C_BE2 + 256], ps[:, 4 + s % 2, 0:256],
                                                        op=ALU.add).then_inc(gate_biased, 1)
                                v.wait_ge(gate_biased, g + 1)
                                rows_here(v, i, s, False)
                                nc.vector.tensor_tensor(m, gath[:, s].rearrange("p j c -> p (j c)"), m,
                                                        op=ALU.mult).then_inc(msg_ready, 1)
                                build_onehot(g + 1, (s + 1) % 2).then_inc(onehot_ready, 1)
                                step_hot_dve(v, i, s, False, False)
                                col = v.value_load(win_row[0:1, bass.ds(g, 1)], min_val=0, max_val=N)
                                v.wait_ge(summed, g + 1)
                                nc.vector.tensor_tensor(acc01[0:D, bass.ds(col, WIN)], acc01[0:D, bass.ds(col, WIN)],
                                                        ps[0:D, s % 2, 0:WIN], op=ALU.add).then_inc(acc_added, 1)
                                copy_index(src_i, g + UN, s).then_inc(idx_ready[s], 1)
                                step_sum_dve(v, i, s, False)
                                leak(g + 2, s % 2)
                                v.wait_ge(onehot_ready, g + 2)
                                v.wait_ge(acc_added, g + 1)
                        next_windows(v)
                rejoin()

            with nc.Block() as block:
                @block.tensor
                def _(pe):
                    for c, (b0, b1) in enumerate(C8):
                        if c >= 2:
                            pe.wait_ge(swh_ready, c - 1)
                        for b in range(b0, b1):
                            m = nc.tensor.transpose(ps[0:TP, c % 2, (b - b0) * D:(b - b0 + 1) * D],
                                                    node_cols(acc01[0:D], b), ident[0:D, 0:D])
                        m.then_inc(swh_sum, 1)

                @block.vector
                def _(v):
                    link = linked(v, dve_done)
                    link(nc.vector.tensor_tensor(eg[:, C_RES:C_RES + 1], eg[:, C_RES:C_RES + 1],
                                                 eg[:, C_DOT:C_DOT + 1], op=ALU.mult))
                    for c, (b0, b1) in enumerate(C8):
                        v.wait_ge(swh_sum, c + 1)
                        nc.vector.scalar_tensor_tensor(flat(y[:, b0:b1, :]), ps[0:TP, c % 2, 0:(b1 - b0) * D],
                                                       eg[0:TP, C_RES:C_RES + 1], flat(y[:, b0:b1, :]),
                                                       ALU.mult, ALU.add).then_inc(swh_ready, 1)
                    v.wait_ge(swh_ready, len(C8))
                    node_stats(v, link, y)
                    norm_tiles_dve(v, link, y, h)
                    v.wait_ge(h_ready, 1)
                    link(nc.vector.tensor_tensor(h[:], h[:], const_bc(eg[0:TP, C_G:C_G + D]), op=ALU.mult))
                    link(nc.vector.tensor_tensor(y[:], h[:], const_bc(eg[0:TP, C_B:C_B + D]), op=ALU.add))

                @block.scalar
                def _(act):
                    norm_tiles_act(act, y, h, ACT.Identity, h_ready)
            rejoin()

        with nc.Block() as block:
            @block.vector
            def _(v):
                nc.vector.tensor_tensor(x[:], x[:], y[:], op=ALU.add).then_inc(h_ready, 1)

            @block.sync
            def _(sp):
                sp.wait_ge(h_ready, 1)
                sp.dma_start(out.rearrange("(p b) c -> p b c", b=TB), x[:]).then_inc(out_done, 16)
                sp.wait_ge(out_done, 16)


def kernel(**inputs):
    import numpy as np
    import concourse.bacc as bacc
    from concourse.bass_utils import run_bass_kernel_spmd as run

    nc = bacc.Bacc("TRN2", target_bir_lowering=False, num_devices=1)
    arrays, args = {}, {}
    for name, value in inputs.items():
        arr = np.ascontiguousarray(value)
        arrays[f"in_{name}"] = arr
        args[name] = nc.dram_tensor(f"in_{name}", arr.shape, mybir.dt.from_np(arr.dtype), kind="ExternalInput").ap()
    out = nc.dram_tensor("out", (N, D), F32, kind="ExternalOutput").ap()
    gnn_kernel(nc, args, out)
    r = run(nc, [arrays], core_ids=[0])
    return r.results[0]["out"]
```

```python
import concourse.bass as bass
from concourse import mybir
from contextlib import ExitStack

F32 = mybir.dt.float32
I32 = mybir.dt.int32
BF16 = mybir.dt.bfloat16
F16 = mybir.dt.float16
ALU = mybir.AluOpType
ACT = mybir.ActivationFunctionType
AX = mybir.AxisListType.X

N, D, E, ED, L3L, REL = 3125, 64, 53125, 32, 5, 3
TP, TB = 125, 25
GE, EJ = 512, 4
G = -(-E // GE)
UN = 4
WIN = 64
NC = N + WIN
TAIL = E - (G - 1) * GE
SPAN_MAX = -(-N // WIN)
PAIRS = G // 2
MID = N // 2
NEVER = 5000.0
PARTS = 3
FAR = 1.0e6
LN_EPS = BN_EPS = 1e-5

C_WE1, C_WE2, C_W1, C_W2, C_B2, C_G, C_B, C_BE2 = 0, 256, 384, 512, 576, 640, 704, 768
C_B1, C_BE1, C_RES, C_DOT, C_END = 1024, 1025, 1026, 1027, 1028
S_W, S_ROOT, S_END = 0, 64, 128


def chunks(total, step):
    return [(i, min(i + step, total)) for i in range(0, total, step)]


def gnn_kernel(nc, a, out):
    ctx = ExitStack()
    with ctx:
        def sb(name, shape, dt=F32):
            return ctx.enter_context(nc.sbuf_tensor(name, shape, dt))

        ctx.enter_context(nc.allow_non_contiguous_dma(reason="columns of biases, loaded once"))
        table = nc.dram_tensor("table", (2 * N, D), F32, kind="Internal").ap()
        eg_dram = nc.dram_tensor("eg_dram", (L3L, 128, C_END), F32, kind="Internal").ap()

        src_rows = nc.dram_tensor("src_rows", (PAIRS, 2 * 128), F16, kind="Internal").ap()
        sign_rows = nc.dram_tensor("sign_rows", (PAIRS, 2 * 128), F16, kind="Internal").ap()

        sign_all = nc.dram_tensor("sign_all", (G, 2, 128), F16, kind="Internal").ap()

        first = sb("first", [G, 2])
        last = sb("last", [G, 1])
        dstrel = sb("dstrel", [128, G, EJ])
        spline_w = sb("spline_w", [128, G, EJ, 2])
        rel_w = sb("rel_w", [128, G, EJ, REL])
        w_c = sb("w_c", [128, 2, EJ, 2])
        sign_w = sb("sign_w", [128, G, EJ, 2])
        deg_w = sb("deg_w", [128, G, EJ, 3])
        src_i = sb("src_i", [128, G, EJ], I32)
        srcsign_i = sb("srcsign_i", [128, G, EJ], I32)
        first_row = sb("first_row", [1, G])
        span_row = sb("span_row", [1, G])
        span = sb("span", [1, 2], I32)
        win_row = sb("win_row", [1, G], I32)
        win_f = sb("win_f", [1, G])
        iota_i = sb("iota_i", [128, WIN], I32)
        iota0 = sb("iota0", [128, WIN])
        iota = sb("iota", [128, WIN])
        idx = sb("idx", [128, UN, EJ], I32)
        gath = sb("gath", [128, UN, EJ, D])
        onehot = sb("onehot", [128, 2, EJ, WIN])
        msg_w = sb("msg_w", [128, 2, EJ, REL * D + 3])
        msg = sb("msg", [128, 2, EJ, D])
        attr_in = sb("attr_in", [128, UN, EJ * ED])
        attr_t = sb("attr_t", [128, G, 128])
        hid_e = sb("hid_e", [128, 2, 2 * 128])

        x = sb("x", [TP, TB, D])
        h = sb("h", [TP, TB, D])
        y = sb("y", [TP, TB, D])
        wide = sb("wide", [TP, TB, 2 * D])
        hid_t = sb("hid_t", [128, TB * 128])
        def laid(t, at):
            return t[:, at:at + G * EJ].rearrange("p (g j) -> p g j", j=EJ)
        src_f = laid(onehot[:, :, :, :].rearrange("p a j w -> p (a j w)"), 0)
        type_f = laid(gath[:, :, :, :].rearrange("p s j c -> p (s j c)"), 0)
        weight = laid(gath[:, :, :, :].rearrange("p s j c -> p (s j c)"), 512)
        raw_i = msg_w[0:G].rearrange("p a j c -> p (a j c)")[:, 0:3 * GE].bitcast(I32).rearrange("p (k i) -> p k i", i=GE)
        raw_f = hid_t[0:G, 0:5 * GE].rearrange("p (k i) -> p k i", i=GE)
        h_t = sb("h_t", [D + 1, TB, TP])
        acc01 = sb("acc01", [2 * D, NC])
        acc2_all = sb("acc2", [128, NC])
        acc2 = acc2_all[0:D + 3, :]
        deg = sb("deg", [TP, TB, 3])
        ndinv = sb("ndinv", [TP, TB])
        mean = sb("mean", [TP, TB])
        nbias = sb("nbias", [TP, TB])
        var = sb("var", [TP, TB])
        scratch = wide[:, :, :].rearrange("p b c -> p (b c)")
        rz = scratch[:, 0:32 * D].rearrange("p (q b c) -> p q b c", q=2, c=2 * D)
        cand = scratch[:, 32 * D:48 * D].rearrange("p (q b c) -> p q b c", q=2, c=D)
        mix = gath[0:TP].rearrange("p s j c -> p (s j c)").rearrange("p (q b c) -> p q b c", q=2, c=D)
        stats = sb("stats", [TP, TB, 6])
        parts_n = TB * PARTS * D
        parts = [sb("parts", [TP, TB, PARTS * D], BF16)[:, :, :],
                 acc2_all[0:TP, 0:parts_n // 2].bitcast(BF16).rearrange("p (b c) -> p b c", b=TB)]
        src_hot = [t.bitcast(BF16).rearrange("p (b c) -> p b c", b=TB) for t in (scratch[:, :], hid_t[0:TP, :])]
        src_bc = sb("src_bc", [128, 2, 2 * 128], F16)
        node_i = sb("node_i", [TP, TB], I32)
        node_no = sb("node_no", [TP, TB, 128], F16)
        rows16 = sb("rows16", [G, 3, 128], F16)
        sign16 = sb("sign16", [G, 128])
        bn6 = sb("bn6", [D, 7, 6])
        bn2 = sb("bn2", [D, 2])
        bnsc = sb("bnsc", [D, 4])

        ident = sb("ident", [128, 128])
        epsc = sb("epsc", [128, 1])
        wrel = sb("wrel", [D, REL, D])
        wrel_t = sb("wrel_t", [D, REL * D])
        m01 = sb("m01", [2 * D, 3 * D])
        m2 = sb("m2", [D, 3 * D])
        b_in = sb("b_in", [TP, D])
        nat = attr_in[:, :, :].rearrange("p s c -> p (s c)")
        gru_nat = nat[0:D, 0:6 * D].rearrange("p (m g e) -> p m g e", m=2, g=3)
        w_ih = sb("w_ih", [D + 1, 3, D])
        w_hh = sb("w_hh", [D + 1, 3, D])
        gb = sb("gb", [D, 2])
        w1_nat = nat[:, 6 * D:8 * D].rearrange("p (k e) -> p k e", k=2)
        w1pn = sb("w1pn", [2 * D, 2, 2 * D])
        w2_nat = msg[0:D, 0].rearrange("p j c -> p (j c)").rearrange("p (k e) -> p k e", k=2)
        w2pn = sb("w2pn", [2 * D, 2, D])
        b1pn = sb("b1pn", [TP, 2, 2 * D])
        b2pn = sb("b2pn", [TP, 2, D])
        spl_all = sb("spl_all", [128, 2, S_END])
        spl = sb("spl", [128, S_END])
        eg_all = attr_t[:, :, :].rearrange("p g c -> p (g c)")[:, 0:L3L * C_END].rearrange("p (l c) -> p l c", c=C_END)
        eg = acc2_all[:, 0:C_END]
        eg_norm = acc2_all[:, C_END:C_END + 2 * D]
        eg_res = acc2_all[:, C_END + 2 * D:C_END + 2 * D + 1]

        ps = ctx.enter_context(nc.psum_tensor("ps", [128, 8, 512], F32))
        sems = []

        def sem(name):
            s = ctx.enter_context(nc.semaphore(name))
            sems.append(s)
            return s

        cleared, loads, loads2 = sem("cleared"), sem("loads"), sem("loads2")
        dve_done, act_done, pe_step, ps_read, pool_done = (
            sem("dve_done"), sem("act_done"), sem("pe_step"), sem("ps_read"), sem("pool_done"))
        norm_ready, windows_set, msgw_ready = sem("norm_ready"), sem("windows_set"), sem("msgw_ready")
        targets_local, weights_turned, bn_ready = sem("targets_local"), sem("weights_turned"), sem("bn_ready")
        rows16_ready = sem("rows16_ready")
        last_weighed, part_rounded, left_ready = sem("last_weighed"), sem("part_rounded"), sem("left_ready")
        sums_turned, y_added, y_ready, eg_kept = sem("sums_turned"), sem("y_added"), sem("y_ready"), sem("eg_kept")
        tables_ready, part_ready = sem("tables_ready"), sem("part_ready")
        stored, h_ready, var_ready, std_ready = sem("stored"), sem("h_ready"), sem("var_ready"), sem("std_ready")
        product_ready, chunk_ready, deg_turned, deg_read = (
            sem("product_ready"), sem("chunk_ready"), sem("deg_turned"), sem("deg_read"))
        gates_done, rz_ready, pre_ready, cand_ready, hnew_ready, hnew_turned, ht_ready = (
            sem("gates_done"), sem("rz_ready"), sem("pre_ready"), sem("cand_ready"),
            sem("hnew_ready"), sem("hnew_turned"), sem("ht_ready"))
        idx_ready = [sem(f"idx_ready{s}") for s in range(UN)]
        gathered = [sem(f"gathered{s}") for s in range(UN)]
        attr_loaded = [sem(f"attr_loaded{s}") for s in range(UN)]
        idx_seen, onehot_ready, summed, acc_added = (
            sem("idx_seen"), sem("onehot_ready"), sem("summed"), sem("acc_added"))
        attr_turned, attr_kept, attr_seen = sem("attr_turned"), sem("attr_kept"), sem("attr_seen")
        hid_biased = sem("hid_biased")
        hid_sum, hid_ready, gate_done, msg_ready = (
            sem("hid_sum"), sem("hid_ready"), sem("gate_done"), sem("msg_ready"))
        out_done = sem("out_done")
        src_loaded = [sem(f"src_loaded{q}") for q in range(2)]
        hot_ready, rows_gathered, rows_summed, gate_biased = (
            sem("hot_ready"), sem("rows_gathered"), sem("rows_summed"), sem("gate_biased"))

        def rejoin():
            nc.multi_engine_barrier(list(mybir.ALL_ENGINES),
                                    sems_to_clear=range(sems[0].num, sems[-1].num + 1))

        def linked(eng, done):
            count = [0]

            def link(ins):
                count[0] += 1
                ins.then_inc(done, 1)
                eng.wait_ge(done, count[0])
            return link

        def by_tile(t):
            return t.rearrange("c (p b) -> c b p", b=TB)

        def row_bc(ap2, width):
            return ap2.unsqueeze(2).to_broadcast([ap2.shape[0], ap2.shape[1], width])

        def const_bc(ap1):
            return ap1.unsqueeze(1).to_broadcast([ap1.shape[0], TB, ap1.shape[1]])

        def bcast_rows(ap1, parts):
            return ap1.unsqueeze(0).to_broadcast([parts, ap1.shape[0]])

        with nc.Block() as block:
            @block.gpsimd
            def _(pool):
                nc.gpsimd.memset(raw_i[:], 0).then_inc(cleared, 1)
                nc.gpsimd.memset(raw_f[:], 0.0).then_inc(cleared, 1)
                nc.gpsimd.memset(eg_all[:], 0.0).then_inc(cleared, 1)
                nc.gpsimd.memset(spl_all[:], 0.0).then_inc(cleared, 1)
                nc.gpsimd.memset(ident[:], 0.0).then_inc(pool_done, 1)
                nc.gpsimd.iota(iota_i[:], pattern=[[1, WIN]], base=0, channel_multiplier=0).then_inc(pool_done, 1)
                nc.gpsimd.iota(node_i[:], pattern=[[1, TB]], base=-MID, channel_multiplier=TB).then_inc(pool_done, 1)
                pool.wait_ge(pool_done, 1)
                nc.gpsimd.affine_select(out=ident[:], in_=ident[:], compare_op=ALU.not_equal, fill=1.0,
                                        base=0, pattern=[[-1, 128]], channel_multiplier=1).then_inc(pool_done, 1)
                nc.gpsimd.memset(acc01[:], 0.0).then_inc(pool_done, 1)
                nc.gpsimd.memset(acc2[:], 0.0).then_inc(pool_done, 1)
                pool.wait_ge(pool_done, 6)

            @block.vector
            def _(v):
                for t in (dstrel, src_f, type_f, weight, h_t, y, spline_w, first_row, w1pn):
                    nc.vector.memset(t[:], 0.0).then_inc(dve_done, 1)
                nc.vector.memset(epsc[:], LN_EPS).then_inc(dve_done, 1)
                v.wait_ge(dve_done, 10)
                nc.vector.memset(h_t[D:D + 1, :, :], 1.0).then_inc(dve_done, 1)
                v.wait_ge(pool_done, 4)
                nc.vector.tensor_copy(iota0[:], iota_i[:]).then_inc(dve_done, 1)
                nc.vector.tensor_copy(node_no[:], row_bc(node_i[:], 128)).then_inc(dve_done, 1)
                nc.vector.memset(src_bc[:], 0.0).then_inc(dve_done, 1)
                v.wait_ge(dve_done, 14)

            @block.sync
            def _(sp):
                sp.wait_ge(cleared, 2)
                n = 0
                full, tail = (G - 1) * GE, TAIL
                for k, name in enumerate(("src", "dst", "edge_type_3")):
                    v = a[name]
                    sp.dma_start(raw_i[0:G - 1, k, :], v[0:full].rearrange("(g i) -> g i", i=GE)).then_inc(loads, 16)
                    sp.dma_start(raw_i[G - 1:G, k, 0:tail], v[full:E].unsqueeze(0)).then_inc(loads, 16)
                    n += 2
                sp.dma_start(raw_i[G - 1:G, 1, tail:GE], a["dst"][E - (GE - tail):E].unsqueeze(0)).then_inc(loads, 16)
                n += 1
                for k, v in ((3, a["edge_weight"]), (4, a["edge_weight1"].rearrange("e o -> (e o)"))):
                    sp.dma_start(raw_f[0:G - 1, k, :], v[0:full].rearrange("(g i) -> g i", i=GE)).then_inc(loads, 16)
                    sp.dma_start(raw_f[G - 1:G, k, 0:tail], v[full:E].unsqueeze(0)).then_inc(loads, 16)
                    n += 2
                sp.wait_ge(loads, 16 * n)

            @block.scalar
            def _(act):
                act.dma_start(x[:], a["x"].rearrange("(p b) c -> p b c", b=TB)).then_inc(loads2, 16)
                act.dma_start(wrel[:], a["L0_gnn_weight"].rearrange("r d e -> d r e")).then_inc(loads2, 16)
                act.dma_start(gru_nat[:, 0], a["L0_gnn_w_ih"].rearrange("(g d) e -> d g e", g=3)).then_inc(loads2, 16)
                act.dma_start(gru_nat[:, 1], a["L0_gnn_w_hh"].rearrange("(g d) e -> d g e", g=3)).then_inc(loads2, 16)
                bi, bh = a["L0_gnn_b_ih"].unsqueeze(0), a["L0_gnn_b_hh"].unsqueeze(0)
                w_ih_row = w_ih[D:D + 1].rearrange("p g e -> p (g e)")
                act.dma_start(w_ih_row[:, 0:D], bi[:, 2 * D:3 * D]).then_inc(loads2, 16)
                act.dma_start(w_ih_row[:, D:3 * D], bi[:, 0:2 * D]).then_inc(loads2, 16)
                act.dma_start(w_hh[D:D + 1].rearrange("p g e -> p (g e)"), bh).then_inc(loads2, 16)
                act.dma_start(b_in[:], bcast_rows(a["L0_gnn_b_ih"][2 * D:3 * D], TP)).then_inc(loads2, 16)
                act.dma_start(gb[:, 0:1], a["L0_gnn_gamma"].unsqueeze(1)).then_inc(loads2, 16)
                act.dma_start(gb[:, 1:2], a["L0_gnn_beta"].unsqueeze(1)).then_inc(loads2, 16)
                n = 10
                for k, s in enumerate("pn"):
                    act.dma_start(w1_nat[:, k], a[f"L1_gnn_W1{s}"]).then_inc(loads2, 16)
                    act.dma_start(w2_nat[:, k], a[f"L1_gnn_W2{s}"]).then_inc(loads2, 16)
                    act.dma_start(b1pn[:, k], bcast_rows(a[f"L1_gnn_b1{s}"], TP)).then_inc(loads2, 16)
                    act.dma_start(b2pn[:, k], bcast_rows(a[f"L1_gnn_b2{s}"], TP)).then_inc(loads2, 16)
                    n += 4
                act.wait_ge(loads2, 16 * n)
        rejoin()

        HALF = 13

        def node_stats(v, link, src, b0=0, b1=TB, turn=1):
            for b in range(b0, b1):
                s = nc.vector.bn_stats(stats[:, b, :], src[:, b, :])
            link(s)
            gap, mn, vr, st = nbias[:, b0:b1], mean[:, b0:b1], var[:, b0:b1], stats[:, b0:b1]
            link(nc.vector.tensor_tensor(gap, st[:, :, 1], st[:, :, 4], op=ALU.subtract))
            link(nc.vector.tensor_tensor(gap, gap, gap, op=ALU.mult))
            link(nc.vector.tensor_tensor(vr, st[:, :, 2], st[:, :, 5], op=ALU.add))
            link(nc.vector.tensor_scalar(vr, vr, 1.0 / D, None, ALU.mult))
            nc.vector.scalar_tensor_tensor(vr, gap, 0.25, vr, ALU.mult, ALU.add).then_inc(var_ready, 1)
            link(nc.vector.tensor_tensor(mn, st[:, :, 1], st[:, :, 4], op=ALU.add))
            link(nc.vector.tensor_scalar(mn, mn, 0.5, None, ALU.mult))
            v.wait_ge(std_ready, turn)
            link(nc.vector.reciprocal(vr, vr))
            nc.vector.scalar_tensor_tensor(gap, mn, -1.0, vr, ALU.mult, ALU.mult).then_inc(norm_ready, 1)

        def norm_tiles_dve(v, link, src, dst, b0=0, b1=HALF):
            for b in range(b0, b1):
                s = nc.vector.tensor_scalar(dst[:, b, :], src[:, b, :], mean[:, b:b + 1], var[:, b:b + 1],
                                            ALU.subtract, ALU.mult)
            link(s)

        def norm_tiles_act(act, src, dst, func, done, stats_of=(0, TB), b0=HALF, b1=TB, turn=1):
            act.wait_ge(var_ready, turn)
            vr = var[:, stats_of[0]:stats_of[1]]
            nc.scalar.activation(vr, vr, ACT.Sqrt, bias=epsc[0:TP, :]).then_inc(std_ready, 1)
            act.wait_ge(norm_ready, turn)
            for b in range(b0, b1):
                s = nc.scalar.activation(dst[:, b, :], src[:, b, :], func, bias=nbias[:, b:b + 1],
                                         scale=var[:, b:b + 1])
            s.then_inc(done, 1)

        def layer_norm_relu(v, link, src, dst, done):
            node_stats(v, link, src)
            norm_tiles_dve(v, link, src, dst)
            link(nc.vector.tensor_scalar(dst[:, 0:HALF, :], dst[:, 0:HALF, :], 0.0, None, ALU.max))
            v.sem_inc(done, 1)

        def make_parts(v, link, rows, left, out_parts):
            for k in range(PARTS):
                part = out_parts[..., k * D:(k + 1) * D]
                link(nc.vector.tensor_copy(part, rows if k == 0 else left))
                if k < PARTS - 1:
                    link(nc.vector.tensor_tensor(left, rows if k == 0 else left, part, op=ALU.subtract))

        def parts_of_h(v, link, b0, b1):
            left = hid_t[0:TP, :].rearrange("p (b k c) -> p b k c", b=TB, k=2)[:, b0:b1, 0, :]
            make_parts(v, link, h[:, b0:b1, :], left, parts[0][:, b0:b1, :])

        def first_windows(v):
            nc.vector.tensor_copy(iota[:], iota0[:]).then_inc(windows_set, 1)
            nc.vector.tensor_copy(win_f[:], first_row[:]).then_inc(windows_set, 1)
            nc.vector.tensor_copy(win_row[:], first_row[:]).then_inc(windows_set, 1)

        def load_late_constants(sp):
            n = 0
            for l in (0, 1):
                sp_w = a[f"L2_gnn_w{l + 1}"]
                sp.dma_start(spl_all[:, l, S_W:S_W + D], sp_w.rearrange("k d e -> (k d) e")).then_inc(loads2, 16)
                sp.dma_start(spl_all[0:D, l, S_ROOT:S_ROOT + D], a[f"L2_gnn_root{l + 1}"]).then_inc(loads2, 16)
                sp.dma_start(spl_all[D:D + 1, l, S_ROOT:S_ROOT + D],
                              a[f"L2_gnn_b{l + 1}"].unsqueeze(0)).then_inc(loads2, 16)
                n += 3
            for j in range(EJ):
                o = C_WE1 + j * D
                sp.dma_start(eg_all[ED * j:ED * j + ED, :, o:o + D],
                              a["L3_gnn_We1"].rearrange("l k d -> k l d")).then_inc(loads2, 16)
                n += 1
            for j in range(2):
                o = C_WE2 + j * D
                sp.dma_start(eg_all[D * j:D * j + D, :, o:o + D],
                              a["L3_gnn_We2"].rearrange("l k d -> k l d")).then_inc(loads2, 16)
                sp.dma_start(eg_all[D * j:D * j + D, :, C_BE1:C_BE1 + 1],
                              a["L3_gnn_be1"].rearrange("l k -> k l").unsqueeze(2)).then_inc(loads2, 16)
                n += 2
            sp.dma_start(eg_all[0:D, :, C_W1:C_W1 + 2 * D],
                          a["L3_gnn_W1"].rearrange("l k d -> k l d")).then_inc(loads2, 16)
            sp.dma_start(eg_all[:, :, C_W2:C_W2 + D],
                          a["L3_gnn_W2"].rearrange("l k d -> k l d")).then_inc(loads2, 16)
            sp.dma_start(eg_all[:, :, C_B1:C_B1 + 1],
                          a["L3_gnn_b1"].rearrange("l k -> k l").unsqueeze(2)).then_inc(loads2, 16)
            n += 3
            for c, name in ((C_B2, "b2"), (C_G, "ln_g"), (C_B, "ln_b")):
                v = a[f"L3_gnn_{name}"]
                sp.dma_start(eg_all[:, :, c:c + D],
                              v.unsqueeze(0).to_broadcast([128, L3L, D])).then_inc(loads2, 16)
                n += 1
            for j in range(EJ):
                o = C_BE2 + j * D
                sp.dma_start(eg_all[:, :, o:o + D],
                              a["L3_gnn_be2"].unsqueeze(0).to_broadcast([128, L3L, D])).then_inc(loads2, 16)
                n += 1
            for c, name in ((C_RES, "res_w"), (C_DOT, "dot_scale")):
                v = a[f"L3_gnn_{name}"]
                sp.dma_start(eg_all[:, :, c:c + 1],
                              v.unsqueeze(0).unsqueeze(2).to_broadcast([128, L3L, 1])).then_inc(loads2, 16)
                n += 1
            return n

        table_h = table[0:N, :].rearrange("(p b) c -> p b c", b=TB)
        table_n = table[N:2 * N, :].rearrange("(p b) c -> p b c", b=TB)

        def flat(ap):
            return ap.rearrange("p a b -> p (a b)")

        def node_cols(ap, b):
            return ap[:, b:b + TB * (TP - 1) + 1:TB]

        with nc.Block() as block:
            @block.vector
            def _(v):
                link = linked(v, dve_done)
                link(nc.vector.tensor_copy(flat(raw_f[:, 0:3, :]), flat(raw_i)))
                link(nc.vector.tensor_reduce(first[:, 0:1], raw_f[:, 1, :], AX, ALU.min))
                link(nc.vector.tensor_reduce(last[:], raw_f[:, 1, :], AX, ALU.max))
                link(nc.vector.tensor_tensor(first[:, 1:2], last[:], first[:, 0:1], op=ALU.subtract))
                nc.vector.tensor_scalar(raw_f[:, 1, :], raw_f[:, 1, :], first[:, 0:1], None,
                                        ALU.subtract).then_inc(targets_local, 1)
                for k, dst in ((0, src_f), (1, dstrel), (2, type_f), (3, weight)):
                    v.wait_ge(pe_step, k + 1)
                    nc.vector.tensor_copy(dst[:, 0:G, :],
                                          ps[:, k, 0:EJ * G].rearrange("p (j g) -> p g j", j=EJ)).then_inc(ps_read, 1)
                v.wait_ge(pe_step, 5)
                nc.vector.tensor_copy(spline_w[:, 0:G, :, 1],
                                      ps[:, 4, 0:EJ * G].rearrange("p (j g) -> p g j", j=EJ)).then_inc(ps_read, 1)
                v.wait_ge(pe_step, 6)
                nc.vector.tensor_copy(first_row[:, 0:G], ps[0:1, 5, 0:G]).then_inc(ps_read, 1)
                nc.vector.tensor_copy(span_row[:], ps[0:1, 5, 128:128 + G]).then_inc(ps_read, 1)
                v.wait_ge(ps_read, 7)
                nc.vector.tensor_scalar(spline_w[:, :, :, 0], spline_w[:, :, :, 1], -1.0, 1.0, ALU.mult, ALU.add)
                for r in range(REL):
                    nc.vector.scalar_tensor_tensor(rel_w[:, :, :, r], type_f[:], float(r), weight[:],
                                                   ALU.is_equal, ALU.mult)
                for t in (sign_w, deg_w):
                    nc.vector.tensor_scalar(t[:, :, :, 0], weight[:], 0.0, None, ALU.max)
                    nc.vector.tensor_scalar(t[:, :, :, 1], weight[:], -1.0, 0.0, ALU.mult, ALU.max)
                nc.vector.memset(deg_w[:, :, :, 2], 1.0)
                link(nc.vector.tensor_copy(src_i[:], src_f[:]))
                link(nc.vector.tensor_scalar(type_f[:], weight[:], 0.0, float(N), ALU.is_lt, ALU.mult))
                link(nc.vector.tensor_tensor(srcsign_i[:], type_f[:], src_f[:], op=ALU.add))
                link(nc.vector.tensor_reduce(span_row[:, 0:1], span_row[:], AX, ALU.max))
                link(nc.vector.tensor_copy(span[:, 0:1], span_row[:, 0:1]))
                link(nc.vector.tensor_scalar(span[:, 0:1], span[:, 0:1], WIN.bit_length() - 1, None,
                                             ALU.logical_shift_right))
                link(nc.vector.tensor_scalar(span[:, 0:1], span[:, 0:1], 1.0, None, ALU.add))
                w3 = raw_f[:, 3, :].rearrange("g (p j) -> g j p", j=EJ)[:, EJ - 1, :]
                s3 = raw_f[:, 0, :].rearrange("g (p j) -> g j p", j=EJ)[:, EJ - 1, :]
                link(nc.vector.tensor_scalar(rows16[:, 0, :], s3, float(-MID), None, ALU.add))
                for k, op in ((1, ALU.is_lt), (2, ALU.is_ge)):
                    link(nc.vector.tensor_scalar(sign16[:], w3, 0.0, NEVER, op, ALU.mult))
                    link(nc.vector.tensor_tensor(rows16[:, k, :], sign16[:], rows16[:, 0, :], op=ALU.add))
                v.sem_inc(rows16_ready, 1)
                layer_norm_relu(v, link, x, h, h_ready)
                first_windows(v)
                parts_of_h(v, link, 0, HALF)
                link(nc.vector.tensor_tensor(b1pn[:, 0], b1pn[:, 0], b1pn[:, 1], op=ALU.subtract))
                link(nc.vector.tensor_tensor(b2pn[:, 0], b2pn[:, 0], b2pn[:, 1], op=ALU.subtract))
                v.wait_ge(act_done, 3)
                link(nc.vector.tensor_tensor(w_hh[D:D + 1, 0:2, :], w_hh[D:D + 1, 0:2, :], w_ih[D:D + 1, 1:3, :],
                                             op=ALU.add))
                v.wait_ge(h_ready, 2)
                parts_of_h(v, link, HALF, TB)

            @block.gpsimd
            def _(pool):
                pool.wait_ge(targets_local, 1)
                nc.gpsimd.affine_select(out=raw_f[:, 1, :], in_=raw_f[:, 1, :], compare_op=ALU.is_ge, fill=FAR,
                                        base=E - 1, pattern=[[-1, GE]], channel_multiplier=-GE).then_inc(pool_done, 1)
                pool.wait_ge(pool_done, 1)

            @block.tensor
            def _(pe):
                for m in (0, 1):
                    for g in range(3):
                        t = nc.tensor.transpose(ps[0:D, 6, (3 * m + g) * D:(3 * m + g + 1) * D],
                                                gru_nat[:, m, g, :], ident[0:D, 0:D])
                t.then_inc(weights_turned, 1)
                for k in range(2):
                    nc.tensor.transpose(ps[0:D, 7, k * 128:(k + 1) * 128], w1_nat[:, k, :], ident[:, :])
                for k in range(2):
                    t = nc.tensor.transpose(ps[:, 7, 256 + k * D:256 + (k + 1) * D], w2_nat[:, k, :], ident[0:D, 0:D])
                t.then_inc(weights_turned, 1)
                pe.wait_ge(targets_local, 1)
                for k in range(5):
                    if k == 1:
                        pe.wait_ge(pool_done, 1)
                    for j in range(EJ):
                        t = nc.tensor.transpose(ps[:, k, j * G:(j + 1) * G],
                                                raw_f[:, k, :].rearrange("g (p j) -> g j p", j=EJ)[:, j, :],
                                                ident[0:G, 0:G])
                    t.then_inc(pe_step, 1)
                for k in range(2):
                    t = nc.tensor.transpose(ps[0:1, 5, k * 128:k * 128 + G], first[:, k:k + 1], ident[0:G, 0:G])
                t.then_inc(pe_step, 1)
                pe.wait_ge(act_done, 5)
                for r in range(REL):
                    t = nc.tensor.transpose(ps[0:D, 6, r * D:(r + 1) * D], wrel[:, r, :], ident[0:D, 0:D])
                t.then_inc(weights_turned, 1)
                pe.wait_ge(act_done, 6)
                w_ih_k = w_ih[0:D].rearrange("p g e -> p (g e)")
                nc.tensor.matmul(ps[:, 7, 0:3 * D], wrel_t[:, 0:2 * D], w_ih_k, start=True, stop=True)
                nc.tensor.matmul(ps[0:D, 7, 256:256 + 3 * D], wrel_t[:, 2 * D:3 * D], w_ih_k,
                                 start=True, stop=True).then_inc(weights_turned, 1)

            @block.scalar
            def _(act):
                act.wait_ge(weights_turned, 1)
                g_ih = ps[0:D, 6, 0:3 * D].rearrange("p (g e) -> p g e", g=3)
                nc.scalar.copy(w_ih[0:D, 0, :], g_ih[:, 2, :]).then_inc(act_done, 1)
                nc.scalar.copy(w_ih[0:D, 1:3, :], g_ih[:, 0:2, :]).then_inc(act_done, 1)
                nc.scalar.copy(w_hh[0:D, :, :], ps[0:D, 6, 3 * D:6 * D].rearrange("p (g e) -> p g e", g=3)).then_inc(act_done, 1)
                act.wait_ge(weights_turned, 2)
                for k in range(2):
                    c = nc.scalar.copy(w1pn[k * D:(k + 1) * D, k, :], ps[0:D, 7, k * 128:(k + 1) * 128])
                c.then_inc(act_done, 1)
                nc.scalar.copy(w2pn[:], ps[:, 7, 256:256 + 2 * D].rearrange("p (k e) -> p k e", k=2)).then_inc(act_done, 1)
                act.wait_ge(weights_turned, 3)
                nc.scalar.copy(wrel_t[:], ps[0:D, 6, 0:REL * D]).then_inc(act_done, 1)
                act.wait_ge(weights_turned, 4)
                nc.scalar.copy(m01[:], ps[:, 7, 0:3 * D]).then_inc(act_done, 1)
                nc.scalar.copy(m2[:], ps[0:D, 7, 256:256 + 3 * D]).then_inc(act_done, 1)
                norm_tiles_act(act, x, h, ACT.Relu, h_ready)
                act.wait_ge(act_done, 8)

            @block.sync
            def _(sp):
                n = load_late_constants(sp)
                sp.wait_ge(rows16_ready, 1)
                for pair, k, at in ((src_rows, 0, None), (sign_rows, 1, 0), (sign_rows, 2, 1)):
                    rows = pair[0:G // 2, :].rearrange("m (e p) -> m e p", e=2)
                    if at is None:
                        sp.dma_start(rows.rearrange("m e p -> (m e) p"), rows16[:, k, :]).then_inc(stored, 16)
                    else:
                        sp.dma_start(sign_all[:, at, :], rows16[:, k, :]).then_inc(stored, 16)
                sp.wait_ge(stored, 48)
                sp.dma_start(sign_rows[0:G // 2, :].rearrange("m (k p) -> m k p", k=2),
                             sign_all.rearrange("(m e) k p -> m e k p", e=2)[:, 1]).then_inc(loads, 16)
                sp.wait_ge(loads2, 16 * n)
                sp.dma_start(eg_dram.rearrange("l p c -> p l c"), eg_all[:, :, :]).then_inc(loads2, 16)
                sp.wait_ge(h_ready, 2)
                sp.dma_start(table_h, h[:]).then_inc(stored, 16)
                sp.wait_ge(loads2, 16 * n + 16)
                sp.wait_ge(loads, 16)
                sp.wait_ge(stored, 64)
        rejoin()

        SPAN = nc.values_load(span[0:1, 0:1], min_val=1, max_val=SPAN_MAX)

        def next_windows(v):
            nc.vector.tensor_scalar(iota[:], iota[:], float(WIN), None, ALU.add).then_inc(windows_set, 1)
            nc.vector.tensor_scalar(win_f[:], win_f[:], float(WIN), float(N), ALU.add, ALU.min).then_inc(windows_set, 1)
            v.wait_ge(windows_set, 2)
            nc.vector.tensor_copy(win_row[:], win_f[:]).then_inc(windows_set, 1)
            v.wait_ge(windows_set, 3)

        def on_pe(s, both):
            return both or s % 2 == 1

        def gather_rows(pool, rows, both):
            with pool.Fori(0, G // UN) as i:
                for s in range(UN):
                    pool.wait_ge(idx_ready[s], i + 1)
                    pool.sem_inc(idx_seen, 1)
                    for j in range(EJ - on_pe(s, both)):
                        nc.gpsimd.indirect_dma_start(
                            out=gath[:, s, j, :], out_offset=None, in_=table[0:rows, :],
                            in_offset=bass.IndirectOffsetOnAxis(ap=idx[:, s, j:j + 1], axis=0),
                        ).then_inc(gathered[s], 16)
            for s in range(UN):
                pool.wait_ge(gathered[s], 16 * (EJ - on_pe(s, both)) * (G // UN))
            pool.dma_reset(range(gathered[0].num, gathered[-1].num + 1))

        def rows_here(eng, i, s, both):
            per_turn = 16 * (EJ - on_pe(s, both))
            eng.wait_ge(gathered[s], i * per_turn + per_turn)
            if both:
                eng.wait_ge(rows_summed, i * UN + s + 1)
            elif on_pe(s, both):
                eng.wait_ge(rows_summed, i * 2 + s // 2 + 1)

        def load_sources(sp, pairs, m, q):
            row = pairs[bass.ds(m, 1), :].to_broadcast([128, 2 * 128])
            sp.dma_start(src_bc[:, q, :], row).then_inc(src_loaded[q], 16)

        def hot_half(q, half, both, signed):
            e0 = 0 if both or signed else 1
            b0, b1 = (0, 13) if half == 0 else (13, TB)
            shape = [TP, b1 - b0, 2 - e0, 128]
            columns = src_bc[0:TP, q, 128 * e0:256].rearrange("p (e c) -> p e c", e=2 - e0)
            return nc.vector.tensor_tensor(
                src_hot[q][:, b0:b1, 128 * e0:256].rearrange("p b (e c) -> p b e c", e=2 - e0),
                columns.unsqueeze(1).to_broadcast(shape),
                node_no[:, b0:b1, :].unsqueeze(2).to_broadcast(shape), op=ALU.is_equal)

        def gather_pe(q, odd, signed, bank):
            terms = [(k, b) for k in range(1 + signed) for b in range(TB)]
            for n, (k, b) in enumerate(terms):
                c0 = k * 128 if signed else odd * 128
                m = nc.tensor.matmul(ps[:, bank, 0:PARTS * D], src_hot[q][:, b, c0:c0 + 128], parts[k][:, b, :],
                                     start=(n == 0), stop=(n == len(terms) - 1))
            m.then_inc(rows_gathered, 1)

        def sum_parts(slot, bank):
            return nc.vector.tensor_reduce(gath[:, slot, EJ - 1, :],
                                           ps[:, bank, 0:PARTS * D].rearrange("p (k c) -> p c k", k=PARTS),
                                           AX, ALU.add)

        def step_hot_dve(v, i, s, both, signed, last):
            if last:
                return
            if s % 2 == 0:
                v.wait_ge(src_loaded[s // 2], i * 16 + 32)
                hot_half(s // 2, 0, both, signed)
            else:
                hot_half(s // 2, 1, both, signed).then_inc(hot_ready, 1)

        def step_gather_pe(pe, i, s, both, signed, last):
            if on_pe(s, both) and not (last and s >= UN - 2):
                pe.wait_ge(hot_ready, i * 2 + s // 2 + 2)
                pe.wait_ge(rows_summed, i * UN + s + 1 if both else i * 2 + s // 2 + 1)
                gather_pe((s // 2 + 1) % 2, s % 2, signed, 6 + s % 2)

        def step_sum_dve(v, i, s, both, last):
            if on_pe(s, both) and not (last and s >= UN - 2):
                v.wait_ge(rows_gathered, i * UN + s + 3 if both else i * 2 + s // 2 + 2)
                sum_parts((s + 2) % UN, 6 + s % 2).then_inc(rows_summed, 1)

        def first_hot_dve(v, both, signed):
            for q in range(2):
                v.wait_ge(src_loaded[q], 16)
                hot_half(q, 0, both, signed)
                hot_half(q, 1, both, signed).then_inc(hot_ready, 1)
            for g in range(2):
                if on_pe(g, both):
                    v.wait_ge(rows_gathered, g + 1 if both else 1)
                    sum_parts(g, 6 + g).then_inc(rows_summed, 1)

        def first_gather_pe(pe, both, signed):
            pe.wait_ge(hot_ready, 1)
            for g in range(2):
                if on_pe(g, both):
                    gather_pe(0, g, signed, 6 + g)

        def group(ap, g):
            return ap[:, bass.ds(g, 1), :].rearrange("p a j -> p (a j)")

        def build_onehot(g, slot):
            return nc.vector.tensor_tensor(
                onehot[:, slot], iota[:].unsqueeze(1).to_broadcast([128, EJ, WIN]),
                group(dstrel, g).unsqueeze(2).to_broadcast([128, EJ, WIN]), op=ALU.is_equal)

        def copy_index(index, g, slot):
            return nc.vector.tensor_scalar(idx[:, slot, :], group(index, g), 0.0, None, ALU.add)

        def weighted_pass(index, weights, R, first_layer, both):
            signed = index is srcsign_i
            rows, pairs = (2 * N, sign_rows) if signed else (N, src_rows)
            built = 3 if first_layer else 2
            adds = 2 if first_layer else 1

            with nc.Block(no_gpsimd_drain=True) as block:
                @block.gpsimd
                def _(pool):
                    gather_rows(pool, rows, both)

                @block.vector
                def _(v):
                    def prepare(g, slot):
                        build_onehot(g, slot).then_inc(onehot_ready, 1)
                        nc.vector.tensor_copy(w_c[:, slot],
                                              weights[:, bass.ds(g, 1), :, 0:2].rearrange("p a j r -> p (a j) r")
                                              ).then_inc(onehot_ready, 1)
                        if first_layer:
                            nc.vector.tensor_copy(msg_w[:, slot, :, REL * D:REL * D + 3],
                                                  deg_w[:, bass.ds(g, 1), :, :].rearrange("p a j r -> p (a j) r")
                                                  ).then_inc(onehot_ready, 1)

                    def weigh_last(g, slot):
                        w = weights[:, bass.ds(g, 1), :, R - 1].rearrange("p a j -> p (a j)")
                        nc.vector.tensor_tensor(msg_w[:, slot % 2, :, 2 * D:3 * D], gath[:, slot],
                                                w.unsqueeze(2).to_broadcast([128, EJ, D]),
                                                op=ALU.mult).then_inc(last_weighed, 1)

                    for s in range(UN):
                        copy_index(index, s, s).then_inc(idx_ready[s], 1)
                    prepare(0, 0)
                    first_hot_dve(v, both, signed)
                    def turn(i, last):
                        for s in range(UN):
                            g = i * UN + s
                            if first_layer:
                                rows_here(v, i, s, both)
                                weigh_last(g, s)
                            if not (last and s == UN - 1):
                                prepare(g + 1, (s + 1) % 2)
                            step_hot_dve(v, i, s, both, signed, last)
                            if not last:
                                v.wait_ge(msgw_ready, g + 1)
                                if first_layer:
                                    v.wait_ge(last_weighed, g + 1)
                                copy_index(index, g + UN, s).then_inc(idx_ready[s], 1)
                            col = v.value_load(win_row[0:1, bass.ds(g, 1)], min_val=0, max_val=N)
                            v.wait_ge(summed, g + 1)
                            nc.vector.tensor_tensor(acc01[:, bass.ds(col, WIN)], acc01[:, bass.ds(col, WIN)],
                                                    ps[:, s % 2, 0:WIN], op=ALU.add).then_inc(acc_added, 1)
                            if first_layer:
                                nc.vector.tensor_tensor(acc2[:, bass.ds(col, WIN)], acc2[:, bass.ds(col, WIN)],
                                                        ps[0:D + 3, s % 2, WIN:2 * WIN], op=ALU.add).then_inc(acc_added, 1)
                            step_sum_dve(v, i, s, both, last)
                            v.wait_ge(acc_added, adds * g + adds)

                    with v.Fori(0, G // UN - 1) as i:
                        turn(i, False)
                    turn(G // UN - 1, True)
                    next_windows(v)

                @block.scalar
                def _(act):
                    if first_layer:
                        act.sem_inc(attr_kept, 2)
                    with act.Fori(0, G // UN) as i:
                        for s in range(UN):
                            g = i * UN + s
                            rows_here(act, i, s, both)
                            act.wait_ge(onehot_ready, built * g + built)
                            for j in range(EJ):
                                for r in range(2):
                                    m = nc.scalar.activation(msg_w[:, s % 2, j, r * D:(r + 1) * D], gath[:, s, j, :],
                                                             ACT.Copy, scale=w_c[:, s % 2, j, r:r + 1])
                            m.then_inc(msgw_ready, 1)
                            if first_layer:
                                act.wait_ge(attr_turned, g + 1)
                                act.sem_inc(attr_seen, 1)
                                nc.scalar.copy(attr_t[:, bass.ds(g, 1), :].rearrange("p a c -> p (a c)"),
                                               ps[:, 2 + s % 2, 0:128]).then_inc(attr_kept, 1)

                @block.tensor
                def _(pe):
                    def turn(i, last):
                        for s in range(UN):
                            g = i * UN + s
                            if first_layer:
                                pe.wait_ge(attr_loaded[s], i * 16 + 16)
                                pe.wait_ge(attr_kept, g + 1)
                                nc.tensor.transpose(ps[:, 2 + s % 2, 0:128], attr_in[:, s, :],
                                                    ident[:, :]).then_inc(attr_turned, 1)
                            step_gather_pe(pe, i, s, both, signed, last)
                            pe.wait_ge(onehot_ready, built * g + built)
                            pe.wait_ge(msgw_ready, g + 1)
                            if first_layer:
                                pe.wait_ge(last_weighed, g + 1)
                            for j in range(EJ):
                                m = nc.tensor.matmul(ps[:, s % 2, 0:WIN], msg_w[:, s % 2, j, 0:2 * D],
                                                     onehot[:, s % 2, j, :], start=(j == 0), stop=(j == EJ - 1))
                            if first_layer:
                                for j in range(EJ):
                                    m = nc.tensor.matmul(ps[0:D + 3, s % 2, WIN:2 * WIN],
                                                         msg_w[:, s % 2, j, 2 * D:3 * D + 3],
                                                         onehot[:, s % 2, j, :], start=(j == 0), stop=(j == EJ - 1))
                            m.then_inc(summed, 1)

                    first_gather_pe(pe, both, signed)
                    with pe.Fori(0, G // UN - 1) as i:
                        turn(i, False)
                    turn(G // UN - 1, True)

                @block.sync
                def _(sp):
                    for q in range(2):
                        load_sources(sp, pairs, q, q)
                    if not first_layer:
                        source_loop(sp, pairs)
                        return
                    attr = a["edge_attr_32"]

                    def load(g, s, parts=128):
                        rows = attr[bass.ds(g * GE, parts * EJ), :]
                        sp.dma_start(attr_in[0:parts, s, :],
                                     rows.rearrange("(p j) k -> p (j k)", j=EJ)).then_inc(attr_loaded[s], 16)
                    for s in range(UN):
                        load(s, s)

                    def sources_before(i, s):
                        if s == 1:
                            next_sources(sp, pairs, i, 1)
                        if s == 3:
                            next_sources(sp, pairs, i + 1, 0)
                    next_sources(sp, pairs, 0, 0)
                    with sp.Fori(0, G // UN - 2) as i:
                        for s in range(UN):
                            sources_before(i, s)
                            sp.wait_ge(attr_turned, i * UN + s + 1)
                            load(i * UN + s + UN, s)
                    for s in range(UN - 1):
                        sources_before(G // UN - 2, s)
                        sp.wait_ge(attr_turned, G - 2 * UN + s + 1)
                        load(G - UN + s, s)
                    sp.wait_ge(attr_turned, G - UN)
                    whole, rest = TAIL // EJ, TAIL % EJ
                    if rest:
                        e0 = E - rest
                        sp.dma_start(attr_in[whole:whole + 1, UN - 1, 0:rest * ED],
                                     attr[e0:E, :].rearrange("j k -> (j k)").unsqueeze(0)).then_inc(loads, 16)
                        sp.wait_ge(loads, 16)
                    load(G - 1, UN - 1, parts=whole)
                    for q in range(2):
                        sp.wait_ge(src_loaded[q], 16 * (G // UN))
            rejoin()

        def next_sources(sp, pairs, i, q):
            sp.wait_ge(hot_ready, i * 2 + q + 1)
            load_sources(sp, pairs, i * 2 + q + 2, q)

        def source_loop(sp, pairs):
            with sp.Fori(0, G // UN - 1) as i:
                for q in range(2):
                    next_sources(sp, pairs, i, q)
            for q in range(2):
                sp.wait_ge(src_loaded[q], 16 * (G // UN))

        def weighted_round(index, weights, R, first_layer=False, both=False):
            with nc.Fori(0, SPAN):
                weighted_pass(index, weights, R, first_layer, both)

        C4 = chunks(TB, 4)
        C8 = chunks(TB, 8)

        def tiles4(bank, b0, b1, parts=D):
            return ps[0:parts, bank, 0:(b1 - b0) * TP].rearrange("p (b n) -> p b n", n=TP)

        CG = [(0, 8), (8, 15), (15, 21), (21, TB)]
        with nc.Fori(0, 2):
            weighted_round(src_i, rel_w, REL, first_layer=True)
            with nc.Block() as block:
                @block.tensor
                def _(pe):
                    def gates(q):
                        b0, b1 = CG[q]
                        for b in range(b0, b1):
                            t = ps[0:TP, 4 * (q % 2) + (b - b0) // 2,
                                   256 * ((b - b0) % 2):256 * ((b - b0) % 2) + 256]
                            nc.tensor.matmul(t[:, 0:3 * D], node_cols(acc01, b), m01[:], start=True, stop=False)
                            nc.tensor.matmul(t[:, 0:3 * D], node_cols(acc2[0:D], b), m2[:], start=False, stop=False)
                            nc.tensor.matmul(t[:, D:3 * D], h_t[:, b, :], w_hh[:, 0:2, :].rearrange("p g e -> p (g e)"),
                                             start=False, stop=True)
                            m = nc.tensor.matmul(t[:, 3 * D:4 * D], h_t[:, b, :], w_hh[:, 2, :], start=True, stop=True)
                        m.then_inc(gates_done, 1)

                    def turn(q):
                        pe.wait_ge(hnew_ready, q + 1)
                        b0, b1 = CG[q]
                        for c in range(-(-(b1 - b0) // 4)):
                            for b in range(b0 + 4 * c, min(b1, b0 + 4 * c + 4)):
                                o = (b - b0 - 4 * c) * TP
                                m = nc.tensor.transpose(ps[0:D, 4 * (q % 2) + c, o:o + TP], h[:, b, :],
                                                        ident[0:TP, 0:TP])
                            m.then_inc(hnew_turned, 1)

                    for b in range(TB):
                        m = nc.tensor.transpose(ps[0:TP, 7, 3 * b:3 * b + 3], node_cols(acc2[D:D + 3], b),
                                                ident[D:D + 3, D:D + 3])
                    m.then_inc(deg_turned, 1)
                    for q in range(len(CG)):
                        if q == 1:
                            pe.wait_ge(deg_read, 1)
                        if q >= 2:
                            pe.wait_ge(ht_ready, 2 * q - 2)
                        gates(q)
                        if q >= 1:
                            turn(q - 1)
                    turn(len(CG) - 1)

                def gate_bank(q):
                    n = CG[q][1] - CG[q][0]
                    return ps[0:TP, 4 * (q % 2):4 * (q % 2) + 4, :].rearrange("p k (t c) -> p (k t) c", t=2)[:, 0:n, :]

                @block.scalar
                def _(act):
                    def keep(q):
                        b0, b1 = CG[q]
                        for c in range(-(-(b1 - b0) // 4)):
                            act.wait_ge(hnew_turned, 2 * q + c + 1)
                            t0, t1 = b0 + 4 * c, min(b1, b0 + 4 * c + 4)
                            nc.scalar.copy(h_t[0:D, t0:t1, :], tiles4(4 * (q % 2) + c, t0, t1)).then_inc(ht_ready, 1)

                    for q, (b0, b1) in enumerate(CG):
                        act.wait_ge(gates_done, q + 1)
                        nc.scalar.activation(rz[:, q % 2, 0:b1 - b0, :], gate_bank(q)[:, :, D:3 * D],
                                             ACT.Sigmoid).then_inc(rz_ready, 1)
                        act.wait_ge(pre_ready, q + 1)
                        nc.scalar.activation(cand[:, q % 2, 0:b1 - b0, :], cand[:, q % 2, 0:b1 - b0, :],
                                             ACT.Tanh).then_inc(cand_ready, 1)
                        if q >= 1:
                            keep(q - 1)
                    keep(len(CG) - 1)

                @block.vector
                def _(v):
                    link = linked(v, dve_done)
                    first_windows(v)
                    v.wait_ge(deg_turned, 1)
                    nc.vector.tensor_copy(deg[:], ps[0:TP, 7, 0:3 * TB].rearrange("p (b k) -> p b k", k=3)).then_inc(deg_read, 1)
                    for q, (b0, b1) in enumerate(CG):
                        n = b1 - b0
                        t = gate_bank(q)
                        r_, z_ = rz[:, q % 2, 0:n, 0:D], rz[:, q % 2, 0:n, D:2 * D]
                        cn, mx = cand[:, q % 2, 0:n, :], mix[:, q % 2, 0:n, :]
                        v.wait_ge(rz_ready, q + 1)
                        link(nc.vector.tensor_tensor(cn, r_, t[:, :, 3 * D:4 * D], op=ALU.mult))
                        link(nc.vector.tensor_tensor(cn, cn, t[:, :, 0:D], op=ALU.add))
                        nc.vector.tensor_tensor(cn, cn, b_in[:].unsqueeze(1).to_broadcast([TP, n, D]),
                                                op=ALU.add).then_inc(pre_ready, 1)
                        v.wait_ge(cand_ready, q + 1)
                        link(nc.vector.tensor_tensor(mx, y[:, b0:b1, :], cn, op=ALU.subtract))
                        link(nc.vector.tensor_tensor(mx, mx, z_, op=ALU.mult))
                        nc.vector.tensor_tensor(h[:, b0:b1, :], cn, mx, op=ALU.add).then_inc(hnew_ready, 1)
                        v.wait_ge(hnew_ready, q + 1)
                        link(nc.vector.tensor_copy(y[:, b0:b1, :], h[:, b0:b1, :]))
                        parts_of_h(v, link, b0, b1)

                @block.sync
                def _(sp):
                    sp.wait_ge(hnew_ready, len(CG))
                    sp.dma_start(table_h, h[:]).then_inc(stored, 16)
                    sp.wait_ge(stored, 16)

                @block.gpsimd
                def _(pool):
                    pool.wait_ge(gates_done, len(CG))
                    nc.gpsimd.memset(acc01[:], 0.0).then_inc(pool_done, 1)
                    nc.gpsimd.memset(acc2[:], 0.0).then_inc(pool_done, 1)
                    pool.wait_ge(pool_done, 2)
            rejoin()

        def start_sums_pe(pe):
            for c, (b0, b1) in enumerate(C4):
                if c >= 2:
                    pe.wait_ge(ps_read, c - 1)
                for b in range(b0, b1):
                    t = nc.tensor.transpose(ps[:, 4 + c % 2, (b - b0) * TP:(b - b0 + 1) * TP], wide[:, b, :],
                                            ident[0:TP, 0:TP])
                t.then_inc(pe_step, 1)

        def signed_rest():
            return [hid_t[0:TP, :].rearrange("p (b k c) -> p b k c", b=TB, k=2)[:, :, k, :] for k in range(2)]

        def signed_parts_dve(v):
            left = signed_rest()
            for n in range(PARTS - 1):
                for k in range(2):
                    v.wait_ge(part_rounded, 2 * n + k + 1)
                    if n > 0:
                        v.wait_ge(left_ready, 2 * (n - 1) + k + 1)
                    nc.vector.tensor_tensor(left[k], wide[:, :, k * D:(k + 1) * D] if n == 0 else left[k],
                                            parts[k][:, :, n * D:(n + 1) * D], op=ALU.subtract).then_inc(left_ready, 1)

        def start_round_act(act):
            left = signed_rest()

            def keep_sums(c):
                b0, b1 = C4[c]
                act.wait_ge(pe_step, c + 1)
                nc.scalar.copy(by_tile(acc01[:, 0:N])[:, b0:b1, :], tiles4(4 + c % 2, b0, b1, 128)).then_inc(ps_read, 1)

            for n in range(PARTS):
                for k in range(2):
                    if n > 0:
                        act.wait_ge(left_ready, 2 * (n - 1) + k + 1)
                    nc.scalar.copy(parts[k][:, :, n * D:(n + 1) * D],
                                   wide[:, :, k * D:(k + 1) * D] if n == 0 else left[k]).then_inc(part_rounded, 1)
                    keep_sums(2 * n + k)
            for c in range(2 * PARTS, len(C4)):
                keep_sums(c)

        with nc.Block() as block:
            @block.vector
            def _(v):
                link = linked(v, dve_done)
                h_flat = flat(h_t[0:D])
                for c, (n0, n1) in enumerate(chunks(N, 512)):
                    s = nc.vector.bn_stats(bn6[:, c, :], h_flat[:, n0:n1])
                link(s)
                nc.vector.bn_aggr(bn2[:], bn6[:].rearrange("p c k -> p (c k)")).then_inc(bn_ready, 1)
                link(nc.vector.tensor_scalar(deg[:, :, 0:2], deg[:, :, 0:2], 1.0, None, ALU.add))
                nc.vector.tensor_scalar(deg[:, :, 2:3], deg[:, :, 2:3], 1.0, None, ALU.max).then_inc(deg_turned, 1)
                v.wait_ge(bn_ready, 2)
                link(nc.vector.reciprocal(bnsc[:, 0:1], bnsc[:, 2:3]))
                link(nc.vector.tensor_tensor(bnsc[:, 0:1], bnsc[:, 0:1], gb[:, 0:1], op=ALU.mult))
                link(nc.vector.scalar_tensor_tensor(bnsc[:, 1:2], bn2[:, 0:1], -1.0, bnsc[:, 0:1], ALU.mult, ALU.mult))
                nc.vector.tensor_tensor(bnsc[:, 1:2], bnsc[:, 1:2], gb[:, 1:2], op=ALU.add).then_inc(bn_ready, 1)
                v.wait_ge(deg_turned, 2)
                link(nc.vector.reciprocal(deg[:], deg[:]))
                link(nc.vector.tensor_scalar(ndinv[:], deg[:, :, 1], -1.0, None, ALU.mult))
                for c, (b0, b1) in enumerate(C8):
                    v.wait_ge(product_ready, c + 1)
                    nc.vector.tensor_tensor(x[:, b0:b1, :], x[:, b0:b1, :],
                                            ps[0:TP, 2 + c % 2, 0:(b1 - b0) * D].rearrange("p (b c) -> p b c", c=D),
                                            op=ALU.add).then_inc(deg_read, 1)
                v.wait_ge(deg_read, len(C8))
                layer_norm_relu(v, link, x, h, h_ready)
                v.wait_ge(h_ready, 2)
                for k in range(2):
                    nc.vector.tensor_tensor(wide[:, :, k * D:(k + 1) * D], h[:], row_bc(deg[:, :, k], D),
                                            op=ALU.mult).then_inc(tables_ready, 1)
                first_windows(v)
                v.wait_ge(tables_ready, 2)
                signed_parts_dve(v)

            @block.scalar
            def _(act):
                act.wait_ge(bn_ready, 1)
                nc.scalar.activation(bnsc[:, 2:3], bn2[:, 1:2], ACT.Sqrt, bias=epsc[0:D, :]).then_inc(bn_ready, 1)
                act.wait_ge(deg_turned, 1)
                nc.scalar.activation(deg[:, :, 0:2], deg[:, :, 0:2], ACT.Sqrt).then_inc(deg_turned, 1)
                act.wait_ge(bn_ready, 3)
                for c, (b0, b1) in enumerate(C8):
                    nc.scalar.activation(hid_t[0:D, b0 * TP:b1 * TP], flat(h_t[0:D, b0:b1, :]), ACT.Identity,
                                         bias=bnsc[:, 1:2], scale=bnsc[:, 0:1]).then_inc(chunk_ready, 1)
                norm_tiles_act(act, x, h, ACT.Relu, h_ready)
                act.wait_ge(tables_ready, 2)
                start_round_act(act)

            @block.tensor
            def _(pe):
                for c, (b0, b1) in enumerate(C8):
                    pe.wait_ge(chunk_ready, c + 1)
                    if c >= 2:
                        pe.wait_ge(deg_read, c - 1)
                    for b in range(b0, b1):
                        t = nc.tensor.transpose(ps[0:TP, 2 + c % 2, (b - b0) * D:(b - b0 + 1) * D],
                                                hid_t[0:D, b * TP:(b + 1) * TP], ident[0:D, 0:D])
                    t.then_inc(product_ready, 1)
                pe.wait_ge(tables_ready, 2)
                start_sums_pe(pe)

            @block.sync
            def _(sp):
                sp.wait_ge(tables_ready, 1)
                sp.dma_start(table_h, wide[:, :, 0:D]).then_inc(stored, 16)
                sp.wait_ge(tables_ready, 2)
                sp.dma_start(table_n, wide[:, :, D:2 * D]).then_inc(stored, 16)
                sp.wait_ge(stored, 32)
        rejoin()

        weighted_round(srcsign_i, sign_w, 2)

        C2 = chunks(TB, 2)
        with nc.Block() as block:
            @block.tensor
            def _(pe):
                def second(c):
                    b0, b1 = C4[c]
                    pe.wait_ge(h_ready, c + 1)
                    if c >= 2:
                        pe.wait_ge(ht_ready, c - 1)
                    for b in range(b0, b1):
                        m = nc.tensor.transpose(ps[:, 2 + c % 2, (b - b0) * TP:(b - b0 + 1) * TP], wide[:, b, :],
                                                ident[0:TP, 0:TP])
                    m.then_inc(hnew_turned, 1)

                def third(c):
                    b0, b1 = C4[c]
                    pe.wait_ge(ht_ready, c + 1)
                    if c >= 2:
                        pe.wait_ge(deg_read, c - 1)
                    for b in range(b0, b1):
                        m = nc.tensor.matmul(ps[0:TP, 6 + c % 2, (b - b0) * 128:(b - b0 + 1) * 128],
                                             hid_t[:, b * TP:(b + 1) * TP], flat(w2pn[:]), start=True, stop=True)
                    m.then_inc(gates_done, 1)

                for c, (b0, b1) in enumerate(C2):
                    if c >= 2:
                        pe.wait_ge(chunk_ready, c - 1)
                    for b in range(b0, b1):
                        m = nc.tensor.matmul(ps[0:TP, c % 2, (b - b0) * 256:(b - b0 + 1) * 256],
                                             node_cols(acc01, b), flat(w1pn[:]), start=True, stop=True)
                    m.then_inc(product_ready, 1)
                    if c >= 3 and c % 2 == 1:
                        second(c // 2 - 1)
                        if c >= 5:
                            third(c // 2 - 2)
                second(len(C4) - 2)
                third(len(C4) - 3)
                second(len(C4) - 1)
                third(len(C4) - 2)
                third(len(C4) - 1)
                pe.wait_ge(deg_read, len(C4))
                start_sums_pe(pe)

            @block.scalar
            def _(act):
                for c, (b0, b1) in enumerate(C4):
                    act.wait_ge(hnew_turned, c + 1)
                    nc.scalar.copy(hid_t[:, b0 * TP:b1 * TP], ps[:, 2 + c % 2, 0:(b1 - b0) * TP]).then_inc(ht_ready, 1)
                act.wait_ge(deg_read, len(C4))
                start_round_act(act)

            @block.vector
            def _(v):
                def first_out(c):
                    b0, b1 = C2[c]
                    v.wait_ge(product_ready, c + 1)
                    for b in range(b0, b1):
                        o = (b - b0) * 256
                        m = nc.vector.scalar_tensor_tensor(wide[:, b, :], ps[0:TP, c % 2, o:o + 128], deg[:, b, 0:1],
                                                           b1pn[:, 0], ALU.mult, ALU.add)
                    m.then_inc(part_ready, 1)
                    v.wait_ge(part_ready, c + 1)
                    for b in range(b0, b1):
                        o = (b - b0) * 256 + 128
                        m = nc.vector.scalar_tensor_tensor(wide[:, b, :], ps[0:TP, c % 2, o:o + 128], ndinv[:, b:b + 1],
                                                           wide[:, b, :], ALU.mult, ALU.add)
                    m.then_inc(chunk_ready, 1)

                def next_tables(c):
                    b0, b1 = C4[c]
                    v.wait_ge(gates_done, c + 1)
                    nc.vector.tensor_tensor(
                        wide[:, b0:b1, :].rearrange("p b (k e) -> p b k e", k=2),
                        ps[0:TP, 6 + c % 2, 0:(b1 - b0) * 128].rearrange("p (b k e) -> p b k e", k=2, e=D),
                        deg[:, b0:b1, 0:2].unsqueeze(3).to_broadcast([TP, b1 - b0, 2, D]),
                        op=ALU.mult).then_inc(deg_read, 1)

                for c, (b0, b1) in enumerate(C4):
                    first_out(2 * c)
                    if 2 * c + 1 < len(C2):
                        first_out(2 * c + 1)
                    v.wait_ge(chunk_ready, min(2 * c + 2, len(C2)))
                    nc.vector.tensor_scalar(wide[:, b0:b1, :], wide[:, b0:b1, :], 0.0, None, ALU.max).then_inc(h_ready, 1)
                    if c >= 3:
                        next_tables(c - 3)
                for c in range(len(C4) - 3, len(C4)):
                    next_tables(c)
                v.wait_ge(deg_read, len(C4))
                first_windows(v)
                signed_parts_dve(v)

            @block.sync
            def _(sp):
                sp.wait_ge(deg_read, len(C4))
                sp.dma_start(table_h, wide[:, :, 0:D]).then_inc(stored, 16)
                sp.dma_start(table_n, wide[:, :, D:2 * D]).then_inc(stored, 16)
                sp.wait_ge(stored, 32)
        rejoin()

        weighted_round(srcsign_i, sign_w, 2)

        def turn_nodes(pe, src, c):
            b0, b1 = C4[c]
            if c >= 2:
                pe.wait_ge(ht_ready, c - 1)
            for b in range(b0, b1):
                m = nc.tensor.transpose(ps[0:D, 6 + c % 2, (b - b0) * TP:(b - b0 + 1) * TP], src[:, b, :],
                                        ident[0:TP, 0:TP])
            m.then_inc(hnew_turned, 1)

        def keep_nodes(act, c):
            b0, b1 = C4[c]
            act.wait_ge(hnew_turned, c + 1)
            nc.scalar.copy(h_t[0:D, b0:b1, :], tiles4(6 + c % 2, b0, b1)).then_inc(ht_ready, 1)

        with nc.Block() as block:
            @block.tensor
            def _(pe):
                for c, (b0, b1) in enumerate(C4):
                    if c >= 2:
                        pe.wait_ge(chunk_ready, c - 1)
                    for b in range(b0, b1):
                        m = nc.tensor.transpose(ps[0:TP, c % 2, (b - b0) * 128:(b - b0 + 1) * 128],
                                                node_cols(acc01, b), ident[:, :])
                    m.then_inc(product_ready, 1)
                pe.wait_ge(h_ready, 2)
                for c in range(len(C4)):
                    turn_nodes(pe, h, c)

            @block.vector
            def _(v):
                link = linked(v, dve_done)
                for c, (b0, b1) in enumerate(C4):
                    v.wait_ge(product_ready, c + 1)
                    nc.vector.tensor_tensor(
                        wide[:, b0:b1, :].rearrange("p b (k e) -> p b k e", k=2),
                        ps[0:TP, c % 2, 0:(b1 - b0) * 128].rearrange("p (b k e) -> p b k e", k=2, e=D),
                        deg[:, b0:b1, 0:2].unsqueeze(3).to_broadcast([TP, b1 - b0, 2, D]),
                        op=ALU.mult).then_inc(chunk_ready, 1)
                v.wait_ge(chunk_ready, len(C4))
                link(nc.vector.tensor_tensor(h[:], wide[:, :, 0:D], wide[:, :, D:2 * D], op=ALU.subtract))
                link(nc.vector.tensor_tensor(h[:], h[:], const_bc(b2pn[:, 0]), op=ALU.add))
                link(nc.vector.scalar_tensor_tensor(flat(x[:]), flat(h[:]), 0.0, flat(x[:]), ALU.max, ALU.add))
                layer_norm_relu(v, link, x, h, h_ready)
                first_windows(v)
                parts_of_h(v, link, 0, HALF)
                v.wait_ge(h_ready, 2)
                parts_of_h(v, link, HALF, TB)

            @block.scalar
            def _(act):
                norm_tiles_act(act, x, h, ACT.Relu, h_ready)
                for c in range(len(C4)):
                    keep_nodes(act, c)

            @block.gpsimd
            def _(pool):
                pool.wait_ge(product_ready, len(C4))
                nc.gpsimd.memset(acc01[:], 0.0).then_inc(pool_done, 1)
                pool.wait_ge(pool_done, 1)

            @block.sync
            def _(sp):
                sp.wait_ge(h_ready, 2)
                sp.dma_start(table_h, h[:]).then_inc(stored, 16)
                sp.wait_ge(stored, 16)
        rejoin()

        with nc.Fori(0, 2) as l:
            weighted_round(src_i, spline_w, 2, both=True)
            with nc.Block() as block:
                @block.tensor
                def _(pe):
                    pe.wait_ge(cleared, 1)
                    for c, (b0, b1) in enumerate(C4):
                        if c >= 2:
                            pe.wait_ge(chunk_ready, c - 1)
                        for b in range(b0, b1):
                            o = 2 * (b - b0) * D
                            nc.tensor.matmul(ps[0:TP, c % 2, o:o + D], node_cols(acc01, b), spl[:, S_W:S_W + D],
                                             start=True, stop=True)
                            m = nc.tensor.matmul(ps[0:TP, c % 2, o + D:o + 2 * D], h_t[:, b, :],
                                                 spl[0:D + 1, S_ROOT:S_ROOT + D], start=True, stop=True)
                        m.then_inc(product_ready, 1)
                        if c >= 1:
                            pe.wait_ge(chunk_ready, c)
                            turn_nodes(pe, h, c - 1)
                    pe.wait_ge(chunk_ready, len(C4))
                    turn_nodes(pe, h, len(C4) - 1)

                @block.vector
                def _(v):
                    link = linked(v, dve_done)
                    first_windows(v)
                    nc.vector.tensor_copy(spl[:], spl_all[:, bass.ds(l, 1), :].rearrange("p a c -> p (a c)")).then_inc(cleared, 1)
                    for c, (b0, b1) in enumerate(C4):
                        v.wait_ge(product_ready, c + 1)
                        t = ps[0:TP, c % 2, 0:(b1 - b0) * 128].rearrange("p (b k e) -> p b k e", k=2, e=D)
                        nc.vector.tensor_tensor(wide[:, b0:b1, 0:D], t[:, :, 0, :], row_bc(deg[:, b0:b1, 2], D),
                                                op=ALU.mult).then_inc(part_ready, 1)
                        v.wait_ge(part_ready, c + 1)
                        nc.vector.tensor_tensor(h[:, b0:b1, :], wide[:, b0:b1, 0:D], t[:, :, 1, :],
                                                op=ALU.add).then_inc(chunk_ready, 1)
                        v.wait_ge(chunk_ready, c + 1)
                        parts_of_h(v, link, b0, b1)

                @block.scalar
                def _(act):
                    for c in range(len(C4)):
                        keep_nodes(act, c)

                @block.gpsimd
                def _(pool):
                    pool.wait_ge(product_ready, len(C4))
                    nc.gpsimd.memset(acc01[:], 0.0).then_inc(pool_done, 1)
                    pool.wait_ge(pool_done, 1)

                @block.sync
                def _(sp):
                    sp.wait_ge(chunk_ready, len(C4))
                    sp.dma_start(table_h, h[:]).then_inc(stored, 16)
                    sp.wait_ge(stored, 16)
            rejoin()

        QUARTERS = [(0, 6), (6, 12), (12, 19), (19, TB)]
        PART = [(0, 12), (12, TB)]

        def edge_gated_nodes(post, l):
            with nc.Block() as block:
                @block.tensor
                def _(pe):
                    def first_product(c):
                        b0, b1 = C4[c]
                        pe.wait_ge(ht_ready, c + 1)
                        if c == 0:
                            pe.wait_ge(loads, 16)
                            if post:
                                pe.wait_ge(y_added, len(QUARTERS))
                        if c >= 2:
                            pe.wait_ge(rz_ready, c - 1)
                        nc.tensor.matmul(ps[:, c % 2, 0:(b1 - b0) * TP], eg[0:D, C_W1:C_W1 + 2 * D],
                                         flat(h_t[0:D, b0:b1, :]), start=True, stop=True).then_inc(product_ready, 1)

                    def second_product(c):
                        b0, b1 = C4[c]
                        pe.wait_ge(cand_ready, c + 1)
                        if c >= 2:
                            pe.wait_ge(chunk_ready, c - 1)
                        for b in range(b0, b1):
                            m = nc.tensor.matmul(ps[0:TP, 2 + c % 2, (b - b0) * D:(b - b0 + 1) * D],
                                                 hid_t[:, b * TP:(b + 1) * TP], eg[:, C_W2:C_W2 + D],
                                                 start=True, stop=True)
                        m.then_inc(gates_done, 1)

                    def turn_y(c):
                        pe.wait_ge(y_ready, 1 if C4[c][1] <= PART[0][1] else 2 if post else 3)
                        turn_nodes(pe, y, c)

                    if post:
                        for c, (b0, b1) in enumerate(QUARTERS):
                            if c >= 2:
                                pe.wait_ge(y_added, c - 1)
                            for b in range(b0, b1):
                                m = nc.tensor.transpose(ps[0:TP, c % 2, (b - b0) * D:(b - b0 + 1) * D],
                                                        node_cols(acc01[0:D], b), ident[0:D, 0:D])
                            m.then_inc(sums_turned, 1)
                    if l is not None:
                        turn_y(0)
                        for c in range(len(C4)):
                            if c + 1 < len(C4):
                                turn_y(c + 1)
                            first_product(c)
                            if c >= 1:
                                second_product(c - 1)
                        second_product(len(C4) - 1)

                @block.scalar
                def _(act):
                    if post:
                        b0, b1 = PART[0]
                        norm_tiles_act(act, y, h, ACT.Identity, h_ready, PART[0], b0, b1, 1)
                        b0, b1 = PART[1]
                        norm_tiles_act(act, y, h, ACT.Identity, h_ready, PART[1], (b0 + b1) // 2, b1, 2)
                    else:
                        b0, b1 = PART[0]
                        norm_tiles_act(act, x, y, ACT.Relu, y_ready, PART[0], b0, b1, 1)
                        b0, b1 = PART[1]
                        norm_tiles_act(act, x, y, ACT.Relu, y_ready, PART[1], (b0 + b1) // 2, b1, 2)
                    if l is not None:
                        keep_nodes(act, 0)
                        for c, (b0, b1) in enumerate(C4):
                            if c + 1 < len(C4):
                                keep_nodes(act, c + 1)
                            act.wait_ge(product_ready, c + 1)
                            nc.scalar.activation(hid_t[:, b0 * TP:b1 * TP], ps[:, c % 2, 0:(b1 - b0) * TP],
                                                 ACT.Identity, bias=eg[:, C_B1:C_B1 + 1]).then_inc(rz_ready, 1)

                @block.vector
                def _(v):
                    link = linked(v, dve_done)

                    def add_sums(c):
                        b0, b1 = QUARTERS[c]
                        v.wait_ge(sums_turned, c + 1)
                        nc.vector.scalar_tensor_tensor(flat(y[:, b0:b1, :]), ps[0:TP, c % 2, 0:(b1 - b0) * D],
                                                       eg_res[0:TP], flat(y[:, b0:b1, :]),
                                                       ALU.mult, ALU.add).then_inc(y_added, 1)

                    def scale_shift(b0, b1):
                        link(nc.vector.tensor_tensor(h[:, b0:b1, :], h[:, b0:b1, :],
                                                     eg_norm[0:TP, 0:D].unsqueeze(1).to_broadcast([TP, b1 - b0, D]),
                                                     op=ALU.mult))
                        nc.vector.tensor_tensor(y[:, b0:b1, :], h[:, b0:b1, :],
                                                eg_norm[0:TP, D:2 * D].unsqueeze(1).to_broadcast([TP, b1 - b0, D]),
                                                op=ALU.add).then_inc(y_ready, 1)

                    if post:
                        nc.vector.tensor_tensor(eg_res, eg[:, C_RES:C_RES + 1], eg[:, C_DOT:C_DOT + 1],
                                                op=ALU.mult).then_inc(eg_kept, 1)
                        nc.vector.tensor_copy(eg_norm, eg[:, C_G:C_G + 2 * D]).then_inc(eg_kept, 1)
                        v.wait_ge(eg_kept, 2)
                        for k, (b0, b1) in enumerate(PART):
                            add_sums(2 * k)
                            add_sums(2 * k + 1)
                            v.wait_ge(y_added, 2 * k + 2)
                            node_stats(v, link, y, b0, b1, k + 1)
                        b0, b1 = PART[0]
                        v.wait_ge(h_ready, 1)
                        scale_shift(b0, b1)
                        b0, b1 = PART[1]
                        v.wait_ge(norm_ready, 2)
                        norm_tiles_dve(v, link, y, h, b0, (b0 + b1) // 2)
                        v.wait_ge(h_ready, 2)
                        scale_shift(b0, b1)
                        v.wait_ge(y_ready, 2)
                    else:
                        for k, (b0, b1) in enumerate(PART):
                            link(nc.vector.tensor_tensor(x[:, b0:b1, :], x[:, b0:b1, :], h[:, b0:b1, :], op=ALU.add))
                            node_stats(v, link, x, b0, b1, k + 1)
                        v.wait_ge(norm_ready, 2)
                        mid = (b0 + b1) // 2
                        norm_tiles_dve(v, link, x, y, b0, mid)
                        nc.vector.tensor_scalar(y[:, b0:mid, :], y[:, b0:mid, :], 0.0, None,
                                                ALU.max).then_inc(y_ready, 1)

                    def leaky(c):
                        b0, b1 = C4[c]
                        v.wait_ge(rz_ready, c + 1)
                        t = hid_t[:, b0 * TP:b1 * TP]
                        nc.vector.scalar_tensor_tensor(t, t, 0.1, t, ALU.mult, ALU.max).then_inc(cand_ready, 1)

                    def table_rows(c):
                        b0, b1 = C4[c]
                        v.wait_ge(gates_done, c + 1)
                        nc.vector.tensor_tensor(
                            h[:, b0:b1, :], ps[0:TP, 2 + c % 2, 0:(b1 - b0) * D].rearrange("p (b e) -> p b e", e=D),
                            eg[0:TP, C_B2:C_B2 + D].unsqueeze(1).to_broadcast([TP, b1 - b0, D]),
                            op=ALU.add).then_inc(chunk_ready, 1)

                    def table_parts(c):
                        b0, b1 = C4[c]
                        v.wait_ge(chunk_ready, c + 1)
                        make_parts(v, link, h[:, b0:b1, :], wide[:, b0:b1, 0:D], parts[0][:, b0:b1, :])

                    if l is not None:
                        first_windows(v)
                        for c in range(len(C4)):
                            leaky(c)
                            if c >= 1:
                                table_rows(c - 1)
                                table_parts(c - 1)
                        table_rows(len(C4) - 1)
                        table_parts(len(C4) - 1)

                @block.gpsimd
                def _(pool):
                    if l is not None:
                        if post:
                            pool.wait_ge(sums_turned, len(QUARTERS))
                        nc.gpsimd.memset(acc01[0:D, :], 0.0).then_inc(pool_done, 1)
                        pool.wait_ge(pool_done, 1)

                @block.sync
                def _(sp):
                    if l is not None:
                        if post:
                            sp.wait_ge(eg_kept, 2)
                        sp.dma_start(eg[:], eg_dram[bass.ds(l, 1)].rearrange("a p c -> (a p) c")).then_inc(loads, 16)
                        sp.wait_ge(chunk_ready, len(C4))
                        sp.dma_start(table_h, h[:]).then_inc(stored, 16)
                        sp.wait_ge(stored, 16)
            rejoin()

        def edge_gated_round():
            with nc.Fori(0, SPAN):
                with nc.Block(no_gpsimd_drain=True) as block:
                    @block.gpsimd
                    def _(pool):
                        gather_rows(pool, N, False)

                    @block.sync
                    def _(sp):
                        for q in range(2):
                            load_sources(sp, src_rows, q, q)
                        source_loop(sp, src_rows)

                    @block.scalar
                    def _(act):
                        with act.Fori(0, G // 2) as i:
                            for s in range(2):
                                act.wait_ge(hid_sum, i * 2 + s + 1)
                                nc.scalar.activation(hid_e[:, s, :], ps[:, 2 + s, 0:256], ACT.Identity,
                                                     bias=eg[:, C_BE1:C_BE1 + 1]).then_inc(hid_biased, 1)

                    @block.tensor
                    def _(pe):
                        def hidden(g, s):
                            for k in range(2):
                                m = nc.tensor.matmul(ps[:, 2 + s, 128 * k:128 * k + 128],
                                                     eg[:, C_WE1 + 128 * k:C_WE1 + 128 * k + 128],
                                                     attr_t[:, bass.ds(g, 1), :].rearrange("p a c -> p (a c)"),
                                                     start=True, stop=True)
                            m.then_inc(hid_sum, 1)

                        def gates(s):
                            for k in range(2):
                                m = nc.tensor.matmul(ps[:, 4 + s, 128 * k:128 * k + 128], hid_e[:, s, 128 * k:128 * k + 128],
                                                     eg[:, C_WE2:C_WE2 + 128], start=True, stop=True)
                            m.then_inc(gate_done, 1)

                        hidden(0, 0)
                        hidden(1, 1)
                        pe.wait_ge(hid_ready, 1)
                        gates(0)
                        first_gather_pe(pe, False, False)

                        def turn(i, last):
                            for s in range(UN):
                                g = i * UN + s
                                if not (last and s == UN - 1):
                                    pe.wait_ge(hid_ready, g + 2)
                                    gates((s + 1) % 2)
                                if not (last and s >= UN - 2):
                                    hidden(g + 2, s % 2)
                                pe.wait_ge(msg_ready, g + 1)
                                for j in range(EJ):
                                    m = nc.tensor.matmul(ps[0:D, s % 2, 0:WIN], msg[:, s % 2, j, :],
                                                         onehot[:, s % 2, j, :], start=(j == 0), stop=(j == EJ - 1))
                                m.then_inc(summed, 1)
                                step_gather_pe(pe, i, s, False, False, last)

                        with pe.Fori(0, G // UN - 1) as i:
                            turn(i, False)
                        turn(G // UN - 1, True)

                    @block.vector
                    def _(v):
                        def leak(g, s):
                            v.wait_ge(hid_biased, g + 1)
                            nc.vector.scalar_tensor_tensor(hid_e[:, s, :], hid_e[:, s, :], 0.1, hid_e[:, s, :],
                                                           ALU.mult, ALU.max).then_inc(hid_ready, 1)

                        for s in range(UN):
                            copy_index(src_i, s, s).then_inc(idx_ready[s], 1)
                        build_onehot(0, 0).then_inc(onehot_ready, 1)
                        v.wait_ge(onehot_ready, 1)
                        leak(0, 0)
                        leak(1, 1)
                        first_hot_dve(v, False, False)

                        def turn(i, last):
                            for s in range(UN):
                                g = i * UN + s
                                m = msg[:, s % 2].rearrange("p j c -> p (j c)")
                                v.wait_ge(gate_done, g + 1)
                                nc.vector.tensor_tensor(m, eg[:, C_BE2:C_BE2 + 256], ps[:, 4 + s % 2, 0:256],
                                                        op=ALU.add).then_inc(gate_biased, 1)
                                v.wait_ge(gate_biased, g + 1)
                                rows_here(v, i, s, False)
                                nc.vector.tensor_tensor(m, gath[:, s].rearrange("p j c -> p (j c)"), m,
                                                        op=ALU.mult).then_inc(msg_ready, 1)
                                if not (last and s == UN - 1):
                                    build_onehot(g + 1, (s + 1) % 2).then_inc(onehot_ready, 1)
                                step_hot_dve(v, i, s, False, False, last)
                                col = v.value_load(win_row[0:1, bass.ds(g, 1)], min_val=0, max_val=N)
                                v.wait_ge(summed, g + 1)
                                nc.vector.tensor_tensor(acc01[0:D, bass.ds(col, WIN)], acc01[0:D, bass.ds(col, WIN)],
                                                        ps[0:D, s % 2, 0:WIN], op=ALU.add).then_inc(acc_added, 1)
                                if not last:
                                    copy_index(src_i, g + UN, s).then_inc(idx_ready[s], 1)
                                step_sum_dve(v, i, s, False, last)
                                if not (last and s >= UN - 2):
                                    leak(g + 2, s % 2)
                                v.wait_ge(onehot_ready, min(g + 2, G) if last else g + 2)
                                v.wait_ge(acc_added, g + 1)

                        with v.Fori(0, G // UN - 1) as i:
                            turn(i, False)
                        turn(G // UN - 1, True)
                        next_windows(v)
                rejoin()

        edge_gated_nodes(False, 0)
        with nc.Fori(1, L3L) as l:
            edge_gated_round()
            edge_gated_nodes(True, l)
        edge_gated_round()
        edge_gated_nodes(True, None)

        with nc.Block() as block:
            @block.vector
            def _(v):
                nc.vector.tensor_tensor(x[:], x[:], y[:], op=ALU.add).then_inc(h_ready, 1)

            @block.sync
            def _(sp):
                sp.wait_ge(h_ready, 1)
                sp.dma_start(out.rearrange("(p b) c -> p b c", b=TB), x[:]).then_inc(out_done, 16)
                sp.wait_ge(out_done, 16)


def kernel(**inputs):
    import numpy as np
    import concourse.bacc as bacc
    from concourse.bass_utils import run_bass_kernel_spmd as run

    nc = bacc.Bacc("TRN2", target_bir_lowering=False, num_devices=1)
    arrays, args = {}, {}
    for name, value in inputs.items():
        arr = np.ascontiguousarray(value)
        arrays[f"in_{name}"] = arr
        args[name] = nc.dram_tensor(f"in_{name}", arr.shape, mybir.dt.from_np(arr.dtype), kind="ExternalInput").ap()
    out = nc.dram_tensor("out", (N, D), F32, kind="ExternalOutput").ap()
    gnn_kernel(nc, args, out)
    r = run(nc, [arrays], core_ids=[0])
    return r.results[0]["out"]
```
